# Optimizing a Trainium2 kernel written in Bass

```python
import numpy as np
import jax
import jax.numpy as jnp

def _softmax(x, axis=-1):
    return jax.nn.softmax(x, axis=axis)

def _gelu(x):
    return jax.nn.gelu(x, approximate=True)

def _silu(x):
    return jax.nn.silu(x)

def _sigmoid(x):
    return jax.nn.sigmoid(x)

def _layernorm(x, axis=-1, eps=1e-05):
    m = jnp.mean(x, axis=axis, keepdims=True)
    v = jnp.var(x, axis=axis, keepdims=True)
    return (x - m) / jnp.sqrt(v + eps)

def _scatter_add(tgt, idx, src, axis=0):
    return tgt.at[idx].add(src)

def _segment_sum(src, seg, n):
    return jax.ops.segment_sum(src, seg, n)
kernel_name = 'mk_gnn_resnorm_d2_gnn_r8_6657ee'

def setup_inputs(seed: int=0):
    np.random.seed(seed)
    _w = jnp.asarray

    def _rec_inputs():
        import jax
        import jax.numpy as jnp
        _gk = jax.random.key(seed)
        x = -0.000202 + 1 * jax.random.normal(jax.random.fold_in(_gk, 1), (6250, 128), jnp.float32)
        _s = jax.random.randint(jax.random.fold_in(_gk, 2), (100000,), 0, 6250, jnp.int32)
        _d = jax.random.randint(jax.random.fold_in(_gk, 3), (100000,), 0, 6250, jnp.int32)
        _loop = jnp.arange(6250, dtype=jnp.int32)
        src = jnp.concatenate([_s, _d, _loop])
        dst = jnp.concatenate([_d, _s, _loop])
        _o = jnp.argsort(dst, stable=True)
        src = src[_o]
        dst = dst[_o]
        edge_type_9 = jax.random.randint(jax.random.fold_in(_gk, 13), (206250,), 0, 9, jnp.int32)
        return (x, src, dst, edge_type_9)
    x, src, dst, edge_type_9 = _rec_inputs()

    def _L0_gnn_setup():
        import jax, jax.numpy as jnp
        import numpy as np
        NUM_EDGE_TYPES = 8
        HIDDEN = 128
        N_NODES = 6250
        N_EDGES = 75000

        def _gru_cell(x, h, W_ih, W_hh, b_ih, b_hh):
            H = h.shape[-1]
            gi = x @ W_ih.T + b_ih
            gh = h @ W_hh.T + b_hh
            i_r, i_z, i_n = (gi[:, :H], gi[:, H:2 * H], gi[:, 2 * H:])
            h_r, h_z, h_n = (gh[:, :H], gh[:, H:2 * H], gh[:, 2 * H:])
            r = jax.nn.sigmoid(i_r + h_r)
            z = jax.nn.sigmoid(i_z + h_z)
            n = jnp.tanh(i_n + r * h_n)
            return (1.0 - z) * n + z * h
        key = jax.random.key(seed)
        ks = jax.random.split(key, 10)
        H = HIDDEN
        h = jax.random.normal(ks[0], (N_NODES, H), dtype=jnp.float32)
        edge_index = jax.random.randint(ks[1], (2, N_EDGES), 0, N_NODES, dtype=jnp.int32)
        edge_type = jax.random.randint(ks[2], (N_EDGES,), 0, NUM_EDGE_TYPES + 1, dtype=jnp.int32)
        s = 1.0 / np.sqrt(H)
        W_msg = jax.random.uniform(ks[3], (H, H), jnp.float32, -s, s)
        b_msg = jax.random.uniform(ks[4], (H,), jnp.float32, -s, s)
        edge_embed = jax.random.normal(ks[5], (NUM_EDGE_TYPES + 1, H), dtype=jnp.float32)
        W_ih = jax.random.uniform(ks[6], (3 * H, H), jnp.float32, -s, s)
        W_hh = jax.random.uniform(ks[7], (3 * H, H), jnp.float32, -s, s)
        b_ih = jax.random.uniform(ks[8], (3 * H,), jnp.float32, -s, s)
        b_hh = jax.random.uniform(ks[9], (3 * H,), jnp.float32, -s, s)
        return {'h': h, 'edge_index': edge_index, 'edge_type': edge_type, 'num_nodes': N_NODES, 'W_msg': W_msg, 'b_msg': b_msg, 'edge_embed': edge_embed, 'W_ih': W_ih, 'W_hh': W_hh, 'b_ih': b_ih, 'b_hh': b_hh}
    _L0_gnn_all = _L0_gnn_setup()
    _L0_gnn_in = {k: v for k, v in _L0_gnn_all.items() if k in ('W_msg', 'b_msg', 'edge_embed', 'W_ih', 'W_hh', 'b_ih', 'b_hh')}
    del _L0_gnn_all

    def _L1_gnn_setup():
        import jax, jax.numpy as jnp
        import numpy as np
        NEG_SLOPE = 0.2
        key = jax.random.key(seed)
        k1, k2, k3, k4, k5 = jax.random.split(key, 5)
        N, D, E = (1250, 128, 80000)
        feat = jax.random.normal(k1, (N, D), dtype=jnp.float32)
        fc_weight = jax.random.normal(k2, (D, D), dtype=jnp.float32) / jnp.sqrt(jnp.float32(D))
        attn = jax.random.normal(k3, (1, 1, D), dtype=jnp.float32) * 0.1
        eps = jnp.zeros((1,), dtype=jnp.float32)
        src = jax.random.randint(k4, (E,), 0, N, dtype=jnp.int32)
        dst = jax.random.randint(k5, (E,), 0, N, dtype=jnp.int32)
        return {'feat': feat, 'fc_weight': fc_weight, 'attn': attn, 'eps': eps, 'src': src, 'dst': dst}
    _L1_gnn_all = _L1_gnn_setup()
    _L1_gnn_in = {k: v for k, v in _L1_gnn_all.items() if k in ('fc_weight', 'attn', 'eps')}
    del _L1_gnn_all
    return {'x': x, 'src': src, 'dst': dst, 'edge_type_9': edge_type_9, 'L0_gnn_W_msg': _L0_gnn_in['W_msg'], 'L0_gnn_b_msg': _L0_gnn_in['b_msg'], 'L0_gnn_edge_embed': _L0_gnn_in['edge_embed'], 'L0_gnn_W_ih': _L0_gnn_in['W_ih'], 'L0_gnn_W_hh': _L0_gnn_in['W_hh'], 'L0_gnn_b_ih': _L0_gnn_in['b_ih'], 'L0_gnn_b_hh': _L0_gnn_in['b_hh'], 'L1_gnn_fc_weight': _L1_gnn_in['fc_weight'], 'L1_gnn_attn': _L1_gnn_in['attn'], 'L1_gnn_eps': _L1_gnn_in['eps']}

def reference(x, src, dst, edge_type_9, L0_gnn_W_msg, L0_gnn_b_msg, L0_gnn_edge_embed, L0_gnn_W_ih, L0_gnn_W_hh, L0_gnn_b_ih, L0_gnn_b_hh, L1_gnn_fc_weight, L1_gnn_attn, L1_gnn_eps):
    import jax
    import jax.numpy as jnp

    def _L0_gnn_ref(h, edge_index, edge_type, num_nodes, W_msg, b_msg, edge_embed, W_ih, W_hh, b_ih, b_hh):
        import jax, jax.numpy as jnp
        import numpy as np
        NUM_EDGE_TYPES = 8
        HIDDEN = 128
        N_NODES = 6250
        N_EDGES = 75000

        def _gru_cell(x, h, W_ih, W_hh, b_ih, b_hh):
            H = h.shape[-1]
            gi = x @ W_ih.T + b_ih
            gh = h @ W_hh.T + b_hh
            i_r, i_z, i_n = (gi[:, :H], gi[:, H:2 * H], gi[:, 2 * H:])
            h_r, h_z, h_n = (gh[:, :H], gh[:, H:2 * H], gh[:, 2 * H:])
            r = jax.nn.sigmoid(i_r + h_r)
            z = jax.nn.sigmoid(i_z + h_z)
            n = jnp.tanh(i_n + r * h_n)
            return (1.0 - z) * n + z * h
        src = edge_index[0]
        dst = edge_index[1]
        src_h = h[src] @ W_msg.T + b_msg
        emb = edge_embed[jnp.clip(edge_type, 0, NUM_EDGE_TYPES)]
        msg = src_h + emb
        messages = jax.ops.segment_sum(msg, dst, num_segments=num_nodes)
        h_new = _gru_cell(messages, h[:num_nodes], W_ih, W_hh, b_ih, b_hh)
        result = jnp.zeros_like(h).at[:num_nodes].set(h_new)
        return result

    def _L1_gnn_ref(feat, fc_weight, attn, eps, src, dst):
        import jax, jax.numpy as jnp
        import numpy as np
        NEG_SLOPE = 0.2
        N = feat.shape[0]
        proj = feat @ fc_weight.T
        el = proj[src]
        er = proj[dst]
        a = attn.reshape(-1)
        e = jnp.sum(jax.nn.leaky_relu(el + er, NEG_SLOPE) * a, axis=-1)
        gate = jax.nn.sigmoid(jnp.sum(el * er, axis=-1))
        w = jax.nn.sigmoid(e * gate)
        msg = feat[src] * w[:, None]
        neigh_sum = jax.ops.segment_sum(msg, dst, num_segments=N)
        deg = jax.ops.segment_sum(jnp.ones_like(w), dst, num_segments=N)
        neigh = neigh_sum / jnp.maximum(deg, 1.0)[:, None]
        rst = (1.0 + eps[0]) * feat + neigh
        return rst
    edge_index = jnp.stack([src, dst])
    x = _layernorm(x + _L0_gnn_ref(x, edge_index, edge_type_9, 6250, L0_gnn_W_msg, L0_gnn_b_msg, L0_gnn_edge_embed, L0_gnn_W_ih, L0_gnn_W_hh, L0_gnn_b_ih, L0_gnn_b_hh), axis=-1)
    x = _layernorm(x + _L1_gnn_ref(x, L1_gnn_fc_weight, L1_gnn_attn, L1_gnn_eps, src, dst), axis=-1)
    return x

_drawn_inputs = setup_inputs


def setup_inputs(seed=0):
    import zlib

    import numpy as np

    out = dict(_drawn_inputs(seed))
    spreads = {}
    factors = {'L0_gnn_b_ih': 8.0, 'L0_gnn_b_hh': 8.0, 'L1_gnn_fc_weight': 2.898, 'L1_gnn_attn': 3.083}
    for name, (base, spread) in spreads.items():
        noise = np.random.default_rng([zlib.crc32(name.encode()), seed]).standard_normal(out[name].shape)
        drawn = base * np.exp(spread * noise) if base else spread * noise
        out[name] = jnp.asarray(drawn.astype(out[name].dtype))
    for name, factor in factors.items():
        out[name] = (out[name] * factor).astype(out[name].dtype)
    return out
```

```python
from contextlib import ExitStack, contextmanager

import concourse.bass as bass
from concourse import mybir

F32 = mybir.dt.float32
BF16 = mybir.dt.bfloat16
I32 = mybir.dt.int32
ALU = mybir.AluOpType
ACT = mybir.ActivationFunctionType
AX = mybir.AxisListType
RMAX = bass.bass_isa.ReduceOp.max

P = 128
CHUNK = 7
NC = 4
GROUP = CHUNK * NC
NODES = 112
QUAD = 4
LN_EPS = 1e-5
LEAK = 0.2
FAR = 1.0e6


def graph_layers(nc, x, src, dst, edge_type, W_msg, b_msg, edge_embed, W_ih, W_hh, b_ih, b_hh,
                 fc_weight, attn, eps, out):
    N, D = x.shape
    E = src.shape[0]
    NT = edge_embed.shape[0]
    assert D == P and W_ih.shape == (3 * D, D)
    NG = -(-E // (P * GROUP))
    TILES = NG * GROUP
    QN = QUAD * NODES
    NQ = 2 * (-(-N // (2 * QN)))
    NTL = NQ * QUAD
    NPAD = max(NTL * NODES, N + P)
    MAXB = NG * (-(-N // P))
    WIDE = max(NPAD, NTL * D)

    rows = nc.dram_tensor("rows", [NPAD, 2 * D], F32).ap()
    parts = nc.dram_tensor("parts", [NPAD, 3 * D], BF16).ap()

    with ExitStack() as whole:
        def sb(name, shape, dt, ctx=whole):
            return ctx.enter_context(nc.sbuf_tensor(name, shape, dt))

        def psum(name, shape, dt, ctx):
            return ctx.enter_context(nc.psum_tensor(name, shape, dt))

        def sem(name):
            return whole.enter_context(nc.semaphore(name))

        nodes = sb("nodes", [NODES, NTL, D], F32)
        work = sb("work", [P, WIDE], F32)
        sums = sb("sums", [P, NPAD], F32)
        counts = sb("counts", [NT, NPAD], F32)
        src_tab = sb("src_tab", [P, TILES], I32)
        dst_f = sb("dst_f", [P, TILES], F32)
        type_f = sb("type_f", [P, TILES], F32)
        first_f = sb("first_f", [P, NG], F32)
        first_i = sb("first_i", [P, NG], I32)
        nwin_i = sb("nwin_i", [P, NG], I32)
        iota_f = sb("iota_f", [P, P], F32)
        ident = sb("ident", [P, P], F32)
        ident_b = sb("ident_b", [P, P], BF16)
        wT = sb("wT", [P, 8, D], F32)
        table = sb("table", [NT, D], F32)
        bih = sb("bih", [P, 3], F32)
        bhh = sb("bhh", [P, 3], F32)
        brz = sb("brz", [P, 2], F32)
        a_all = sb("a_all", [P, D], F32)
        c_x = sb("c_x", [NODES, 1], F32)
        ones = sb("ones", [NT, 1], F32)
        rdeg = sb("rdeg", [NODES, NTL], F32)
        stats = sb("stats", [NODES, QUAD, 6], F32)
        moments = sb("moments", [NODES, NTL, 2], F32)
        rstd = sb("rstd", [NODES, NTL], F32)
        dl = sb("dl", [P, GROUP], F32)
        idx = sb("idx", [P, NC, CHUNK], I32)

        chunk_begun = sem("chunk_begun")

        @contextmanager
        def every_body(eng, counter):
            eng.reg_mov(counter, 0)
            with eng.Fori(0, NG) as g:
                nw = eng.value_load(nwin_i[0:1, bass.ds(g, 1)], min_val=1, max_val=-(-N // P))
                with eng.Fori(0, nw) as j:
                    yield g, j, eng.snap(counter, min_val=0, max_val=MAXB)
                    eng.reg_add(counter, counter, 1)

        with ExitStack() as ph:
            dst_i = sb("dst_i", [P, TILES], I32, ph)
            type_i = sb("type_i", [P, TILES], I32, ph)
            iota_i = sb("iota_i", [P, P], I32, ph)
            raw = sb("raw", [P, 8, D], F32, ph)
            bmsg = sb("bmsg", [NT, D], F32, ph)
            far = sb("far", [P, GROUP], F32, ph)
            ext = sb("ext", [P, 2 * NG], F32, ph)
            ext_all = sb("ext_all", [P, 2 * NG], F32, ph)
            span_f = sb("span_f", [P, NG], F32, ph)
            span_i = sb("span_i", [P, NG], I32, ph)
            win_i = sb("win_i", [P, NG], I32, ph)
            w_ps = psum("w_ps", [P, 8, D], F32, ph)
            iota_done = sem("iota_done")
            zeroed = sem("zeroed")
            select_done = sem("select_done")
            pads_done = sem("pads_done")
            edges_in = sem("edges_in")
            nodes_in = sem("nodes_in")
            weights_in = sem("weights_in")
            small_in = sem("small_in")
            pad_rows_out = sem("pad_rows_out")
            zeros_done = sem("zeros_done")
            prep = sem("prep")
            ext_done = sem("ext_done")
            ext_reduced = sem("ext_reduced")
            w_turned = sem("w_turned")
            w_copied = sem("w_copied")

            full = NG - 1
            rem = E - full * P * GROUP
            rp, rl = rem // GROUP, rem % GROUP
            n_edge_dmas = 3 * ((full > 0) + (rp > 0) + (rl > 0))
            ft, fr = N // NODES, N % NODES
            n_node_dmas = (ft > 0) + (fr > 0)

            with nc.Block() as block:
                @block.sync
                def _(sp):
                    sp.wait_ge(pads_done, 4)
                    for tab, edges in ((dst_i, dst), (src_tab, src), (type_i, edge_type)):
                        if full:
                            sp.dma_start(tab[:, 0:full * GROUP].rearrange("p (g j) -> p g j", j=GROUP),
                                         edges[0:full * P * GROUP].rearrange("(g p j) -> p g j", p=P, j=GROUP)
                                         ).then_inc(edges_in, 16)
                        at = full * P * GROUP
                        if rp:
                            sp.dma_start(tab[0:rp, full * GROUP:TILES],
                                         edges[at:at + rp * GROUP].rearrange("(p j) -> p j", j=GROUP)
                                         ).then_inc(edges_in, 16)
                        if rl:
                            sp.dma_start(tab[rp:rp + 1, full * GROUP:full * GROUP + rl],
                                         edges[at + rp * GROUP:E].rearrange("(p j) -> p j", p=1)
                                         ).then_inc(edges_in, 16)
                    if ft:
                        sp.dma_start(nodes[:, 0:ft, :], x[0:ft * NODES, :].rearrange("(t p) f -> p t f", p=NODES)
                                     ).then_inc(nodes_in, 16)
                    if fr:
                        sp.dma_start(nodes[0:fr, ft, :], x[ft * NODES:N, :]).then_inc(nodes_in, 16)
                    sp.wait_ge(zeros_done, 2)
                    for r in range(NTL * NODES, NPAD, P):
                        m = min(P, NPAD - r)
                        sp.dma_start(rows[r:r + m, :], work[0:m, 0:2 * D]).then_inc(pad_rows_out, 16)
                        sp.dma_start(parts[r:r + m, :], work[0:m, 0:3 * D // 2].bitcast(BF16)
                                     ).then_inc(pad_rows_out, 16)
                    if NPAD > NTL * NODES:
                        sp.wait_ge(pad_rows_out, 32 * (-(-(NPAD - NTL * NODES) // P)))
                    sp.wait_ge(edges_in, 16 * n_edge_dmas)
                    sp.wait_ge(nodes_in, 16 * n_node_dmas)

                @block.gpsimd
                def _(pool):
                    pool.iota(iota_i[:], pattern=[[1, P]], base=0, channel_multiplier=0).then_inc(iota_done, 1)
                    pool.memset(ident[:], 0.0).then_inc(zeroed, 1)
                    pool.wait_ge(zeroed, 1)
                    pool.affine_select(out=ident[:], in_=ident[:], compare_op=ALU.not_equal, fill=1.0, base=0,
                                       pattern=[[-1, P]], channel_multiplier=1).then_inc(select_done, 1)
                    pool.wait_ge(ext_done, 4)
                    pool.partition_all_reduce(ext_all[:], ext[:], P, RMAX).then_inc(ext_reduced, 1)

                @block.scalar
                def _(act):
                    act.dma_start(raw[:, 0, :], W_msg).then_inc(weights_in, 16)
                    act.dma_start(raw[:, 1, :], fc_weight).then_inc(weights_in, 16)
                    act.dma_start(raw[:, 2:5, :], W_ih.rearrange("(g h) k -> h g k", g=3)).then_inc(weights_in, 16)
                    act.dma_start(raw[:, 5:8, :], W_hh.rearrange("(g h) k -> h g k", g=3)).then_inc(weights_in, 16)
                    with nc.allow_non_contiguous_dma(reason="bias columns, 768 elements"):
                        act.dma_start(bih[:], b_ih.rearrange("(g h) -> h g", g=3)).then_inc(small_in, 16)
                        act.dma_start(bhh[:], b_hh.rearrange("(g h) -> h g", g=3)).then_inc(small_in, 16)
                    act.dma_start(table[:], edge_embed).then_inc(small_in, 16)
                    act.dma_start(bmsg[:], b_msg.rearrange("(o f) -> o f", o=1).to_broadcast([NT, D])
                                  ).then_inc(small_in, 16)
                    act.dma_start(a_all[:], attn.rearrange("a b f -> (a b) f").to_broadcast([P, D])
                                  ).then_inc(small_in, 16)
                    act.dma_start(c_x[:], eps.rearrange("(o f) -> o f", o=1).to_broadcast([NODES, 1])
                                  ).then_inc(small_in, 16)
                    act.wait_ge(w_turned, 8)
                    act.copy(wT[:, 0:4, :], w_ps[:, 0:4, :]).then_inc(w_copied, 1)
                    act.copy(wT[:, 4:8, :], w_ps[:, 4:8, :]).then_inc(w_copied, 1)

                @block.tensor
                def _(pe):
                    pe.wait_ge(weights_in, 64)
                    pe.wait_ge(select_done, 1)
                    for i in range(8):
                        pe.transpose(w_ps[:, i, :], raw[:, i, :], ident[:]).then_inc(w_turned, 1)

                @block.vector
                def _(dve):
                    last = slice(full * GROUP, TILES)
                    dve.memset(src_tab[:, last], 0).then_inc(pads_done, 1)
                    dve.memset(dst_i[:, last], -1).then_inc(pads_done, 1)
                    dve.memset(type_i[:, last], 0).then_inc(pads_done, 1)
                    dve.memset(nodes[:, ft:NTL, :], 0.0).then_inc(pads_done, 1)
                    dve.memset(work[:, 0:2 * D], 0.0).then_inc(zeros_done, 1)
                    dve.memset(sums[:], 0.0).then_inc(zeros_done, 1)
                    dve.memset(counts[:], 0.0)
                    dve.memset(ones[:], 1.0)
                    dve.wait_ge(iota_done, 1)
                    dve.tensor_copy(iota_f[:], iota_i[:])
                    dve.wait_ge(select_done, 1)
                    dve.tensor_copy(ident_b[:], ident[:])
                    dve.wait_ge(small_in, 96)
                    dve.tensor_tensor(table[:], table[:], bmsg[:], ALU.add)
                    dve.tensor_tensor(brz[:], bih[:, 0:2], bhh[:, 0:2], ALU.add)
                    dve.tensor_scalar(c_x[:], c_x[:], 2.0, None, ALU.add)
                    dve.wait_ge(edges_in, 16 * n_edge_dmas)
                    dve.tensor_copy(dst_f[:], dst_i[:]).then_inc(prep, 1)
                    dve.tensor_scalar(type_f[:], type_i[:], 0.0, float(NT - 1), ALU.max, ALU.min)
                    dve.wait_ge(prep, 1)
                    dve.tensor_scalar(far[:], dst_f[:, last], 0.0, FAR, ALU.is_lt, ALU.mult).then_inc(prep, 1)
                    dve.tensor_reduce(ext[:, NG:2 * NG], dst_f[:].rearrange("p (g j) -> p g j", j=GROUP),
                                      AX.X, ALU.max).then_inc(ext_done, 1)
                    dve.tensor_reduce(ext[:, 0:NG], dst_f[:].rearrange("p (g j) -> p g j", j=GROUP),
                                      AX.X, ALU.min).then_inc(ext_done, 1)
                    dve.wait_ge(prep, 2)
                    dve.tensor_tensor(far[:], far[:], dst_f[:, last], ALU.add).then_inc(prep, 1)
                    dve.wait_ge(prep, 3)
                    dve.wait_ge(ext_done, 2)
                    dve.tensor_reduce(ext[:, full:full + 1], far[:], AX.X, ALU.min).then_inc(ext_done, 1)
                    dve.wait_ge(ext_done, 3)
                    dve.tensor_scalar(ext[:, 0:NG], ext[:, 0:NG], -1.0, None, ALU.mult).then_inc(ext_done, 1)
                    dve.wait_ge(ext_reduced, 1)
                    dve.tensor_scalar(first_f[:], ext_all[:, 0:NG], -1.0, None, ALU.mult)
                    dve.tensor_scalar(first_i[:], ext_all[:, 0:NG], -1.0, None, ALU.mult)
                    dve.tensor_tensor(span_f[:], ext_all[:, NG:2 * NG], ext_all[:, 0:NG], ALU.add).then_inc(prep, 1)
                    dve.wait_ge(prep, 4)
                    dve.tensor_copy(span_i[:], span_f[:]).then_inc(prep, 1)
                    dve.wait_ge(prep, 5)
                    dve.tensor_single_scalar(win_i[:], span_i[:], 7, ALU.arith_shift_right).then_inc(prep, 1)
                    dve.wait_ge(prep, 6)
                    dve.tensor_scalar(nwin_i[:], win_i[:], 1.0, None, ALU.add)

        with ExitStack() as ph:
            got = sb("got0", [P, NC, CHUNK, D], F32, ph)
            hot = sb("hot0", [P, NC, CHUNK, P], F32, ph)
            kind = sb("kind", [P, NC, CHUNK, NT], F32, ph)
            xt_ps = psum("xt_ps", [P, 512], F32, ph)
            sum_ps = psum("sum_ps", [P, 512], F32, ph)
            cnt_ps = psum("cnt_ps", [P, 512], F32, ph)
            idx_in = [sem(f"idx_in0_{c}") for c in range(NC)]
            gathered = [sem(f"gathered0_{c}") for c in range(NC)]
            hot_done = sem("hot_done0")
            summed = sem("summed0")
            added = sem("added0")
            dl_done = sem("dl_done0")
            xt_done = sem("xt_done")
            xt_copied = sem("xt_copied")

            with nc.Block() as block:
                @block.sync
                def _(sp):
                    with every_body(sp, sp.alloc_register("k_sp0")) as (g, j, k):
                        for c in range(NC):
                            sp.wait_ge(summed, NC * k + c + 1)
                            sp.dma_start(idx[:, c, :], src_tab[:, bass.ds(g * GROUP + c * CHUNK, CHUNK)]
                                         ).then_inc(idx_in[c], 16)

                @block.gpsimd
                def _(pool):
                    with every_body(pool, pool.alloc_register("k_pool0")) as (g, j, k):
                        for c in range(NC):
                            pool.wait_ge(idx_in[c], 16 * k + 16)
                            pool.sem_inc(chunk_begun, 1)
                            for i in range(CHUNK):
                                pool.indirect_dma_start(
                                    got[:, c, i, :], None, x,
                                    bass.IndirectOffsetOnAxis(ap=idx[:, c, i:i + 1], axis=0)
                                ).then_inc(gathered[c], 16)

                @block.vector
                def _(dve):
                    dve.sem_inc(dl_done, 1)
                    count = dve.alloc_register("k_dve0")
                    dve.reg_mov(count, 0)
                    dve.sem_inc(added, 2)
                    where = dve.alloc_register("where_dve0")
                    with dve.Fori(0, NG) as g:
                        nw = dve.value_load(nwin_i[0:1, bass.ds(g, 1)], min_val=1, max_val=-(-N // P))
                        base = dve.value_load(first_i[0:1, bass.ds(g, 1)], min_val=0, max_val=N - 1)
                        dve.reg_mov(where, base)
                        dve.wait_ge(dl_done, dve.snap(count, min_val=0, max_val=MAXB) + g + 1)
                        dve.tensor_scalar(dl[:], dst_f[:, bass.ds(g * GROUP, GROUP)],
                                          first_f[:, bass.ds(g, 1)], None, ALU.subtract).then_inc(dl_done, 1)
                        with dve.Fori(0, nw) as j:
                            k = dve.snap(count, min_val=0, max_val=MAXB)
                            dve.wait_ge(dl_done, k + g + 2)
                            for c in range(NC):
                                dve.wait_ge(summed, NC * k + c + 1)
                                dve.tensor_tensor(
                                    kind[:, c, :, :],
                                    type_f[:, bass.ds(g * GROUP + c * CHUNK, CHUNK)].unsqueeze(2)
                                    .to_broadcast([P, CHUNK, NT]),
                                    iota_f[:, 0:NT].unsqueeze(1).to_broadcast([P, CHUNK, NT]), ALU.is_equal)
                                dve.tensor_tensor(
                                    hot[:, c, :, :],
                                    iota_f[:].unsqueeze(1).to_broadcast([P, CHUNK, P]),
                                    dl[:, c * CHUNK:(c + 1) * CHUNK].unsqueeze(2).to_broadcast([P, CHUNK, P]),
                                    ALU.is_equal).then_inc(hot_done, 1)
                            dve.wait_ge(hot_done, NC * k + NC)
                            dve.tensor_scalar(dl[:], dl[:], float(P), None, ALU.subtract).then_inc(dl_done, 1)
                            dve.wait_ge(summed, NC * k + 2 * NC)
                            dve.wait_ge(added, 2 * k + 2)
                            at = dve.snap(where, min_val=0, max_val=N - 1)
                            dve.tensor_tensor(sums[:, bass.ds(at, P)], sums[:, bass.ds(at, P)],
                                              sum_ps[:, 0:P], ALU.add).then_inc(added, 1)
                            dve.tensor_tensor(counts[:, bass.ds(at, P)], counts[:, bass.ds(at, P)],
                                              cnt_ps[0:NT, 0:P], ALU.add).then_inc(added, 1)
                            dve.reg_add(where, where, P)
                            dve.reg_add(count, count, 1)

                @block.scalar
                def _(act):
                    act.sem_inc(xt_copied, 1)
                    with act.Fori(0, NQ) as q:
                        act.wait_ge(xt_done, q + 1)
                        act.copy(work[:, bass.ds(q * QN, QN)], xt_ps[:, 0:QN]).then_inc(xt_copied, 1)

                @block.tensor
                def _(pe):
                    for q in range(NQ):
                        pe.wait_ge(xt_copied, q + 1)
                        for i in range(QUAD):
                            t = pe.transpose(xt_ps[:, i * NODES:(i + 1) * NODES],
                                             nodes[:, q * QUAD + i, :],
                                             ident[0:NODES, 0:NODES])
                        t.then_inc(xt_done, 1)
                    pe.sem_inc(summed, NC)
                    with every_body(pe, pe.alloc_register("k_pe0")) as (g, j, k):
                        pe.wait_ge(added, 2 * k + 2)
                        for c in range(NC):
                            pe.wait_ge(gathered[c], 16 * CHUNK * k + 16 * CHUNK)
                            pe.wait_ge(hot_done, NC * k + c + 1)
                            for i in range(CHUNK):
                                n = c * CHUNK + i
                                pe.matmul(cnt_ps[0:NT, 0:P], kind[:, c, i, :], hot[:, c, i, :],
                                          start=(n == 0), stop=(n == GROUP - 1))
                                mm = pe.matmul(sum_ps[:, 0:P], got[:, c, i, :], hot[:, c, i, :],
                                               start=(n == 0), stop=(n == GROUP - 1))
                            mm.then_inc(summed, 1)

        with ExitStack() as ph:
            msg = sb("msg", [P, QN], F32, ph)
            r_s = sb("r_s", [P, QN], F32, ph)
            z_s = sb("z_s", [P, QN], F32, ph)
            n_s = sb("n_s", [P, QN], F32, ph)
            t_s = sb("t_s", [P, QN], F32, ph)
            d_s = sb("d_s", [P, QN], F32, ph)
            msg_ps = psum("msg_ps", [P, 512], F32, ph)
            r_ps = psum("r_ps", [P, 512], F32, ph)
            z_ps = psum("z_ps", [P, 512], F32, ph)
            i_ps = psum("i_ps", [P, 512], F32, ph)
            h_ps = psum("h_ps", [P, 512], F32, ph)
            msg_done = sem("msg_done")
            msg_copied = sem("msg_copied")
            gates = sem("gates")
            r_done = sem("r_done")
            z_done = sem("z_done")
            pre_done = sem("pre_done")
            n_done = sem("n_done")
            y_done = sem("y_done")

            with nc.Block() as block:
                @block.tensor
                def _(pe):
                    pe.sem_inc(gates, 3)
                    with pe.Fori(0, NQ) as q:
                        cols = bass.ds(q * QN, QN)
                        pe.wait_ge(msg_copied, q + 1)
                        pe.matmul(msg_ps[:, 0:QN], wT[:, 0, :], sums[:, cols], start=True, stop=False)
                        pe.matmul(msg_ps[:, 0:QN], table[:], counts[:, cols], start=False, stop=True
                                  ).then_inc(msg_done, 1)
                        pe.wait_ge(z_done, q + 1)
                        pe.wait_ge(pre_done, 2 * q + 2)
                        pe.matmul(r_ps[:, 0:QN], wT[:, 5, :], work[:, cols], start=True, stop=False)
                        pe.matmul(z_ps[:, 0:QN], wT[:, 6, :], work[:, cols], start=True, stop=False)
                        pe.matmul(h_ps[:, 0:QN], wT[:, 7, :], work[:, cols], start=True, stop=True)
                        pe.wait_ge(msg_copied, q + 2)
                        pe.matmul(r_ps[:, 0:QN], wT[:, 2, :], msg[:], start=False, stop=True).then_inc(gates, 1)
                        pe.matmul(i_ps[:, 0:QN], wT[:, 4, :], msg[:], start=True, stop=True).then_inc(gates, 1)
                        pe.matmul(z_ps[:, 0:QN], wT[:, 3, :], msg[:], start=False, stop=True).then_inc(gates, 1)

                @block.scalar
                def _(act):
                    act.sem_inc(msg_copied, 1)
                    act.sem_inc(z_done, 1)
                    with act.Fori(0, NQ) as q:
                        act.wait_ge(msg_done, q + 1)
                        act.wait_ge(gates, 3 * q + 3)
                        act.copy(msg[:], msg_ps[:, 0:QN]).then_inc(msg_copied, 1)
                        act.wait_ge(gates, 3 * q + 4)
                        act.activation(r_s[:], r_ps[:, 0:QN], ACT.Sigmoid, bias=brz[:, 0:1]).then_inc(r_done, 1)
                        act.wait_ge(gates, 3 * q + 6)
                        act.wait_ge(y_done, 4 * q + 4)
                        act.activation(z_s[:], z_ps[:, 0:QN], ACT.Sigmoid, bias=brz[:, 1:2]).then_inc(z_done, 1)
                        act.wait_ge(pre_done, 2 * q + 4)
                        act.activation(n_s[:], t_s[:], ACT.Tanh, bias=bih[:, 2:3]).then_inc(n_done, 1)

                @block.vector
                def _(dve):
                    dve.sem_inc(pre_done, 2)
                    dve.sem_inc(y_done, 4)
                    with dve.Fori(0, NQ) as q:
                        cols = bass.ds(q * QN, QN)
                        dve.wait_ge(r_done, q + 1)
                        dve.wait_ge(gates, 3 * q + 5)
                        dve.scalar_tensor_tensor(out=t_s[:], in0=h_ps[:, 0:QN], scalar=bhh[:, 2:3], in1=r_s[:],
                                                 op0=ALU.add, op1=ALU.mult).then_inc(pre_done, 1)
                        dve.wait_ge(pre_done, 2 * q + 3)
                        dve.tensor_tensor(t_s[:], t_s[:], i_ps[:, 0:QN], ALU.add).then_inc(pre_done, 1)
                        dve.wait_ge(n_done, q + 1)
                        dve.wait_ge(z_done, q + 2)
                        dve.tensor_tensor(d_s[:], work[:, cols], n_s[:], ALU.subtract).then_inc(y_done, 1)
                        dve.wait_ge(y_done, 4 * q + 5)
                        dve.tensor_tensor(d_s[:], d_s[:], z_s[:], ALU.mult).then_inc(y_done, 1)
                        dve.wait_ge(y_done, 4 * q + 6)
                        dve.tensor_tensor(d_s[:], d_s[:], n_s[:], ALU.add).then_inc(y_done, 1)
                        dve.wait_ge(y_done, 4 * q + 7)
                        dve.tensor_tensor(work[:, cols], work[:, cols], d_s[:], ALU.add).then_inc(y_done, 1)

        with ExitStack() as ph:
            y_ps = psum("y_ps", [NODES, QUAD, D], F32, ph)
            deg_ps = psum("deg_ps", [NODES, 512], F32, ph)
            y_turned = sem("y_turned")
            y_copied = sem("y_copied")
            stats_done = sem("stats_done")
            aggr_done = sem("aggr_done")
            spread = sem("spread0")

            with nc.Block() as block:
                @block.tensor
                def _(pe):
                    for q in range(NQ):
                        pe.wait_ge(y_copied, q + 1)
                        for i in range(QUAD):
                            tile = q * QUAD + i
                            pe.matmul(deg_ps[:, tile:tile + 1], counts[:, tile * NODES:(tile + 1) * NODES],
                                      ones[:], start=True, stop=True)
                            t = pe.transpose(y_ps[:, i, :], work[:, tile * NODES:(tile + 1) * NODES], ident[:])
                        t.then_inc(y_turned, 1)

                @block.scalar
                def _(act):
                    act.sem_inc(y_copied, 1)
                    with act.Fori(0, NQ) as q:
                        act.wait_ge(y_turned, q + 1)
                        act.copy(nodes[:, bass.ds(q * QUAD, QUAD), :], y_ps[:]).then_inc(y_copied, 1)
                    act.wait_ge(spread, 1)
                    act.activation(rstd[:], rstd[:], ACT.Sqrt).then_inc(spread, 1)

                @block.vector
                def _(dve):
                    for q in range(NQ):
                        dve.wait_ge(y_copied, q + 2)
                        if q:
                            dve.wait_ge(aggr_done, QUAD * q)
                        for i in range(QUAD):
                            dve.bn_stats(stats[:, i, :], nodes[:, q * QUAD + i, :]).then_inc(stats_done, 1)
                        for i in range(QUAD):
                            dve.wait_ge(stats_done, QUAD * q + i + 1)
                            dve.bn_aggr(moments[:, q * QUAD + i, :], stats[:, i, :]).then_inc(aggr_done, 1)
                    dve.wait_ge(aggr_done, NTL)
                    dve.tensor_scalar(rstd[:], moments[:, :, 1], LN_EPS, None, ALU.add).then_inc(spread, 1)
                    dve.tensor_scalar(rdeg[:], deg_ps[:, 0:NTL], 1.0, None, ALU.max).then_inc(stats_done, 1)
                    dve.wait_ge(stats_done, NTL + 1)
                    dve.reciprocal(rdeg[:], rdeg[:])
                    dve.wait_ge(spread, 2)
                    dve.reciprocal(rstd[:], rstd[:])

        proj = work[0:NODES, 0:NTL * D].rearrange("p (t f) -> p t f", f=D)
        with ExitStack() as ph:
            f_s = sb("f_s", [P, 2, QN], F32, ph)
            rest = sb("rest", [NODES, 2, QUAD, D], F32, ph)
            split = sb("split", [NODES, 2, QUAD, 3, D], BF16, ph)
            f_ps = psum("f_ps", [P, 2, 512], F32, ph)
            p_ps = psum("p_ps", [NODES, 2, QUAD, D], F32, ph)
            normed = sem("normed")
            f_turned = sem("f_turned")
            f_copied = sem("f_copied")
            p_done = sem("p_done")
            p_copied = sem("p_copied")
            cut = sem("cut")
            feat_out = sem("feat_out")
            proj_out = sem("proj_out")
            parts_out = [sem(f"parts_out{b}") for b in range(2)]
            rows_q = rows[0:NTL * NODES, :].rearrange("(t p) f -> p t f", p=NODES)
            parts_q = parts[0:NTL * NODES, :].rearrange("(t p) (s f) -> p t s f", p=NODES, s=3)

            with nc.Block() as block:
                @block.vector
                def _(dve):
                    with dve.Fori(0, NQ) as q:
                        for i in range(QUAD):
                            t = bass.ds(q * QUAD + i, 1)
                            dve.tensor_scalar(nodes[:, t, :].squeeze(1), nodes[:, t, :].squeeze(1),
                                              moments[:, t, 0], rstd[:, t], ALU.subtract, ALU.mult
                                              ).then_inc(normed, 1)
                    with dve.Fori(0, NQ // 2) as h:
                        for b in range(2):
                            q = h * 2 + b
                            pr = proj[:, bass.ds(q * QUAD, QUAD), :]
                            dve.wait_ge(p_copied, q + 3)
                            dve.wait_ge(parts_out[b], 16 * h + 16)
                            dve.tensor_copy(split[:, b, :, 0, :], pr).then_inc(cut, 1)
                            dve.wait_ge(cut, 4 * q + 1)
                            dve.tensor_tensor(rest[:, b, :, :], pr, split[:, b, :, 0, :], ALU.subtract
                                              ).then_inc(cut, 1)
                            dve.wait_ge(cut, 4 * q + 2)
                            dve.tensor_copy(split[:, b, :, 1, :], rest[:, b, :, :]).then_inc(cut, 1)
                            dve.wait_ge(cut, 4 * q + 3)
                            dve.tensor_tensor(split[:, b, :, 2, :], rest[:, b, :, :], split[:, b, :, 1, :],
                                              ALU.subtract).then_inc(cut, 1)

                @block.tensor
                def _(pe):
                    pe.sem_inc(p_done, 2)
                    for h in range(NQ // 2):
                        for b in range(2):
                            q = h * 2 + b
                            pe.wait_ge(normed, QUAD * q + QUAD)
                            pe.wait_ge(f_copied, q + 1)
                            for i in range(QUAD):
                                t = pe.transpose(f_ps[:, b, i * NODES:(i + 1) * NODES],
                                                 nodes[:, q * QUAD + i, :],
                                                 ident[0:NODES, 0:NODES])
                            t.then_inc(f_turned, 1)
                            pe.wait_ge(f_copied, q + 3)
                            pe.wait_ge(p_copied, q + 1)
                            for i in range(QUAD):
                                mm = pe.matmul(p_ps[:, b, i, :], f_s[:, b, i * NODES:(i + 1) * NODES], wT[:, 1, :],
                                               start=True, stop=True)
                            mm.then_inc(p_done, 1)

                @block.scalar
                def _(act):
                    act.sem_inc(f_copied, 2)
                    act.sem_inc(p_copied, 2)
                    with act.Fori(0, NQ // 2) as h:
                        for b in range(2):
                            q = h * 2 + b
                            act.wait_ge(f_turned, q + 1)
                            act.wait_ge(p_done, q + 1)
                            act.copy(f_s[:, b, :], f_ps[:, b, 0:QN]).then_inc(f_copied, 1)
                            act.wait_ge(p_done, q + 3)
                            act.copy(proj[:, bass.ds(q * QUAD, QUAD), :], p_ps[:, b, :, :]).then_inc(p_copied, 1)

                @block.sync
                def _(sp):
                    for b in range(2):
                        sp.sem_inc(parts_out[b], 16)
                    with sp.Fori(0, NQ // 2) as h:
                        for b in range(2):
                            q = h * 2 + b
                            t = bass.ds(q * QUAD, QUAD)
                            sp.wait_ge(normed, QUAD * q + QUAD)
                            sp.dma_start(rows_q[:, t, D:2 * D], nodes[:, t, :]).then_inc(feat_out, 16)
                            sp.wait_ge(p_copied, q + 3)
                            sp.dma_start(rows_q[:, t, 0:D], proj[:, t, :]).then_inc(proj_out, 16)
                            sp.wait_ge(cut, 4 * q + 4)
                            sp.dma_start(parts_q[:, t, :, :], split[:, b, :, :, :]).then_inc(parts_out[b], 16)
                    sp.wait_ge(feat_out, 16 * NQ)
                    sp.wait_ge(proj_out, 16 * NQ)
                    for b in range(2):
                        sp.wait_ge(parts_out[b], 16 * (NQ // 2) + 16)

        with ExitStack() as ph:
            got = sb("got1", [P, NC, CHUNK, 2 * D], F32, ph)
            hot = sb("hot1", [P, NC, CHUNK, P], BF16, ph)
            hot_t = sb("hot_t", [P, 2, CHUNK, P], BF16, ph)
            whot = sb("whot", [P, 2, CHUNK, P], F32, ph)
            win_in = sb("win_in", [P, 3, D], BF16, ph)
            win = sb("win", [P, 3, D], BF16, ph)
            s_s = sb("s_s", [P, CHUNK, D], F32, ph)
            l_s = sb("l_s", [P, CHUNK, D], F32, ph)
            pr_s = sb("pr_s", [P, CHUNK, D], F32, ph)
            q_s = sb("q_s", [P, NC, CHUNK], F32, ph)
            e_s = sb("e_s", [P, NC, CHUNK], F32, ph)
            gate_s = sb("gate_s", [P, NC, CHUNK], F32, ph)
            eg_s = sb("eg_s", [P, NC, CHUNK], F32, ph)
            w_s = sb("w_s", [P, NC, CHUNK], F32, ph)
            hot_ps = psum("hot_ps", [P, 2, 1024], BF16, ph)
            er_ps = psum("er_ps", [P, 2, 1024], F32, ph)
            sum_ps = psum("sum_ps1", [P, 512], F32, ph)
            idx_in = [sem(f"idx_in1_{c}") for c in range(NC)]
            gathered = [sem(f"gathered1_{c}") for c in range(NC)]
            win_loaded = sem("win_loaded")
            win_copied = sem("win_copied")
            dl_done = sem("dl_done1")
            hot_done = sem("hot_done1")
            turned = sem("turned")
            hot_copied = sem("hot_copied")
            er_done = sem("er_done")
            s_done = sem("s_done")
            q_done = sem("q_done")
            l_done = sem("l_done")
            e_done = sem("e_done")
            gate_done = sem("gate_done")
            eg_done = sem("eg_done")
            w_done = sem("w_done")
            whot_done = sem("whot_done")
            summed = sem("summed1")
            bank_zero = sem("bank_zero")
            added = sem("added1")

            with nc.Block() as block:
                @block.sync
                def _(sp):
                    count = sp.alloc_register("k_sp1")
                    sp.reg_mov(count, 0)
                    where = sp.alloc_register("where_sp1")
                    with sp.Fori(0, NG) as g:
                        nw = sp.value_load(nwin_i[0:1, bass.ds(g, 1)], min_val=1, max_val=-(-N // P))
                        base = sp.value_load(first_i[0:1, bass.ds(g, 1)], min_val=0, max_val=N - 1)
                        sp.reg_mov(where, base)
                        with sp.Fori(0, nw) as j:
                            k = sp.snap(count, min_val=0, max_val=MAXB)
                            at = sp.snap(where, min_val=0, max_val=N - 1)
                            sp.wait_ge(win_copied, k + 1)
                            sp.dma_start(win_in[:].rearrange("p s f -> p (s f)"), parts[bass.ds(at, P), :]
                                         ).then_inc(win_loaded, 16)
                            for c in range(NC):
                                sp.wait_ge(summed, NC * k + c + 1)
                                sp.dma_start(idx[:, c, :], src_tab[:, bass.ds(g * GROUP + c * CHUNK, CHUNK)]
                                             ).then_inc(idx_in[c], 16)
                            sp.reg_add(where, where, P)
                            sp.reg_add(count, count, 1)

                @block.gpsimd
                def _(pool):
                    with every_body(pool, pool.alloc_register("k_pool1")) as (g, j, k):
                        for c in range(NC):
                            pool.wait_ge(idx_in[c], 16 * k + 16)
                            pool.sem_inc(chunk_begun, 1)
                            for i in range(CHUNK):
                                pool.indirect_dma_start(
                                    got[:, c, i, :], None, rows,
                                    bass.IndirectOffsetOnAxis(ap=idx[:, c, i:i + 1], axis=0)
                                ).then_inc(gathered[c], 16)

                @block.vector
                def _(dve):
                    def one_hot(c, k):
                        dve.wait_ge(whot_done, NC * k + c + 1)
                        dve.tensor_tensor(
                            hot[:, c, :, :],
                            iota_f[:].unsqueeze(1).to_broadcast([P, CHUNK, P]),
                            dl[:, c * CHUNK:(c + 1) * CHUNK].unsqueeze(2).to_broadcast([P, CHUNK, P]),
                            ALU.is_equal).then_inc(hot_done, 1)

                    def add_body(at, k):
                        dve.wait_ge(summed, NC * k + NC)
                        dve.tensor_tensor(sums[:, bass.ds(at, P)], sums[:, bass.ds(at, P)],
                                          sum_ps[:, 0:P], ALU.add).then_inc(added, 1)

                    dve.memset(sums[:], 0.0).then_inc(bank_zero, 1)
                    dve.memset(sum_ps[:, 0:P], 0.0).then_inc(bank_zero, 1)
                    dve.wait_ge(bank_zero, 2)
                    dve.sem_inc(q_done, 2)
                    dve.sem_inc(dl_done, 1)
                    count = dve.alloc_register("k_dve1")
                    dve.reg_mov(count, 0)
                    where = dve.alloc_register("where_dve1")
                    before = dve.alloc_register("before_dve1")
                    dve.reg_mov(before, 0)
                    with dve.Fori(0, NG) as g:
                        nw = dve.value_load(nwin_i[0:1, bass.ds(g, 1)], min_val=1, max_val=-(-N // P))
                        base = dve.value_load(first_i[0:1, bass.ds(g, 1)], min_val=0, max_val=N - 1)
                        dve.reg_mov(where, base)
                        dve.wait_ge(dl_done, dve.snap(count, min_val=0, max_val=MAXB) + g + 1)
                        dve.tensor_scalar(dl[:], dst_f[:, bass.ds(g * GROUP, GROUP)],
                                          first_f[:, bass.ds(g, 1)], None, ALU.subtract).then_inc(dl_done, 1)
                        with dve.Fori(0, nw) as j:
                            k = dve.snap(count, min_val=0, max_val=MAXB)
                            dve.wait_ge(dl_done, k + g + 2)
                            one_hot(0, k)
                            one_hot(1, k)
                            for c in range(NC):
                                n = NC * k + c
                                el = got[:, c, :, 0:D]
                                er = er_ps[:, c % 2, 0:CHUNK * D].rearrange("p (i f) -> p i f", f=D)
                                dve.wait_ge(gathered[c], 16 * CHUNK * k + 16 * CHUNK)
                                dve.wait_ge(er_done, n + NC + 1)
                                dve.tensor_tensor(s_s[:], el, er, ALU.add).then_inc(s_done, 1)
                                for i in range(CHUNK):
                                    mm = dve.tensor_tensor_reduce(pr_s[:, i, :], el[:, i, :], er[:, i, :], 1.0, 0.0,
                                                                  ALU.mult, ALU.add, q_s[:, c, i:i + 1])
                                mm.then_inc(q_done, 1)
                                dve.wait_ge(s_done, n + 1)
                                dve.scalar_tensor_tensor(out=l_s[:], in0=s_s[:], scalar=LEAK, in1=s_s[:],
                                                         op0=ALU.mult, op1=ALU.max).then_inc(l_done, 1)
                                if c + 2 < NC:
                                    one_hot(c + 2, k)
                                dve.wait_ge(l_done, n + 1)
                                for i in range(CHUNK):
                                    mm = dve.tensor_tensor_reduce(l_s[:, i, :], l_s[:, i, :], a_all[:], 1.0, 0.0,
                                                                  ALU.mult, ALU.add, e_s[:, c, i:i + 1])
                                mm.then_inc(e_done, 1)
                                if c == 0:
                                    add_body(dve.snap(before, min_val=0, max_val=N - 1), k)
                                dve.wait_ge(gate_done, n + 1)
                                dve.wait_ge(e_done, n + 1)
                                dve.tensor_tensor(eg_s[:, c, :], e_s[:, c, :], gate_s[:, c, :], ALU.mult
                                                  ).then_inc(eg_done, 1)
                            dve.wait_ge(hot_done, NC * k + NC)
                            dve.tensor_scalar(dl[:], dl[:], float(P), None, ALU.subtract).then_inc(dl_done, 1)
                            dve.reg_add(count, count, 1)
                            dve.reg_mov(before, dve.snap(where, min_val=0, max_val=N - 1))
                            dve.reg_add(where, where, P)
                    add_body(dve.snap(before, min_val=0, max_val=N - 1), dve.snap(count, min_val=0, max_val=MAXB))

                @block.scalar
                def _(act):
                    def copy_hot(c, k):
                        n = NC * k + c
                        act.wait_ge(turned, n + 1)
                        act.wait_ge(er_done, n + NC - 1)
                        act.copy(hot_t[:, c % 2, :, :],
                                 hot_ps[:, c % 2, 0:CHUNK * P].rearrange("p (i e) -> p i e", e=P)
                                 ).then_inc(hot_copied, 1)

                    act.sem_inc(win_copied, 1)
                    act.sem_inc(hot_copied, 2)
                    act.sem_inc(whot_done, NC)
                    with every_body(act, act.alloc_register("k_act1")) as (g, j, k):
                        act.wait_ge(win_loaded, 16 * k + 16)
                        act.wait_ge(er_done, NC * k + NC)
                        act.copy(win[:], win_in[:]).then_inc(win_copied, 1)
                        copy_hot(0, k)
                        for c in range(NC):
                            n = NC * k + c
                            if c + 1 < NC:
                                copy_hot(c + 1, k)
                            act.wait_ge(q_done, n + 3)
                            act.activation(gate_s[:, c, :], q_s[:, c, :], ACT.Sigmoid).then_inc(gate_done, 1)
                            act.wait_ge(eg_done, n + 1)
                            act.activation(w_s[:, c, :], eg_s[:, c, :], ACT.Sigmoid).then_inc(w_done, 1)
                            act.wait_ge(w_done, n + 1)
                            act.wait_ge(summed, n + NC - 1)
                            for i in range(CHUNK):
                                m = act.activation(whot[:, c % 2, i, :], hot[:, c, i, :], ACT.Copy,
                                                   scale=w_s[:, c, i:i + 1])
                            m.then_inc(whot_done, 1)

                @block.tensor
                def _(pe):
                    def turn(c, k):
                        n = NC * k + c
                        pe.wait_ge(hot_done, n + 1)
                        pe.wait_ge(hot_copied, n + 1)
                        for i in range(CHUNK):
                            t = pe.transpose(hot_ps[:, c % 2, i * P:(i + 1) * P], hot[:, c, i, :], ident_b[:])
                        t.then_inc(turned, 1)

                    def sum_chunk(c, k):
                        n = NC * k + c
                        if c == 0:
                            pe.wait_ge(added, k + 1)
                        pe.wait_ge(whot_done, n + NC + 1)
                        pe.wait_ge(gathered[c], 16 * CHUNK * k + 16 * CHUNK)
                        for i in range(CHUNK):
                            mm = pe.matmul(sum_ps[:, 0:P], got[:, c, i, D:2 * D], whot[:, c % 2, i, :],
                                           start=(c == 0 and i == 0), stop=(c == NC - 1 and i == CHUNK - 1))
                        mm.then_inc(summed, 1)

                    pe.sem_inc(er_done, NC)
                    pe.sem_inc(summed, NC)
                    with every_body(pe, pe.alloc_register("k_pe1")) as (g, j, k):
                        turn(0, k)
                        pe.wait_ge(win_copied, k + 2)
                        for c in range(NC):
                            n = NC * k + c
                            if c + 1 < NC:
                                turn(c + 1, k)
                            pe.wait_ge(hot_copied, n + 3)
                            pe.wait_ge(q_done, n + 1)
                            for i in range(CHUNK):
                                for part in range(3):
                                    mm = pe.matmul(er_ps[:, c % 2, i * D:(i + 1) * D], hot_t[:, c % 2, i, :],
                                                   win[:, part, :], start=(part == 0), stop=(part == 2))
                            mm.then_inc(er_done, 1)
                            if c:
                                sum_chunk(c - 1, k)
                        sum_chunk(NC - 1, k)

        with ExitStack() as ph:
            mean_s = sb("mean_s", [NODES, QUAD, D], F32, ph)
            m_ps = psum("m_ps", [NODES, QUAD, D], F32, ph)
            m_turned = sem("m_turned")
            steps = sem("steps")
            spread = sem("spread1")
            finished = sem("finished")
            stored = sem("stored")
            S = 2 + 2 * QUAD

            with nc.Block() as block:
                @block.tensor
                def _(pe):
                    for q in range(NQ):
                        pe.wait_ge(steps, S * q + 1)
                        for i in range(QUAD):
                            tile = q * QUAD + i
                            t = pe.transpose(m_ps[:, i, :], sums[:, tile * NODES:(tile + 1) * NODES], ident[:])
                        t.then_inc(m_turned, 1)

                @block.scalar
                def _(act):
                    act.wait_ge(spread, 1)
                    act.activation(rstd[:], rstd[:], ACT.Sqrt).then_inc(spread, 1)

                @block.vector
                def _(dve):
                    dve.sem_inc(steps, 1)
                    for q in range(NQ):
                        t = slice(q * QUAD, (q + 1) * QUAD)
                        dve.wait_ge(m_turned, q + 1)
                        dve.wait_ge(steps, S * q + 1)
                        dve.tensor_tensor(mean_s[:], m_ps[:],
                                          rdeg[:, t].unsqueeze(2).to_broadcast([NODES, QUAD, D]), ALU.mult
                                          ).then_inc(steps, 1)
                        dve.wait_ge(steps, S * q + 2)
                        dve.scalar_tensor_tensor(out=nodes[:, t, :], in0=nodes[:, t, :], scalar=c_x[:],
                                                 in1=mean_s[:], op0=ALU.mult, op1=ALU.add).then_inc(steps, 1)
                        dve.wait_ge(steps, S * q + 3)
                        for i in range(QUAD):
                            dve.bn_stats(stats[:, i, :], nodes[:, q * QUAD + i, :]).then_inc(steps, 1)
                        for i in range(QUAD):
                            dve.wait_ge(steps, S * q + 4 + i)
                            dve.bn_aggr(moments[:, q * QUAD + i, :], stats[:, i, :]).then_inc(steps, 1)
                    dve.wait_ge(steps, S * NQ + 1)
                    dve.tensor_scalar(rstd[:], moments[:, :, 1], LN_EPS, None, ALU.add).then_inc(spread, 1)
                    dve.wait_ge(spread, 2)
                    dve.reciprocal(rstd[:], rstd[:]).then_inc(spread, 1)
                    dve.wait_ge(spread, 3)
                    with dve.Fori(0, NTL) as t:
                        one = bass.ds(t, 1)
                        dve.tensor_scalar(nodes[:, one, :].squeeze(1), nodes[:, one, :].squeeze(1),
                                          moments[:, one, 0], rstd[:, one], ALU.subtract, ALU.mult
                                          ).then_inc(finished, 1)

                @block.sync
                def _(sp):
                    at, n = 0, 0
                    while at < ft:
                        m = min(2 * QUAD, ft - at)
                        sp.wait_ge(finished, at + m)
                        sp.dma_start(out[at * NODES:(at + m) * NODES, :].rearrange("(t p) f -> p t f", p=NODES),
                                     nodes[:, at:at + m, :]).then_inc(stored, 16)
                        at, n = at + m, n + 1
                    if fr:
                        sp.wait_ge(finished, ft + 1)
                        sp.dma_start(out[ft * NODES:N, :], nodes[0:fr, ft, :]).then_inc(stored, 16)
                        n += 1
                    sp.wait_ge(stored, 16 * n)


_INS = ['x', 'src', 'dst', 'edge_type_9', 'L0_gnn_W_msg', 'L0_gnn_b_msg', 'L0_gnn_edge_embed', 'L0_gnn_W_ih',
        'L0_gnn_W_hh', 'L0_gnn_b_ih', 'L0_gnn_b_hh', 'L1_gnn_fc_weight', 'L1_gnn_attn', 'L1_gnn_eps']


def kernel(**inputs):
    import numpy as _np
    import concourse.bacc as _bacc
    from concourse import mybir as _mybir
    from concourse.bass_utils import run_bass_kernel_spmd as _run

    nc = _bacc.Bacc("TRN2", target_bir_lowering=False, num_devices=1)
    arrays, args = {}, []
    for name in _INS:
        a = _np.ascontiguousarray(inputs[name])
        arrays[f"in_{name}_dram"] = a
        args.append(nc.dram_tensor(f"in_{name}_dram", a.shape, _mybir.dt.from_np(a.dtype), kind="ExternalInput").ap())
    out = nc.dram_tensor("out_0_dram", inputs['x'].shape, _mybir.dt.float32, kind="ExternalOutput").ap()
    graph_layers(nc, *args, out)
    r = _run(nc, [arrays], core_ids=[0])
    return r.results[0]["out_0_dram"]
```

```python
from contextlib import ExitStack, contextmanager

import concourse.bass as bass
from concourse import mybir

F32 = mybir.dt.float32
F16 = mybir.dt.float16
BF16 = mybir.dt.bfloat16
I32 = mybir.dt.int32
ALU = mybir.AluOpType
ACT = mybir.ActivationFunctionType
AX = mybir.AxisListType
RMAX = bass.bass_isa.ReduceOp.max

P = 128
CHUNK = 7
NC = 4
GROUP = CHUNK * NC
NODES = P
QUAD = 4
WIN = 16
WINS = P // WIN
WT = 6
UT = 3
RING = 4
HALF = WINS // 2
SIXTH = 10923
COUNTED = 0.53
LN_EPS = 1e-5
LEAK = 0.2
FAR = 1.0e6


def graph_layers(nc, x, src, dst, edge_type, W_msg, b_msg, edge_embed, W_ih, W_hh, b_ih, b_hh,
                 fc_weight, attn, eps, out):
    N, D = x.shape
    E = src.shape[0]
    NT = edge_embed.shape[0]
    assert D == P and W_ih.shape == (3 * D, D)
    NG = -(-E // (P * GROUP))
    TILES = NG * GROUP
    QN = QUAD * NODES
    NQ = -(-N // QN)
    NTL = NQ * QUAD
    SPANS = -(-N // P)
    NPAD = max(NTL * NODES, (SPANS + 1) * P)
    MAXB = NG * (-(-N // P))
    KW = -(-(MAXB + 1) // P)
    GC = max(1, min(NG - 1, round(COUNTED * NG)))
    CT = GC * GROUP
    NBK = -(-(CT + WT) // P)
    CTX = NBK * P
    CODES = SPANS * WIN
    BANK = 512
    WC = -(-((SPANS + 1) * WINS) // P)
    WIDE = max(NPAD, NTL * D, 2 * D + 6 * CTX)
    NOWHERE = (SPANS + 2) * P
    MAXR = -(-CT // WT)
    MAXT = max(MAXB, SPANS * MAXR)
    assert NG > 1 and N > P and CTX * SIXTH < 2 ** 24 and BANK < CODES <= 2 * BANK or N < 6250

    rows = nc.dram_tensor("rows", [NPAD, 2 * D], F32).ap()
    parts = nc.dram_tensor("parts", [NPAD, 3 * D], BF16).ap()

    first_of = nc.dram_tensor("first_of", [1, P * KW], I32).ap()
    column_of = nc.dram_tensor("column_of", [1, P * KW], I32).ap()
    first_row = nc.dram_tensor("first_row", [1, P * KW], F32).ap()

    tile_ext = nc.dram_tensor("tile_ext", [2, CTX], F32).ap()
    win_ext = nc.dram_tensor("win_ext", [2, WC * P], F32).ap()
    start_of = nc.dram_tensor("start_of", [1, WC * P], I32).ap()
    rounds_of = nc.dram_tensor("rounds_of", [1, SPANS + 1], I32).ap()

    with ExitStack() as whole:
        def sb(name, shape, dt, ctx=whole):
            return ctx.enter_context(nc.sbuf_tensor(name, shape, dt))

        def psum(name, shape, dt, ctx):
            return ctx.enter_context(nc.psum_tensor(name, shape, dt))

        def sem(name):
            return whole.enter_context(nc.semaphore(name))

        nodes = sb("nodes", [NODES, NTL, D], F32)
        work = sb("work", [P, WIDE], F32)
        sums = sb("sums", [P, max(NPAD, 3 * CTX + 2 * KW * NG)], F32)
        counts = sb("counts", [NT, NPAD], F32)
        src_tab = sb("src_tab", [P, TILES], I32)
        dst_f = sb("dst_f", [P, TILES], F32)
        type_f = sb("type_f", [P, TILES], F32)
        first_f = sb("first_f", [P, P * KW], F32)
        bodies_i = sb("bodies_i", [P, 1], I32)
        trips_i = sb("trips_i", [P, 1], I32)
        skip_i = sb("skip_i", [P, 1], I32)
        iota_f = sb("iota_f", [P, P], F32)
        ident = sb("ident", [P, P], F32)
        ident_b = sb("ident_b", [P, P], BF16)
        wT = sb("wT", [P, 8, D], F32)
        table = sb("table", [NT, D], F32)
        bih = sb("bih", [P, 3], F32)
        bhh = sb("bhh", [P, 3], F32)
        brz = sb("brz", [P, 2], F32)
        a_all = sb("a_all", [P, D], F32)
        c_x = sb("c_x", [NODES, 1], F32)
        ones = sb("ones", [NT, 1], F32)
        rdeg = sb("rdeg", [NODES, NTL], F32)
        stats = sb("stats", [NODES, QUAD, 6], F32)
        moments = sb("moments", [NODES, NTL, 2], F32)
        rstd = sb("rstd", [NODES, NTL], F32)
        dl = sb("dl", [P, GROUP], F32)
        idx = sb("idx", [P, NC, CHUNK], I32)

        chunk_begun = sem("chunk_begun")

        @contextmanager
        def every_body(eng):
            bodies = eng.value_load(bodies_i[0:1, 0:1], min_val=1, max_val=MAXB)
            with eng.Fori(0, bodies) as k:
                yield k

        def node_of(eng, k):
            return eng.value_load(first_of[:, bass.ds(k, 1)], min_val=0, max_val=N - 1)

        def column(eng, k):
            return eng.value_load(column_of[:, bass.ds(k, 1)], min_val=0, max_val=TILES - GROUP)

        layer0 = whole.enter_context(ExitStack())
        packed = sb("packed", [P, CTX, 5], F16, layer0)
        codes_f = sb("codes_f", [P, CODES], F16, layer0)
        iota_h = sb("iota_h", [P, P], F16, layer0)
        span_no = sb("span_no", [P, SPANS + 1], F32, layer0)
        zero_b = sb("zero_b", [P, P], BF16, layer0)

        with ExitStack() as ph:
            dst_i = sb("dst_i", [P, TILES], I32, ph)
            type_i = sb("type_i", [P, TILES], I32, ph)
            iota_i = sb("iota_i", [P, P], I32, ph)
            codes_i = sb("codes_i", [P, max(CTX, CODES)], I32, ph)
            win_no_i = sb("win_no_i", [P, WC], I32, ph)
            span_no_i = sb("span_no_i", [P, SPANS + 1], I32, ph)
            tiles_i = sb("tiles_i", [P, 3, CTX], I32, ph)
            turned_i = tiles_i[:, 0:2, :]
            tiles_f = sums[:, 0:3 * CTX].rearrange("p (j t) -> p j t", j=3)
            both = sums[:, 3 * CTX:3 * CTX + 2 * KW * NG].rearrange("p (u k g) -> p u k g", u=2, g=NG)
            past, prod = both[:, 0, :, :], both[:, 1, :, :]
            scratch = work[:, 2 * D:2 * D + 6 * CTX].rearrange("p (j u t) -> p j u t", j=3, u=2)
            high_i, low_i = scratch[:, 0, :, :].bitcast(I32), scratch[:, 1, :, :].bitcast(I32)
            text_all = scratch[:, 2, :, :]
            meets = sums[:, 0:2 * CTX].rearrange("p (u t) -> p u t", u=2)
            text = sb("text", [P, 2, NBK], F32, ph)
            up = sb("up", [P, CTX], F32, ph)
            down = sb("down", [P, CTX], F32, ph)
            win_lo = sb("win_lo", [P, WC], F32, ph)
            win_hi = sb("win_hi", [P, WC], F32, ph)
            wext = sb("wext", [P, 2, WC], F32, ph)
            wext_all = sb("wext_all", [P, 2, WC * P], F32, ph)
            start_i = sb("start_i", [P, WC * P], I32, ph)
            length = sb("length", [P, WC * P], F32, ph)
            rounds_f = sb("rounds_f", [P, SPANS + 1], F32, ph)
            rounds_i = sb("rounds_i", [P, SPANS + 1], I32, ph)
            in_use = sb("in_use", [P, SPANS + 1], F32, ph)
            top = sb("top", [P, 1], F32, ph)
            trips_f = sb("trips_f", [P, 1], F32, ph)
            trips2_f = sb("trips2_f", [P, 1], F32, ph)
            t_ps = psum("t_ps", [P, 3, CTX], F32, ph)
            tiles_in = sem("tiles_in")
            tiles_set = sem("tiles_set")
            tiles_cast = sem("tiles_cast")
            tiles_turned = sem("tiles_turned")
            packing = sem("packing")
            text_out = sem("text_out")
            text_in = sem("text_in")
            wext_out = sem("wext_out")
            wext_in = sem("wext_in")
            windows = sem("windows")
            packing2 = sem("packing2")
            counting = sem("counting")
            last_past = sb("last_past", [P, KW], F32, ph)
            count_out = sem("count_out")
            raw = sb("raw", [P, 8, D], F32, ph)
            bmsg = sb("bmsg", [NT, D], F32, ph)
            far = sb("far", [P, GROUP], F32, ph)
            ext = sb("ext", [P, 2 * NG], F32, ph)
            ext_all = sb("ext_all", [P, 2 * NG], F32, ph)
            span_f = sb("span_f", [P, NG], F32, ph)
            span_i = sb("span_i", [P, NG], I32, ph)
            win_i = sb("win_i", [P, NG], I32, ph)
            low = sb("low", [P, NG], F32, ph)
            step = sb("step", [P, NG], F32, ph)
            nwin = sb("nwin", [P, NG], F32, ph)
            upto = sb("upto", [P, NG], F32, ph)
            unit = sb("unit", [P, NG], F32, ph)
            k_i = sb("k_i", [P, KW], I32, ph)
            k_f = sb("k_f", [P, KW], F32, ph)
            of_k = sb("of_k", [P, 3, KW], F32, ph)
            first_k = sb("first_k", [P, KW], F32, ph)
            first_ki = sb("first_ki", [P, KW], I32, ph)
            column_ki = sb("column_ki", [P, KW], I32, ph)
            tables_done = sem("tables_done")
            tables_out = sem("tables_out")
            tables_in = sem("tables_in")
            w_ps = psum("w_ps", [P, 8, D], F32, ph)
            iota_done = sem("iota_done")
            zeroed = sem("zeroed")
            select_done = sem("select_done")
            pads_done = sem("pads_done")
            edges_in = sem("edges_in")
            nodes_in = sem("nodes_in")
            weights_in = sem("weights_in")
            small_in = sem("small_in")
            pad_rows_out = sem("pad_rows_out")
            zeros_done = sem("zeros_done")
            prep = sem("prep")
            ext_done = sem("ext_done")
            ext_reduced = sem("ext_reduced")
            w_turned = sem("w_turned")
            w_copied = sem("w_copied")

            full = NG - 1
            rem = E - full * P * GROUP
            rp, rl = rem // GROUP, rem % GROUP
            n_edge_dmas = 3 * ((full > 0) + (rp > 0) + (rl > 0))
            ft, fr = N // NODES, N % NODES
            n_node_dmas = (ft > 0) + (fr > 0)

            with nc.Block() as block:
                @block.sync
                def _(sp):
                    sp.wait_ge(tiles_set, 3)
                    ctf, ctr = CT // P, CT % P
                    n_tile = 0
                    for j, edges in enumerate((src, dst, edge_type)):
                        if ctf:
                            sp.dma_start(tiles_i[:, j, 0:ctf * P].rearrange("p (b e) -> p b e", e=P),
                                         edges[0:ctf * P * P].rearrange("(b p e) -> p b e", p=P, e=P)
                                         ).then_inc(tiles_in, 16)
                            n_tile += 1
                        if ctr:
                            sp.dma_start(tiles_i[0:ctr, j, ctf * P:(ctf + 1) * P],
                                         edges[ctf * P * P:CT * P].rearrange("(p e) -> p e", e=P)
                                         ).then_inc(tiles_in, 16)
                            n_tile += 1
                    sp.wait_ge(pads_done, 4)
                    for tab, edges in ((dst_i, dst), (src_tab, src), (type_i, edge_type)):
                        if full:
                            sp.dma_start(tab[:, 0:full * GROUP].rearrange("p (g j) -> p g j", j=GROUP),
                                         edges[0:full * P * GROUP].rearrange("(g p j) -> p g j", p=P, j=GROUP)
                                         ).then_inc(edges_in, 16)
                        at = full * P * GROUP
                        if rp:
                            sp.dma_start(tab[0:rp, full * GROUP:TILES],
                                         edges[at:at + rp * GROUP].rearrange("(p j) -> p j", j=GROUP)
                                         ).then_inc(edges_in, 16)
                        if rl:
                            sp.dma_start(tab[rp:rp + 1, full * GROUP:full * GROUP + rl],
                                         edges[at + rp * GROUP:E].rearrange("(p j) -> p j", p=1)
                                         ).then_inc(edges_in, 16)
                    if ft:
                        sp.dma_start(nodes[:, 0:ft, :], x[0:ft * NODES, :].rearrange("(t p) f -> p t f", p=NODES)
                                     ).then_inc(nodes_in, 16)
                    if fr:
                        sp.dma_start(nodes[0:fr, ft, :], x[ft * NODES:N, :]).then_inc(nodes_in, 16)
                    sp.wait_ge(tiles_set, 5)
                    with nc.allow_non_contiguous_dma(reason="an extreme per tile or window, once"):
                        for j in range(2):
                            sp.dma_start(tile_ext[j:j + 1, :].rearrange("o (b p) -> p (o b)", p=P),
                                         text[:, j, :]).then_inc(text_out, 16)
                    sp.wait_ge(text_out, 32)
                    for j in range(2):
                        sp.dma_start(text_all[:, j, :], tile_ext[j:j + 1, :].to_broadcast([P, CTX])
                                     ).then_inc(text_in, 16)
                    sp.wait_ge(windows, 2 * WC + 3)
                    with nc.allow_non_contiguous_dma(reason="an extreme per tile or window, once"):
                        for j in range(2):
                            sp.dma_start(win_ext[j:j + 1, :].rearrange("o (c p) -> p (o c)", p=P),
                                         wext[:, j, :]).then_inc(wext_out, 16)
                    sp.wait_ge(wext_out, 32)
                    for j in range(2):
                        sp.dma_start(wext_all[:, j, :], win_ext[j:j + 1, :].to_broadcast([P, WC * P])
                                     ).then_inc(wext_in, 16)
                    sp.wait_ge(windows, 2 * WC + 8)
                    sp.dma_start(start_of, start_i[0:1, :]).then_inc(count_out, 16)
                    sp.dma_start(rounds_of, rounds_i[0:1, :]).then_inc(count_out, 16)
                    sp.wait_ge(count_out, 32)
                    sp.wait_ge(zeros_done, 1)
                    for r in range(NTL * NODES, NPAD, P):
                        m = min(P, NPAD - r)
                        sp.dma_start(rows[r:r + m, :], work[0:m, 0:2 * D]).then_inc(pad_rows_out, 16)
                        sp.dma_start(parts[r:r + m, :], work[0:m, 0:3 * D // 2].bitcast(BF16)
                                     ).then_inc(pad_rows_out, 16)
                    if NPAD > NTL * NODES:
                        sp.wait_ge(pad_rows_out, 32 * (-(-(NPAD - NTL * NODES) // P)))
                    sp.wait_ge(nodes_in, 16 * n_node_dmas)
                    sp.wait_ge(tables_done, 3)
                    for to, table_k in ((first_of, first_ki), (column_of, column_ki), (first_row, first_k)):
                        sp.dma_start(to.rearrange("o (p w) -> (o p) w", w=KW), table_k[:]).then_inc(tables_out, 16)
                    sp.wait_ge(tables_out, 48)
                    sp.dma_start(first_f[:], first_row.to_broadcast([P, P * KW])
                                 ).then_inc(tables_in, 16)
                    sp.wait_ge(tables_in, 16)

                @block.gpsimd
                def _(pool):
                    pool.iota(iota_i[:], pattern=[[1, P]], base=0, channel_multiplier=0).then_inc(iota_done, 1)
                    pool.iota(k_i[:], pattern=[[1, KW]], base=0, channel_multiplier=KW).then_inc(iota_done, 1)
                    pool.iota(codes_i[:], pattern=[[1, max(CTX, CODES)]], base=1, channel_multiplier=0
                              ).then_inc(iota_done, 1)
                    pool.iota(win_no_i[:], pattern=[[WIN * P, WC]], base=0, channel_multiplier=WIN
                              ).then_inc(iota_done, 1)
                    pool.iota(span_no_i[:], pattern=[[WINS, SPANS + 1]], base=0, channel_multiplier=0
                              ).then_inc(iota_done, 1)
                    pool.memset(zero_b[:], 0.0)
                    pool.memset(ident[:], 0.0).then_inc(zeroed, 1)
                    pool.wait_ge(zeroed, 1)
                    pool.affine_select(out=ident[:], in_=ident[:], compare_op=ALU.not_equal, fill=1.0, base=0,
                                       pattern=[[-1, P]], channel_multiplier=1).then_inc(select_done, 1)
                    pool.wait_ge(ext_done, 4)
                    pool.partition_all_reduce(ext_all[:], ext[:], P, RMAX).then_inc(ext_reduced, 1)

                @block.scalar
                def _(act):
                    act.dma_start(raw[:, 0, :], W_msg).then_inc(weights_in, 16)
                    act.dma_start(raw[:, 1, :], fc_weight).then_inc(weights_in, 16)
                    act.dma_start(raw[:, 2:5, :], W_ih.rearrange("(g h) k -> h g k", g=3)).then_inc(weights_in, 16)
                    act.dma_start(raw[:, 5:8, :], W_hh.rearrange("(g h) k -> h g k", g=3)).then_inc(weights_in, 16)
                    with nc.allow_non_contiguous_dma(reason="bias columns, 768 elements"):
                        act.dma_start(bih[:], b_ih.rearrange("(g h) -> h g", g=3)).then_inc(small_in, 16)
                        act.dma_start(bhh[:], b_hh.rearrange("(g h) -> h g", g=3)).then_inc(small_in, 16)
                    act.dma_start(table[:], edge_embed).then_inc(small_in, 16)
                    act.dma_start(bmsg[:], b_msg.rearrange("(o f) -> o f", o=1).to_broadcast([NT, D])
                                  ).then_inc(small_in, 16)
                    act.dma_start(a_all[:], attn.rearrange("a b f -> (a b) f").to_broadcast([P, D])
                                  ).then_inc(small_in, 16)
                    act.dma_start(c_x[:], eps.rearrange("(o f) -> o f", o=1).to_broadcast([NODES, 1])
                                  ).then_inc(small_in, 16)
                    act.wait_ge(w_turned, 8)
                    act.copy(wT[:, 0:4, :], w_ps[:, 0:4, :]).then_inc(w_copied, 1)
                    act.copy(wT[:, 4:8, :], w_ps[:, 4:8, :]).then_inc(w_copied, 1)

                @block.tensor
                def _(pe):
                    pe.wait_ge(weights_in, 64)
                    pe.wait_ge(select_done, 1)
                    for i in range(8):
                        pe.transpose(w_ps[:, i, :], raw[:, i, :], ident[:]).then_inc(w_turned, 1)
                    pe.wait_ge(tiles_cast, 1)
                    for j in range(3):
                        for b in range(NBK):
                            t = pe.transpose(t_ps[:, j, b * P:(b + 1) * P], tiles_f[:, j, b * P:(b + 1) * P],
                                             ident[:])
                        t.then_inc(tiles_turned, 1)

                @block.vector
                def _(dve):
                    last = slice(full * GROUP, TILES)
                    dve.memset(tiles_i[:, 0, :], 0).then_inc(tiles_set, 1)
                    dve.memset(tiles_i[:, 1, :], NOWHERE).then_inc(tiles_set, 1)
                    dve.memset(tiles_i[:, 2, :], 0).then_inc(tiles_set, 1)
                    dve.memset(src_tab[:, last], 0).then_inc(pads_done, 1)
                    dve.memset(dst_i[:, last], -1).then_inc(pads_done, 1)
                    dve.memset(type_i[:, last], 0).then_inc(pads_done, 1)
                    dve.memset(nodes[:, ft:NTL, :], 0.0).then_inc(pads_done, 1)
                    dve.memset(work[:, 0:2 * D], 0.0).then_inc(zeros_done, 1)
                    dve.memset(counts[:], 0.0)
                    dve.memset(ones[:], 1.0)
                    dve.wait_ge(iota_done, 5)
                    dve.tensor_copy(iota_f[:], iota_i[:])
                    dve.tensor_copy(k_f[:], k_i[:])
                    dve.tensor_copy(iota_h[:], iota_i[:])
                    dve.tensor_copy(codes_f[:], codes_i[:, 0:CODES])
                    dve.tensor_copy(up[:], codes_i[:, 0:CTX])
                    dve.tensor_scalar(down[:], codes_i[:, 0:CTX], -1.0, float(CTX + 1), ALU.mult, ALU.add)
                    dve.tensor_copy(win_lo[:], win_no_i[:])
                    dve.tensor_scalar(win_hi[:], win_no_i[:], float(WIN - 1), None, ALU.add)
                    dve.tensor_copy(span_no[:], span_no_i[:])
                    dve.memset(unit[:], 1.0)
                    dve.memset(step[:], 0.0)
                    dve.wait_ge(select_done, 1)
                    dve.tensor_copy(ident_b[:], ident[:])
                    dve.wait_ge(small_in, 96)
                    dve.tensor_tensor(table[:], table[:], bmsg[:], ALU.add)
                    dve.tensor_tensor(brz[:], bih[:, 0:2], bhh[:, 0:2], ALU.add)
                    dve.tensor_scalar(c_x[:], c_x[:], 2.0, None, ALU.add)
                    dve.wait_ge(tiles_in, 16 * 3 * ((CT >= P) + (CT % P > 0)))
                    dve.tensor_copy(tiles_f[:], tiles_i[:]).then_inc(tiles_cast, 1)
                    dve.wait_ge(tiles_cast, 1)
                    by_tile = tiles_f[:, 1, :].rearrange("p (b e) -> p b e", e=P)
                    dve.tensor_reduce(text[:, 0, :], by_tile, AX.X, ALU.min).then_inc(tiles_set, 1)
                    dve.tensor_reduce(text[:, 1, :], by_tile, AX.X, ALU.max).then_inc(tiles_set, 1)
                    dve.wait_ge(edges_in, 16 * n_edge_dmas)
                    dve.tensor_copy(dst_f[:], dst_i[:]).then_inc(prep, 1)
                    dve.tensor_scalar(type_f[:], type_i[:], 0.0, float(NT - 1), ALU.max, ALU.min)
                    dve.wait_ge(prep, 1)
                    dve.tensor_scalar(far[:], dst_f[:, last], 0.0, FAR, ALU.is_lt, ALU.mult).then_inc(prep, 1)
                    dve.tensor_reduce(ext[:, NG:2 * NG], dst_f[:].rearrange("p (g j) -> p g j", j=GROUP),
                                      AX.X, ALU.max).then_inc(ext_done, 1)
                    dve.tensor_reduce(ext[:, 0:NG], dst_f[:].rearrange("p (g j) -> p g j", j=GROUP),
                                      AX.X, ALU.min).then_inc(ext_done, 1)
                    dve.wait_ge(prep, 2)
                    dve.tensor_tensor(far[:], far[:], dst_f[:, last], ALU.add).then_inc(prep, 1)
                    dve.wait_ge(prep, 3)
                    dve.wait_ge(ext_done, 2)
                    dve.tensor_reduce(ext[:, full:full + 1], far[:], AX.X, ALU.min).then_inc(ext_done, 1)
                    dve.wait_ge(ext_done, 3)
                    dve.tensor_scalar(ext[:, 0:NG], ext[:, 0:NG], -1.0, None, ALU.mult).then_inc(ext_done, 1)
                    dve.wait_ge(ext_reduced, 1)
                    dve.tensor_scalar(low[:], ext_all[:, 0:NG], -1.0, None, ALU.mult).then_inc(prep, 1)
                    dve.tensor_tensor(span_f[:], ext_all[:, NG:2 * NG], ext_all[:, 0:NG], ALU.add).then_inc(prep, 1)
                    dve.wait_ge(prep, 5)
                    dve.tensor_copy(span_i[:], span_f[:]).then_inc(prep, 1)
                    dve.wait_ge(prep, 6)
                    dve.tensor_single_scalar(win_i[:], span_i[:], 7, ALU.arith_shift_right).then_inc(prep, 1)
                    dve.wait_ge(prep, 7)
                    dve.tensor_scalar(nwin[:], win_i[:], 1.0, None, ALU.add).then_inc(prep, 1)
                    dve.wait_ge(prep, 8)
                    dve.tensor_tensor_scan(upto[:], unit[:], nwin[:], 0.0, ALU.mult, ALU.add).then_inc(prep, 1)
                    if NG > 1:
                        dve.tensor_tensor(step[:, 0:NG - 1], low[:, 1:NG], low[:, 0:NG - 1], ALU.subtract
                                          ).then_inc(prep, 1)
                    else:
                        dve.sem_inc(prep, 1)
                    dve.wait_ge(prep, 10)
                    dve.tensor_copy(bodies_i[:], upto[:, NG - 1:NG])
                    dve.tensor_copy(skip_i[:], upto[:, GC - 1:GC])
                    dve.tensor_reduce(top[:], ext_all[:, NG:NG + GC], AX.X, ALU.max)
                    wide = [P, KW, NG]
                    dve.tensor_tensor(past[:], k_f[:].unsqueeze(2).to_broadcast(wide),
                                      upto[:].unsqueeze(1).to_broadcast(wide), ALU.is_ge).then_inc(prep, 1)
                    dve.wait_ge(prep, 11)
                    dve.tensor_copy(last_past[:], past[:, :, NG - 1])
                    dve.tensor_reduce(of_k[:, 0, :], past[:], AX.X, ALU.add).then_inc(prep, 1)
                    dve.tensor_tensor(prod[:], past[:], step[:].unsqueeze(1).to_broadcast(wide), ALU.mult
                                      ).then_inc(prep, 1)
                    dve.wait_ge(prep, 13)
                    dve.tensor_tensor(past[:], past[:], nwin[:].unsqueeze(1).to_broadcast(wide), ALU.mult
                                      ).then_inc(prep, 1)
                    dve.tensor_reduce(of_k[:, 1, :], prod[:], AX.X, ALU.add).then_inc(prep, 1)
                    dve.wait_ge(prep, 14)
                    dve.tensor_reduce(of_k[:, 2, :], past[:], AX.X, ALU.add).then_inc(prep, 1)
                    dve.wait_ge(prep, 16)
                    dve.tensor_tensor(of_k[:, 2, :], k_f[:], of_k[:, 2, :], ALU.subtract).then_inc(prep, 1)
                    dve.tensor_scalar(of_k[:, 1, :], of_k[:, 1, :], low[:, 0:1], None, ALU.add).then_inc(prep, 1)
                    dve.wait_ge(prep, 18)
                    dve.scalar_tensor_tensor(out=first_k[:], in0=of_k[:, 2, :], scalar=float(P), in1=of_k[:, 1, :],
                                             op0=ALU.mult, op1=ALU.add).then_inc(prep, 1)
                    dve.tensor_scalar(column_ki[:], of_k[:, 0, :], float(NG - 1), float(GROUP), ALU.min, ALU.mult
                                      ).then_inc(tables_done, 1)
                    dve.wait_ge(prep, 19)
                    dve.tensor_scalar(first_k[:], first_k[:], float(N - 1), None, ALU.min).then_inc(tables_done, 1)
                    dve.wait_ge(tables_done, 2)
                    dve.tensor_copy(first_ki[:], first_k[:]).then_inc(prep, 1)
                    dve.wait_ge(prep, 20)
                    dve.scalar_tensor_tensor(out=first_k[:], in0=last_past[:], scalar=FAR, in1=first_k[:],
                                             op0=ALU.mult, op1=ALU.add).then_inc(tables_done, 1)
                    dve.wait_ge(tiles_turned, 3)
                    dve.tensor_copy(turned_i[:], t_ps[:, 0:2, :]).then_inc(packing, 1)
                    dve.tensor_scalar(packed[:, :, 4], t_ps[:, 2, :], 0.0, float(NT - 1), ALU.max, ALU.min)
                    dve.wait_ge(packing, 1)
                    for j, bits in ((0, 7), (1, 4)):
                        dve.tensor_single_scalar(high_i[:, j, :], turned_i[:, j, :], bits, ALU.arith_shift_right
                                                 ).then_inc(packing, 1)
                        dve.tensor_single_scalar(low_i[:, j, :], turned_i[:, j, :], 2 ** bits - 1, ALU.bitwise_and
                                                 ).then_inc(packing, 1)
                    dve.wait_ge(packing, 5)
                    dve.tensor_scalar(packed[:, :, 2], low_i[:, 1, :], 1.0, None, ALU.add).then_inc(packing, 1)
                    dve.tensor_copy(packed[:, :, 0], high_i[:, 1, :])
                    dve.tensor_copy(packed[:, :, 3], low_i[:, 0, :])
                    dve.wait_ge(packing, 6)
                    dve.scalar_tensor_tensor(out=packed[:, :, 1], in0=high_i[:, 0, :], scalar=float(WIN),
                                             in1=packed[:, :, 2], op0=ALU.mult, op1=ALU.add)
                    dve.wait_ge(text_in, 32)
                    for c in range(WC):
                        if c:
                            dve.wait_ge(windows, 2 * c)
                        dve.tensor_scalar(meets[:, 0, :], text_all[:, 1, :], win_lo[:, c:c + 1], None, ALU.is_ge
                                          ).then_inc(packing, 1)
                        dve.wait_ge(packing, 7 + 2 * c)
                        dve.scalar_tensor_tensor(out=meets[:, 1, :], in0=text_all[:, 0, :],
                                                 scalar=win_hi[:, c:c + 1], in1=meets[:, 0, :],
                                                 op0=ALU.is_le, op1=ALU.mult).then_inc(packing, 1)
                        dve.wait_ge(packing, 8 + 2 * c)
                        dve.tensor_tensor_reduce(meets[:, 0, :], meets[:, 1, :], down[:], 1.0, 0.0,
                                                 ALU.mult, ALU.max, wext[:, 0, c:c + 1]).then_inc(windows, 1)
                        dve.tensor_tensor_reduce(meets[:, 1, :], meets[:, 1, :], up[:], 1.0, 0.0,
                                                 ALU.mult, ALU.max, wext[:, 1, c:c + 1]).then_inc(windows, 1)
                    dve.wait_ge(windows, 2 * WC)
                    dve.tensor_scalar(wext[:, 0, :], wext[:, 0, :], -1.0, float(CTX), ALU.mult, ALU.add
                                      ).then_inc(windows, 1)
                    dve.wait_ge(windows, 2 * WC + 1)
                    dve.tensor_scalar(wext[:, 0, :], wext[:, 0, :], float(CT), None, ALU.min).then_inc(windows, 1)
                    dve.sem_inc(windows, 1)
                    dve.wait_ge(wext_in, 32)
                    dve.tensor_copy(start_i[:], wext_all[:, 0, :]).then_inc(windows, 1)
                    dve.tensor_tensor(length[:], wext_all[:, 1, :], wext_all[:, 0, :], ALU.subtract
                                      ).then_inc(windows, 1)
                    dve.wait_ge(windows, 2 * WC + 5)
                    dve.tensor_reduce(rounds_f[:], length[:, 0:(SPANS + 1) * WINS].rearrange(
                        "p (s i) -> p s i", i=WINS), AX.X, ALU.max).then_inc(windows, 1)
                    dve.wait_ge(windows, 2 * WC + 6)
                    dve.tensor_scalar(rounds_f[:], rounds_f[:], 1.0, float(WT - 1), ALU.max, ALU.add
                                      ).then_inc(counting, 1)
                    dve.wait_ge(counting, 1)
                    dve.tensor_scalar(rounds_i[:], rounds_f[:], float(SIXTH), None, ALU.mult).then_inc(windows, 1)
                    dve.wait_ge(windows, 2 * WC + 7)
                    dve.tensor_single_scalar(rounds_i[:], rounds_i[:], 16, ALU.arith_shift_right
                                             ).then_inc(windows, 1)
                    dve.wait_ge(windows, 2 * WC + 8)
                    dve.tensor_copy(rounds_f[:], rounds_i[:]).then_inc(counting, 1)
                    dve.tensor_scalar(in_use[:], span_no[:], float(WIN), top[:, 0:1], ALU.mult, ALU.is_le
                                      ).then_inc(counting, 1)
                    dve.wait_ge(counting, 3)
                    dve.tensor_tensor(in_use[:], in_use[:], rounds_f[:], ALU.mult).then_inc(counting, 1)
                    dve.tensor_tensor(trips2_f[:], upto[:, NG - 1:NG], upto[:, GC - 1:GC], ALU.subtract
                                      ).then_inc(counting, 1)
                    dve.wait_ge(counting, 5)
                    dve.tensor_reduce(trips_f[:], in_use[:], AX.X, ALU.add).then_inc(counting, 1)
                    dve.wait_ge(counting, 6)
                    dve.tensor_tensor(trips_i[:], trips_f[:], trips2_f[:], ALU.max)
                    dve.memset(sums[:, 0:NPAD], 0.0)

        with layer0 as ph:
            cols_sb = work[:, 0:SPANS * P].rearrange("p (t d) -> p t d", d=P)
            got = sb("got0", [P, NC, CHUNK, D], F32, ph)
            hot = sb("hot0", [P, 2, CHUNK, P], F32, ph)
            hot_b = sb("hot_b", [P, 2, CHUNK, P], BF16, ph)
            kind = sb("kind", [P, 2, CHUNK, NT], BF16, ph)
            stage = sb("stage", [P, 2, HALF * WT, 5], F16, ph)
            win_no = sb("win_no", [P, WINS], F32, ph)
            win_0 = sb("win_0", [P, WINS], F32, ph)
            iota_1 = sb("iota_1", [P, WIN], F32, ph)
            inside = sb("inside", [P, HALF * WT], F32, ph)
            coded = sb("coded", [P, 2, HALF * WT, 2], F32, ph)
            kind_w = sb("kind_w", [P, 2, HALF * WT, NT], BF16, ph)
            hot_w = sb("hot_w", [P, 2, HALF * WT, WIN], BF16, ph)
            left = sb("left", [P, RING, UT, P], BF16, ph)
            right = sb("right", [P, RING, UT, CODES], BF16, ph)
            c_ps = psum("c_ps", [P, 2, 2 * BANK], F32, ph)
            span_ps = psum("span_ps", [P, BANK], F32, ph)
            kinds_ps = psum("kinds_ps", [P, BANK], F32, ph)
            sum_ps = psum("sum_ps", [P, BANK], F32, ph)
            cnt_ps = psum("cnt_ps", [P, BANK], F32, ph)
            idx_in = [sem(f"idx_in0_{c}") for c in range(NC)]
            gathered = [sem(f"gathered0_{c}") for c in range(NC)]
            stage_in = [sem(f"stage_in{h}") for h in range(2)]
            stage_used = sem("stage_used")
            hot_done = sem("hot_done0")
            hot_cast = sem("hot_cast")
            summed = sem("summed0")
            added = sem("added0")
            dl_done = sem("dl_done0")
            inside_done = sem("inside_done")
            coded_done = sem("coded_done")
            made = sem("made")
            counted = sem("counted")
            c_copied = sem("c_copied")
            applied = sem("applied")

            @contextmanager
            def every_trip(eng):
                trips = eng.value_load(trips_i[0:1, 0:1], min_val=1, max_val=MAXT)
                with eng.Fori(0, trips) as k:
                    yield k

            def states(eng, what):
                body, span, turn = (eng.alloc_register(f"{name}_{what}") for name in ("body", "span", "round"))
                eng.reg_mov(body, eng.value_load(skip_i[0:1, 0:1], min_val=1, max_val=MAXB))
                eng.reg_mov(span, 0)
                eng.reg_mov(turn, 0)
                return body, span, turn

            def advance(eng, body, span, turn, tmp):
                rounds = eng.value_load(rounds_of[:, bass.ds(eng.snap(span, min_val=0, max_val=SPANS), 1)],
                                        min_val=1, max_val=MAXR)
                eng.reg_alu(body, body, 1, op=ALU.add)
                eng.reg_alu(body, body, P * KW - 1, op=ALU.min)
                eng.reg_alu(turn, turn, 1, op=ALU.add)
                eng.reg_mov(tmp, rounds)
                eng.reg_alu(tmp, turn, tmp, op=ALU.is_ge)
                eng.reg_alu(span, span, tmp, op=ALU.add)
                eng.reg_alu(span, span, SPANS, op=ALU.min)
                eng.reg_alu(tmp, tmp, 1, op=ALU.bitwise_xor)
                eng.reg_alu(turn, turn, tmp, op=ALU.mult)

            with nc.Block() as block:
                @block.sync
                def _(sp):
                    body, span, turn = states(sp, "sp")
                    tmp, start = sp.alloc_register("tmp_sp"), sp.alloc_register("start_sp")
                    with every_trip(sp) as k:
                        col = column(sp, sp.snap(body, min_val=0, max_val=P * KW - 1))
                        for c in range(NC):
                            for i in (2 * c, 2 * c + 1):
                                at = sp.value_load(start_of[:, bass.ds(
                                    sp.snap(span, min_val=0, max_val=SPANS) * WINS + i, 1)], min_val=0, max_val=CT)
                                sp.reg_alu(tmp, turn, WT, op=ALU.mult)
                                sp.reg_mov(start, at)
                                sp.reg_alu(start, start, tmp, op=ALU.add)
                                sp.reg_alu(start, start, CT, op=ALU.min)
                                j = i % HALF * WT
                                sp.wait_ge(stage_used, 2 * k + i // HALF + 1)
                                sp.dma_start(stage[:, i // HALF, j:j + WT, :],
                                             packed[:, bass.ds(sp.snap(start, min_val=0, max_val=CT), WT), :]
                                             ).then_inc(stage_in[i // HALF], 16)
                            sp.wait_ge(summed, NC * k + c + 1)
                            sp.dma_start(idx[:, c, :], src_tab[:, bass.ds(col + c * CHUNK, CHUNK)]
                                         ).then_inc(idx_in[c], 16)
                        advance(sp, body, span, turn, tmp)

                @block.gpsimd
                def _(pool):
                    with every_trip(pool) as k:
                        for c in range(NC):
                            pool.wait_ge(idx_in[c], 16 * k + 16)
                            pool.sem_inc(chunk_begun, 1)
                            for i in range(CHUNK):
                                pool.indirect_dma_start(
                                    got[:, c, i, :], None, x,
                                    bass.IndirectOffsetOnAxis(ap=idx[:, c, i:i + 1], axis=0)
                                ).then_inc(gathered[c], 16)

                @block.vector
                def _(dve):
                    body, span, turn = states(dve, "dve")
                    tmp = dve.alloc_register("tmp_dve")
                    at_before, span_before = dve.alloc_register("at_before"), dve.alloc_register("span_before")
                    dve.reg_mov(at_before, 0)
                    dve.reg_mov(span_before, 0)
                    dve.tensor_copy(win_0[:], iota_f[:, 0:WINS]).then_inc(dl_done, 1)
                    dve.tensor_scalar(iota_1[:], iota_f[:, 0:WIN], 1.0, None, ALU.add).then_inc(dl_done, 1)
                    dve.wait_ge(dl_done, 2)

                    def add_body(k):
                        at = dve.snap(at_before, min_val=0, max_val=N - 1)
                        at_span = dve.snap(span_before, min_val=0, max_val=SPANS) * P
                        dve.wait_ge(summed, NC * k + NC)
                        dve.wait_ge(applied, k + 1)
                        for j, (to, ps, col) in enumerate(((sums, sum_ps[:, 0:P], at),
                                                           (counts, cnt_ps[0:NT, 0:P], at),
                                                           (sums, span_ps[:, 0:P], at_span),
                                                           (counts, kinds_ps[0:NT, 0:P], at_span))):
                            if j >= 2:
                                dve.wait_ge(added, 4 * k + j - 1)
                            dve.tensor_tensor(to[:, bass.ds(col, P)], to[:, bass.ds(col, P)], ps, ALU.add
                                              ).then_inc(added, 1)

                    dve.sem_inc(stage_used, 2)
                    dve.sem_inc(hot_done, 1)
                    dve.sem_inc(inside_done, 1)
                    dve.sem_inc(coded_done, 1)
                    with every_trip(dve) as k:
                        now = dve.snap(body, min_val=0, max_val=P * KW - 1)
                        col = column(dve, now)
                        dve.wait_ge(hot_done, NC * k + 1)
                        dve.tensor_scalar(dl[:], dst_f[:, bass.ds(col, GROUP)],
                                          first_f[:, bass.ds(now, 1)], None, ALU.subtract).then_inc(dl_done, 1)
                        dve.wait_ge(inside_done, 2 * k + 1)
                        dve.tensor_scalar(win_no[:], win_0[:],
                                          span_no[:, bass.ds(dve.snap(span, min_val=0, max_val=SPANS), 1)],
                                          None, ALU.add).then_inc(dl_done, 1)
                        dve.wait_ge(dl_done, 2 * k + 4)
                        for c in range(NC):
                            n = NC * k + c
                            if c % 2 == 0:
                                h = c // 2
                                st = stage[:, h, :, :]
                                dve.wait_ge(stage_in[h], 16 * HALF * k + 16 * HALF)
                                dve.wait_ge(counted, 2 * (WINS * k + HALF * h + HALF))
                                dve.wait_ge(coded_done, 2 * k + h + 1)
                                dve.tensor_tensor(
                                    inside[:].rearrange("p (i t) -> p i t", t=WT),
                                    st[:, :, 0].rearrange("p (i t) -> p i t", t=WT),
                                    win_no[:, h * HALF:(h + 1) * HALF].unsqueeze(2).to_broadcast([P, HALF, WT]),
                                    ALU.is_equal).then_inc(inside_done, 1)
                                dve.tensor_tensor(
                                    kind_w[:, h, :, :],
                                    st[:, :, 4:5].to_broadcast([P, HALF * WT, NT]),
                                    iota_f[:, 0:NT].unsqueeze(1).to_broadcast([P, HALF * WT, NT]), ALU.is_equal)
                                dve.wait_ge(inside_done, 2 * k + h + 2)
                                dve.tensor_tensor(
                                    coded[:, h, :, :], st[:, :, 1:3],
                                    inside[:].unsqueeze(2).to_broadcast([P, HALF * WT, 2]), ALU.mult
                                ).then_inc(coded_done, 1)
                            dve.wait_ge(summed, n + NC - 1)
                            dve.tensor_tensor(
                                kind[:, c % 2, :, :],
                                type_f[:, bass.ds(col + c * CHUNK, CHUNK)].unsqueeze(2)
                                .to_broadcast([P, CHUNK, NT]),
                                iota_f[:, 0:NT].unsqueeze(1).to_broadcast([P, CHUNK, NT]), ALU.is_equal)
                            dve.tensor_tensor(
                                hot[:, c % 2, :, :],
                                iota_f[:].unsqueeze(1).to_broadcast([P, CHUNK, P]),
                                dl[:, c * CHUNK:(c + 1) * CHUNK].unsqueeze(2).to_broadcast([P, CHUNK, P]),
                                ALU.is_equal).then_inc(hot_done, 1)
                            for u in range(4 * c, 4 * c + 4):
                                i, m = u // 2, 2 * WINS * k + u
                                dve.wait_ge(counted, m + 2 * WINS - RING + 1)
                                j = i % HALF * WT + u % 2 * UT
                                dve.tensor_tensor(
                                    left[:, u % RING, :, :],
                                    iota_h[:].unsqueeze(1).to_broadcast([P, UT, P]),
                                    st[:, j:j + UT, 3:4].to_broadcast([P, UT, P]), ALU.is_equal)
                                if u % (2 * HALF) == 0:
                                    dve.wait_ge(coded_done, 2 * k + h + 2)
                                    dve.tensor_tensor(
                                        hot_w[:, h, :, :],
                                        coded[:, h, :, 1:2].to_broadcast([P, HALF * WT, WIN]),
                                        iota_1[:, 0:WIN].unsqueeze(1).to_broadcast([P, HALF * WT, WIN]),
                                        ALU.is_equal)
                                for t in range(UT):
                                    mm = dve.tensor_scalar(right[:, u % RING, t, :], codes_f[:],
                                                           coded[:, h, j + t, 0:1], None, ALU.is_equal)
                                mm.then_inc(made, 1)
                                if u % (2 * HALF) == 2 * HALF - 1:
                                    dve.wait_ge(made, m + 1)
                                    dve.sem_inc(stage_used, 1)
                            if c == 0:
                                add_body(k)
                                dve.reg_mov(at_before, node_of(dve, now))
                                dve.reg_mov(span_before, span)
                        advance(dve, body, span, turn, tmp)
                    add_body(dve.value_load(trips_i[0:1, 0:1], min_val=1, max_val=MAXT))

                @block.scalar
                def _(act):
                    act.sem_inc(c_copied, 2)
                    with every_trip(act) as k:
                        for c in range(NC):
                            act.wait_ge(hot_done, NC * k + c + 2)
                            act.copy(hot_b[:, c % 2, :, :], hot[:, c % 2, :, :]).then_inc(hot_cast, 1)
                            for i in (2 * c, 2 * c + 1):
                                m = WINS * k + i
                                act.wait_ge(counted, 2 * (m + WINS + 1))
                                if i == 0:
                                    act.wait_ge(applied, k + 1)
                                act.copy(cols_sb[:, :, i * WIN:(i + 1) * WIN],
                                         c_ps[:, i % 2, 0:CODES].rearrange("p (t d) -> p t d", d=WIN)
                                         ).then_inc(c_copied, 1)

                @block.tensor
                def _(pe):
                    for ps in (sum_ps[:, 0:P], cnt_ps[0:NT, 0:P], span_ps[:, 0:P], kinds_ps[0:NT, 0:P]):
                        mm = pe.matmul(ps, zero_b[:, 0:ps.shape[0]], zero_b[:], start=True, stop=True)
                    mm.then_inc(applied, 1)
                    pe.sem_inc(summed, NC)
                    pe.sem_inc(counted, 2 * WINS)
                    with every_trip(pe) as k:
                        for c in range(NC):
                            for i in (2 * c, 2 * c + 1):
                                m, h = WINS * k + i, i // HALF
                                pe.wait_ge(c_copied, m + 1)
                                if i == 0:
                                    pe.wait_ge(added, 4 * k + 4)
                                for t in range(WT):
                                    j, ends = i % HALF * WT + t, dict(start=(t == 0), stop=(t == WT - 1))
                                    u, v = (2 * i + t // UT) % RING, t % UT
                                    if v == 0:
                                        pe.wait_ge(made, 2 * m + t // UT + 1)
                                    for lo in range(0, CODES, BANK):
                                        hi = min(CODES, lo + BANK)
                                        pe.matmul(c_ps[:, i % 2, lo:hi], left[:, u, v, :],
                                                  right[:, u, v, lo:hi], **ends)
                                    mm = pe.matmul(kinds_ps[0:NT, i * WIN:(i + 1) * WIN], kind_w[:, h, j, :],
                                                   hot_w[:, h, j, :], **ends)
                                    if v == UT - 1:
                                        mm.then_inc(counted, 1)
                            pe.wait_ge(gathered[c], 16 * CHUNK * k + 16 * CHUNK)
                            pe.wait_ge(hot_cast, NC * k + c + 1)
                            for i in range(CHUNK):
                                n = c * CHUNK + i
                                pe.matmul(cnt_ps[0:NT, 0:P], kind[:, c % 2, i, :], hot_b[:, c % 2, i, :],
                                          start=(n == 0), stop=(n == GROUP - 1))
                                mm = pe.matmul(sum_ps[:, 0:P], got[:, c, i, :], hot[:, c % 2, i, :],
                                               start=(n == 0), stop=(n == GROUP - 1))
                            mm.then_inc(summed, 1)
                        pe.wait_ge(c_copied, WINS * k + WINS + 2)
                        for t in range(SPANS):
                            mm = pe.matmul(span_ps[:, 0:P], nodes[:, t, :], cols_sb[:, t, :],
                                           start=(t == 0), stop=(t == SPANS - 1))
                        mm.then_inc(applied, 1)

        with ExitStack() as ph:
            msg = sb("msg", [P, QN], F32, ph)
            r_s = sb("r_s", [P, QN], F32, ph)
            z_s = sb("z_s", [P, QN], F32, ph)
            n_s = sb("n_s", [P, QN], F32, ph)
            t_s = sb("t_s", [P, QN], F32, ph)
            d_s = sb("d_s", [P, QN], F32, ph)
            msg_ps = psum("msg_ps", [P, 512], F32, ph)
            r_ps = psum("r_ps", [P, 512], F32, ph)
            z_ps = psum("z_ps", [P, 512], F32, ph)
            i_ps = psum("i_ps", [P, 512], F32, ph)
            h_ps = psum("h_ps", [P, 512], F32, ph)
            xt_ps = psum("xt_ps", [P, 2, 512], F32, ph)
            xt_done = sem("xt_done")
            xt_copied = sem("xt_copied")
            msg_done = sem("msg_done")
            msg_copied = sem("msg_copied")
            gates = sem("gates")
            r_done = sem("r_done")
            z_done = sem("z_done")
            pre_done = sem("pre_done")
            n_done = sem("n_done")
            y_done = sem("y_done")

            with nc.Block() as block:
                @block.tensor
                def _(pe):
                    for q in range(NQ):
                        pe.wait_ge(xt_copied, q + 1)
                        for i in range(QUAD):
                            t = pe.transpose(xt_ps[:, q % 2, i * NODES:(i + 1) * NODES],
                                             nodes[:, q * QUAD + i, :], ident[:])
                        t.then_inc(xt_done, 1)
                    pe.wait_ge(xt_copied, NQ + 2)
                    pe.sem_inc(gates, 3)
                    with pe.Fori(0, NQ) as q:
                        cols = bass.ds(q * QN, QN)
                        pe.wait_ge(msg_copied, q + 1)
                        pe.matmul(msg_ps[:, 0:QN], wT[:, 0, :], sums[:, cols], start=True, stop=False)
                        pe.matmul(msg_ps[:, 0:QN], table[:], counts[:, cols], start=False, stop=True
                                  ).then_inc(msg_done, 1)
                        pe.wait_ge(z_done, q + 1)
                        pe.wait_ge(pre_done, 2 * q + 2)
                        pe.matmul(r_ps[:, 0:QN], wT[:, 5, :], work[:, cols], start=True, stop=False)
                        pe.matmul(z_ps[:, 0:QN], wT[:, 6, :], work[:, cols], start=True, stop=False)
                        pe.matmul(h_ps[:, 0:QN], wT[:, 7, :], work[:, cols], start=True, stop=True)
                        pe.wait_ge(msg_copied, q + 2)
                        pe.matmul(r_ps[:, 0:QN], wT[:, 2, :], msg[:], start=False, stop=True).then_inc(gates, 1)
                        pe.matmul(i_ps[:, 0:QN], wT[:, 4, :], msg[:], start=True, stop=True).then_inc(gates, 1)
                        pe.matmul(z_ps[:, 0:QN], wT[:, 3, :], msg[:], start=False, stop=True).then_inc(gates, 1)

                @block.scalar
                def _(act):
                    act.sem_inc(xt_copied, 2)
                    for q in range(NQ):
                        act.wait_ge(xt_done, q + 1)
                        act.copy(work[:, q * QN:(q + 1) * QN], xt_ps[:, q % 2, 0:QN]).then_inc(xt_copied, 1)
                    act.sem_inc(msg_copied, 1)
                    act.sem_inc(z_done, 1)
                    with act.Fori(0, NQ) as q:
                        act.wait_ge(msg_done, q + 1)
                        act.wait_ge(gates, 3 * q + 3)
                        act.copy(msg[:], msg_ps[:, 0:QN]).then_inc(msg_copied, 1)
                        act.wait_ge(gates, 3 * q + 4)
                        act.activation(r_s[:], r_ps[:, 0:QN], ACT.Sigmoid, bias=brz[:, 0:1]).then_inc(r_done, 1)
                        act.wait_ge(gates, 3 * q + 6)
                        act.wait_ge(y_done, 4 * q + 4)
                        act.activation(z_s[:], z_ps[:, 0:QN], ACT.Sigmoid, bias=brz[:, 1:2]).then_inc(z_done, 1)
                        act.wait_ge(pre_done, 2 * q + 4)
                        act.activation(n_s[:], t_s[:], ACT.Tanh, bias=bih[:, 2:3]).then_inc(n_done, 1)

                @block.vector
                def _(dve):
                    dve.sem_inc(pre_done, 2)
                    dve.sem_inc(y_done, 4)
                    with dve.Fori(0, NQ) as q:
                        cols = bass.ds(q * QN, QN)
                        dve.wait_ge(r_done, q + 1)
                        dve.wait_ge(gates, 3 * q + 5)
                        dve.scalar_tensor_tensor(out=t_s[:], in0=h_ps[:, 0:QN], scalar=bhh[:, 2:3], in1=r_s[:],
                                                 op0=ALU.add, op1=ALU.mult).then_inc(pre_done, 1)
                        dve.wait_ge(pre_done, 2 * q + 3)
                        dve.tensor_tensor(t_s[:], t_s[:], i_ps[:, 0:QN], ALU.add).then_inc(pre_done, 1)
                        dve.wait_ge(n_done, q + 1)
                        dve.wait_ge(z_done, q + 2)
                        dve.tensor_tensor(d_s[:], work[:, cols], n_s[:], ALU.subtract).then_inc(y_done, 1)
                        dve.wait_ge(y_done, 4 * q + 5)
                        dve.tensor_tensor(d_s[:], d_s[:], z_s[:], ALU.mult).then_inc(y_done, 1)
                        dve.wait_ge(y_done, 4 * q + 6)
                        dve.tensor_tensor(d_s[:], d_s[:], n_s[:], ALU.add).then_inc(y_done, 1)
                        dve.wait_ge(y_done, 4 * q + 7)
                        dve.tensor_tensor(work[:, cols], work[:, cols], d_s[:], ALU.add).then_inc(y_done, 1)

        with ExitStack() as ph:
            y_ps = psum("y_ps", [NODES, QUAD, D], F32, ph)
            deg_ps = psum("deg_ps", [NODES, 512], F32, ph)
            y_turned = sem("y_turned")
            y_copied = sem("y_copied")
            stats_done = sem("stats_done")
            aggr_done = sem("aggr_done")
            spread = sem("spread0")

            with nc.Block() as block:
                @block.tensor
                def _(pe):
                    for q in range(NQ):
                        pe.wait_ge(y_copied, q + 1)
                        for i in range(QUAD):
                            tile = q * QUAD + i
                            pe.matmul(deg_ps[:, tile:tile + 1], counts[:, tile * NODES:(tile + 1) * NODES],
                                      ones[:], start=True, stop=True)
                            t = pe.transpose(y_ps[:, i, :], work[:, tile * NODES:(tile + 1) * NODES], ident[:])
                        t.then_inc(y_turned, 1)

                @block.scalar
                def _(act):
                    act.sem_inc(y_copied, 1)
                    with act.Fori(0, NQ) as q:
                        act.wait_ge(y_turned, q + 1)
                        act.copy(nodes[:, bass.ds(q * QUAD, QUAD), :], y_ps[:]).then_inc(y_copied, 1)
                    act.wait_ge(spread, 1)
                    act.activation(rstd[:], rstd[:], ACT.Sqrt).then_inc(spread, 1)

                @block.vector
                def _(dve):
                    for q in range(NQ):
                        dve.wait_ge(y_copied, q + 2)
                        if q:
                            dve.wait_ge(aggr_done, QUAD * q)
                        for i in range(QUAD):
                            dve.bn_stats(stats[:, i, :], nodes[:, q * QUAD + i, :]).then_inc(stats_done, 1)
                        for i in range(QUAD):
                            dve.wait_ge(stats_done, QUAD * q + i + 1)
                            dve.bn_aggr(moments[:, q * QUAD + i, :], stats[:, i, :]).then_inc(aggr_done, 1)
                    dve.wait_ge(aggr_done, NTL)
                    dve.tensor_scalar(rstd[:], moments[:, :, 1], LN_EPS, None, ALU.add).then_inc(spread, 1)
                    dve.tensor_scalar(rdeg[:], deg_ps[:, 0:NTL], 1.0, None, ALU.max).then_inc(stats_done, 1)
                    dve.wait_ge(stats_done, NTL + 1)
                    dve.reciprocal(rdeg[:], rdeg[:])
                    dve.wait_ge(spread, 2)
                    dve.reciprocal(rstd[:], rstd[:])

        def each_quad(eng, quad):
            if NQ > 1:
                with eng.Fori(0, NQ // 2) as h:
                    for b in range(2):
                        quad(h, b)
            if NQ % 2:
                quad(NQ // 2, 0)

        proj = work[0:NODES, 0:NTL * D].rearrange("p (t f) -> p t f", f=D)
        with ExitStack() as ph:
            f_s = sb("f_s", [P, 2, QN], F32, ph)
            rest = sb("rest", [NODES, 2, QUAD, D], F32, ph)
            split = sb("split", [NODES, 2, QUAD, 3, D], BF16, ph)
            f_ps = psum("f_ps", [P, 2, 512], F32, ph)
            p_ps = psum("p_ps", [NODES, 2, QUAD, D], F32, ph)
            normed = sem("normed")
            f_turned = sem("f_turned")
            f_copied = sem("f_copied")
            p_done = sem("p_done")
            p_copied = sem("p_copied")
            cut = sem("cut")
            feat_out = sem("feat_out")
            proj_out = sem("proj_out")
            parts_out = [sem(f"parts_out{b}") for b in range(2)]
            rows_q = rows[0:NTL * NODES, :].rearrange("(t p) f -> p t f", p=NODES)
            parts_q = parts[0:NTL * NODES, :].rearrange("(t p) (s f) -> p t s f", p=NODES, s=3)

            with nc.Block() as block:
                @block.vector
                def _(dve):
                    with dve.Fori(0, NQ) as q:
                        for i in range(QUAD):
                            t = bass.ds(q * QUAD + i, 1)
                            dve.tensor_scalar(nodes[:, t, :].squeeze(1), nodes[:, t, :].squeeze(1),
                                              moments[:, t, 0], rstd[:, t], ALU.subtract, ALU.mult
                                              ).then_inc(normed, 1)
                    def cut_quad(h, b):
                            q = h * 2 + b
                            pr = proj[:, bass.ds(q * QUAD, QUAD), :]
                            dve.wait_ge(p_copied, q + 3)
                            dve.wait_ge(parts_out[b], 16 * h + 16)
                            dve.tensor_copy(split[:, b, :, 0, :], pr).then_inc(cut, 1)
                            dve.wait_ge(cut, 4 * q + 1)
                            dve.tensor_tensor(rest[:, b, :, :], pr, split[:, b, :, 0, :], ALU.subtract
                                              ).then_inc(cut, 1)
                            dve.wait_ge(cut, 4 * q + 2)
                            dve.tensor_copy(split[:, b, :, 1, :], rest[:, b, :, :]).then_inc(cut, 1)
                            dve.wait_ge(cut, 4 * q + 3)
                            dve.tensor_tensor(split[:, b, :, 2, :], rest[:, b, :, :], split[:, b, :, 1, :],
                                              ALU.subtract).then_inc(cut, 1)

                    each_quad(dve, cut_quad)

                @block.tensor
                def _(pe):
                    pe.sem_inc(p_done, 2)
                    for q in range(NQ):
                            b = q % 2
                            pe.wait_ge(normed, QUAD * q + QUAD)
                            pe.wait_ge(f_copied, q + 1)
                            for i in range(QUAD):
                                t = pe.transpose(f_ps[:, b, i * NODES:(i + 1) * NODES],
                                                 nodes[:, q * QUAD + i, :],
                                                 ident[0:NODES, 0:NODES])
                            t.then_inc(f_turned, 1)
                            pe.wait_ge(f_copied, q + 3)
                            pe.wait_ge(p_copied, q + 1)
                            for i in range(QUAD):
                                mm = pe.matmul(p_ps[:, b, i, :], f_s[:, b, i * NODES:(i + 1) * NODES], wT[:, 1, :],
                                               start=True, stop=True)
                            mm.then_inc(p_done, 1)

                @block.scalar
                def _(act):
                    act.sem_inc(f_copied, 2)
                    act.sem_inc(p_copied, 2)
                    def copy_quad(h, b):
                            q = h * 2 + b
                            act.wait_ge(f_turned, q + 1)
                            act.wait_ge(p_done, q + 1)
                            act.copy(f_s[:, b, :], f_ps[:, b, 0:QN]).then_inc(f_copied, 1)
                            act.wait_ge(p_done, q + 3)
                            act.copy(proj[:, bass.ds(q * QUAD, QUAD), :], p_ps[:, b, :, :]).then_inc(p_copied, 1)

                    each_quad(act, copy_quad)

                @block.sync
                def _(sp):
                    for b in range(2):
                        sp.sem_inc(parts_out[b], 16)
                    def store_quad(h, b):
                            q = h * 2 + b
                            t = bass.ds(q * QUAD, QUAD)
                            sp.wait_ge(normed, QUAD * q + QUAD)
                            sp.dma_start(rows_q[:, t, D:2 * D], nodes[:, t, :]).then_inc(feat_out, 16)
                            sp.wait_ge(p_copied, q + 3)
                            sp.dma_start(rows_q[:, t, 0:D], proj[:, t, :]).then_inc(proj_out, 16)
                            sp.wait_ge(cut, 4 * q + 4)
                            sp.dma_start(parts_q[:, t, :, :], split[:, b, :, :, :]).then_inc(parts_out[b], 16)

                    each_quad(sp, store_quad)
                    sp.wait_ge(feat_out, 16 * NQ)
                    sp.wait_ge(proj_out, 16 * NQ)
                    for b in range(2):
                        sp.wait_ge(parts_out[b], 16 * ((NQ + 1 - b) // 2) + 16)

        with ExitStack() as ph:
            got = sb("got1", [P, NC, CHUNK, 2 * D], F32, ph)
            hot = sb("hot1", [P, NC, CHUNK, P], BF16, ph)
            hot_t = sb("hot_t", [P, 2, CHUNK, P], BF16, ph)
            whot = sb("whot", [P, 2, CHUNK, P], F32, ph)
            win_in = sb("win_in", [P, 3, D], BF16, ph)
            win = sb("win", [P, 3, D], BF16, ph)
            s_s = sb("s_s", [P, CHUNK, D], F32, ph)
            l_s = sb("l_s", [P, CHUNK, D], F32, ph)
            pr_s = sb("pr_s", [P, CHUNK, D], F32, ph)
            q_s = sb("q_s", [P, NC, CHUNK], F32, ph)
            e_s = sb("e_s", [P, NC, CHUNK], F32, ph)
            gate_s = sb("gate_s", [P, NC, CHUNK], F32, ph)
            eg_s = sb("eg_s", [P, NC, CHUNK], F32, ph)
            w_s = sb("w_s", [P, NC, CHUNK], F32, ph)
            hot_ps = psum("hot_ps", [P, 2, 1024], BF16, ph)
            er_ps = psum("er_ps", [P, 2, 1024], F32, ph)
            sum_ps = psum("sum_ps1", [P, 512], F32, ph)
            idx_in = [sem(f"idx_in1_{c}") for c in range(NC)]
            gathered = [sem(f"gathered1_{c}") for c in range(NC)]
            win_loaded = sem("win_loaded")
            win_copied = sem("win_copied")
            dl_done = sem("dl_done1")
            hot_done = sem("hot_done1")
            turned = sem("turned")
            hot_copied = sem("hot_copied")
            er_done = sem("er_done")
            s_done = sem("s_done")
            q_done = sem("q_done")
            l_done = sem("l_done")
            e_done = sem("e_done")
            gate_done = sem("gate_done")
            eg_done = sem("eg_done")
            w_done = sem("w_done")
            whot_done = sem("whot_done")
            summed = sem("summed1")
            zeros_set = sem("zeros_set")
            added = sem("added1")

            with nc.Block() as block:
                @block.sync
                def _(sp):
                    sp.dma_start(win_in[:].rearrange("p s f -> p (s f)"), parts[bass.ds(node_of(sp, 0), P), :]
                                 ).then_inc(win_loaded, 16)
                    with every_body(sp) as k:
                        col, at = column(sp, k), node_of(sp, k + 1)
                        for c in range(NC):
                            sp.wait_ge(summed, NC * k + c + 1)
                            sp.dma_start(idx[:, c, :], src_tab[:, bass.ds(col + c * CHUNK, CHUNK)]
                                         ).then_inc(idx_in[c], 16)
                        sp.wait_ge(win_copied, k + 1)
                        sp.dma_start(win_in[:].rearrange("p s f -> p (s f)"), parts[bass.ds(at, P), :]
                                     ).then_inc(win_loaded, 16)

                @block.gpsimd
                def _(pool):
                    with every_body(pool) as k:
                        for c in range(NC):
                            pool.wait_ge(idx_in[c], 16 * k + 16)
                            pool.sem_inc(chunk_begun, 1)
                            for i in range(CHUNK):
                                pool.indirect_dma_start(
                                    got[:, c, i, :], None, rows,
                                    bass.IndirectOffsetOnAxis(ap=idx[:, c, i:i + 1], axis=0)
                                ).then_inc(gathered[c], 16)

                @block.vector
                def _(dve):
                    def relative(k, col):
                        dve.tensor_scalar(dl[:], dst_f[:, bass.ds(col, GROUP)],
                                          first_f[:, bass.ds(k, 1)], None, ALU.subtract).then_inc(dl_done, 1)

                    def one_hot(c, k):
                        dve.wait_ge(whot_done, NC * k + c + 1)
                        dve.tensor_tensor(
                            hot[:, c, :, :],
                            iota_f[:].unsqueeze(1).to_broadcast([P, CHUNK, P]),
                            dl[:, c * CHUNK:(c + 1) * CHUNK].unsqueeze(2).to_broadcast([P, CHUNK, P]),
                            ALU.is_equal).then_inc(hot_done, 1)

                    def add_body(at, k):
                        dve.wait_ge(summed, NC * k + NC)
                        dve.tensor_tensor(sums[:, bass.ds(at, P)], sums[:, bass.ds(at, P)],
                                          sum_ps[:, 0:P], ALU.add).then_inc(added, 1)

                    dve.memset(got[:, NC - 1, :, D:2 * D], 0.0).then_inc(zeros_set, 1)
                    dve.memset(whot[:, 1, :, :], 0.0).then_inc(zeros_set, 1)
                    dve.memset(sums[:, 0:NPAD], 0.0).then_inc(zeros_set, 1)
                    relative(0, column(dve, 0))
                    dve.wait_ge(dl_done, 1)
                    one_hot(0, 0)
                    one_hot(1, 0)
                    dve.wait_ge(zeros_set, 3)
                    dve.sem_inc(q_done, 2)
                    before = dve.alloc_register("before")
                    dve.reg_mov(before, 0)
                    with every_body(dve) as k:
                        for c in range(NC):
                            n = NC * k + c
                            el = got[:, c, :, 0:D]
                            er = er_ps[:, c % 2, 0:CHUNK * D].rearrange("p (i f) -> p i f", f=D)
                            dve.wait_ge(gathered[c], 16 * CHUNK * k + 16 * CHUNK)
                            dve.wait_ge(er_done, n + NC + 1)
                            dve.tensor_tensor(s_s[:], el, er, ALU.add).then_inc(s_done, 1)
                            for i in range(CHUNK):
                                mm = dve.tensor_tensor_reduce(pr_s[:, i, :], el[:, i, :], er[:, i, :], 1.0, 0.0,
                                                              ALU.mult, ALU.add, q_s[:, c, i:i + 1])
                            mm.then_inc(q_done, 1)
                            dve.wait_ge(s_done, n + 1)
                            dve.scalar_tensor_tensor(out=l_s[:], in0=s_s[:], scalar=LEAK, in1=s_s[:],
                                                     op0=ALU.mult, op1=ALU.max).then_inc(l_done, 1)
                            if c == NC - 2:
                                col = column(dve, k + 1)
                                dve.wait_ge(hot_done, NC * k + NC)
                                relative(k + 1, col)
                                dve.wait_ge(dl_done, k + 2)
                            one_hot((c + 2) % NC, k + (c + 2) // NC)
                            dve.wait_ge(l_done, n + 1)
                            for i in range(CHUNK):
                                mm = dve.tensor_tensor_reduce(l_s[:, i, :], l_s[:, i, :], a_all[:], 1.0, 0.0,
                                                              ALU.mult, ALU.add, e_s[:, c, i:i + 1])
                            mm.then_inc(e_done, 1)
                            if c == 0:
                                add_body(dve.snap(before, min_val=0, max_val=N - 1), k)
                                dve.reg_mov(before, node_of(dve, k))
                            dve.wait_ge(gate_done, n + 1)
                            dve.wait_ge(e_done, n + 1)
                            dve.tensor_tensor(eg_s[:, c, :], e_s[:, c, :], gate_s[:, c, :], ALU.mult
                                              ).then_inc(eg_done, 1)
                    add_body(dve.snap(before, min_val=0, max_val=N - 1),
                             dve.value_load(bodies_i[0:1, 0:1], min_val=1, max_val=MAXB))

                @block.scalar
                def _(act):
                    def copy_hot(c, k):
                        n = NC * k + c
                        act.wait_ge(turned, n + 1)
                        act.wait_ge(er_done, n + NC - 1)
                        act.copy(hot_t[:, c % 2, :, :],
                                 hot_ps[:, c % 2, 0:CHUNK * P].rearrange("p (i e) -> p i e", e=P)
                                 ).then_inc(hot_copied, 1)

                    def copy_window(k):
                        act.wait_ge(win_loaded, 16 * k + 16)
                        act.wait_ge(er_done, NC * k + NC)
                        act.copy(win[:], win_in[:]).then_inc(win_copied, 1)

                    act.sem_inc(hot_copied, 2)
                    act.sem_inc(whot_done, NC)
                    copy_window(0)
                    copy_hot(0, 0)
                    with every_body(act) as k:
                        for c in range(NC):
                            n = NC * k + c
                            copy_hot((c + 1) % NC, k + (c + 1) // NC)
                            if c == NC - 1:
                                copy_window(k + 1)
                            act.wait_ge(q_done, n + 3)
                            act.activation(gate_s[:, c, :], q_s[:, c, :], ACT.Sigmoid).then_inc(gate_done, 1)
                            act.wait_ge(eg_done, n + 1)
                            act.activation(w_s[:, c, :], eg_s[:, c, :], ACT.Sigmoid).then_inc(w_done, 1)
                            act.wait_ge(w_done, n + 1)
                            act.wait_ge(summed, n + NC - 1)
                            for i in range(CHUNK):
                                m = act.activation(whot[:, c % 2, i, :], hot[:, c, i, :], ACT.Copy,
                                                   scale=w_s[:, c, i:i + 1])
                            m.then_inc(whot_done, 1)

                @block.tensor
                def _(pe):
                    def turn(c, k):
                        n = NC * k + c
                        pe.wait_ge(hot_done, n + 1)
                        pe.wait_ge(hot_copied, n + 1)
                        for i in range(CHUNK):
                            t = pe.transpose(hot_ps[:, c % 2, i * P:(i + 1) * P], hot[:, c, i, :], ident_b[:])
                        t.then_inc(turned, 1)

                    def sum_rows(c):
                        for i in range(CHUNK):
                            mm = pe.matmul(sum_ps[:, 0:P], got[:, c, i, D:2 * D], whot[:, c % 2, i, :],
                                           start=(c == 0 and i == 0), stop=(c == NC - 1 and i == CHUNK - 1))
                        mm.then_inc(summed, 1)

                    pe.sem_inc(er_done, NC)
                    pe.sem_inc(summed, NC - 1)
                    turn(0, 0)
                    pe.wait_ge(zeros_set, 3)
                    pe.matmul(sum_ps[:, 0:P], got[:, NC - 1, 0, D:2 * D], whot[:, 1, 0, :], start=True, stop=False)
                    with every_body(pe) as k:
                        for c in range(NC):
                            n = NC * k + c
                            turn((c + 1) % NC, k + (c + 1) // NC)
                            if c == 0:
                                pe.wait_ge(win_copied, k + 1)
                            pe.wait_ge(hot_copied, n + 3)
                            pe.wait_ge(q_done, n + 1)
                            for i in range(CHUNK):
                                for part in range(3):
                                    mm = pe.matmul(er_ps[:, c % 2, i * D:(i + 1) * D], hot_t[:, c % 2, i, :],
                                                   win[:, part, :], start=(part == 0), stop=(part == 2))
                            mm.then_inc(er_done, 1)
                            if c == 1:
                                pe.wait_ge(added, k + 1)
                            pe.wait_ge(whot_done, n + NC)
                            sum_rows((c - 1) % NC)
                    bodies = pe.value_load(bodies_i[0:1, 0:1], min_val=1, max_val=MAXB)
                    pe.wait_ge(whot_done, bodies * NC + NC)
                    sum_rows(NC - 1)

        with ExitStack() as ph:
            mean_s = sb("mean_s", [NODES, QUAD, D], F32, ph)
            m_ps = psum("m_ps", [NODES, QUAD, D], F32, ph)
            m_turned = sem("m_turned")
            steps = sem("steps")
            spread = sem("spread1")
            finished = sem("finished")
            stored = sem("stored")
            S = 2 + 2 * QUAD

            with nc.Block() as block:
                @block.tensor
                def _(pe):
                    for q in range(NQ):
                        pe.wait_ge(steps, S * q + 1)
                        for i in range(QUAD):
                            tile = q * QUAD + i
                            t = pe.transpose(m_ps[:, i, :], sums[:, tile * NODES:(tile + 1) * NODES], ident[:])
                        t.then_inc(m_turned, 1)

                @block.scalar
                def _(act):
                    act.wait_ge(spread, 1)
                    act.activation(rstd[:], rstd[:], ACT.Sqrt).then_inc(spread, 1)

                @block.vector
                def _(dve):
                    dve.sem_inc(steps, 1)
                    for q in range(NQ):
                        t = slice(q * QUAD, (q + 1) * QUAD)
                        dve.wait_ge(m_turned, q + 1)
                        dve.wait_ge(steps, S * q + 1)
                        dve.tensor_tensor(mean_s[:], m_ps[:],
                                          rdeg[:, t].unsqueeze(2).to_broadcast([NODES, QUAD, D]), ALU.mult
                                          ).then_inc(steps, 1)
                        dve.wait_ge(steps, S * q + 2)
                        dve.scalar_tensor_tensor(out=nodes[:, t, :], in0=nodes[:, t, :], scalar=c_x[:],
                                                 in1=mean_s[:], op0=ALU.mult, op1=ALU.add).then_inc(steps, 1)
                        dve.wait_ge(steps, S * q + 3)
                        for i in range(QUAD):
                            dve.bn_stats(stats[:, i, :], nodes[:, q * QUAD + i, :]).then_inc(steps, 1)
                        for i in range(QUAD):
                            dve.wait_ge(steps, S * q + 4 + i)
                            dve.bn_aggr(moments[:, q * QUAD + i, :], stats[:, i, :]).then_inc(steps, 1)
                    dve.wait_ge(steps, S * NQ + 1)
                    dve.tensor_scalar(rstd[:], moments[:, :, 1], LN_EPS, None, ALU.add).then_inc(spread, 1)
                    dve.wait_ge(spread, 2)
                    dve.reciprocal(rstd[:], rstd[:]).then_inc(spread, 1)
                    dve.wait_ge(spread, 3)
                    with dve.Fori(0, NTL) as t:
                        one = bass.ds(t, 1)
                        dve.tensor_scalar(nodes[:, one, :].squeeze(1), nodes[:, one, :].squeeze(1),
                                          moments[:, one, 0], rstd[:, one], ALU.subtract, ALU.mult
                                          ).then_inc(finished, 1)

                @block.sync
                def _(sp):
                    at, n = 0, 0
                    while at < ft:
                        m = min(2 * QUAD, ft - at)
                        sp.wait_ge(finished, at + m)
                        sp.dma_start(out[at * NODES:(at + m) * NODES, :].rearrange("(t p) f -> p t f", p=NODES),
                                     nodes[:, at:at + m, :]).then_inc(stored, 16)
                        at, n = at + m, n + 1
                    if fr:
                        sp.wait_ge(finished, ft + 1)
                        sp.dma_start(out[ft * NODES:N, :], nodes[0:fr, ft, :]).then_inc(stored, 16)
                        n += 1
                    sp.wait_ge(stored, 16 * n)


_INS = ['x', 'src', 'dst', 'edge_type_9', 'L0_gnn_W_msg', 'L0_gnn_b_msg', 'L0_gnn_edge_embed', 'L0_gnn_W_ih',
        'L0_gnn_W_hh', 'L0_gnn_b_ih', 'L0_gnn_b_hh', 'L1_gnn_fc_weight', 'L1_gnn_attn', 'L1_gnn_eps']


def kernel(**inputs):
    import numpy as _np
    import concourse.bacc as _bacc
    from concourse import mybir as _mybir
    from concourse.bass_utils import run_bass_kernel_spmd as _run

    nc = _bacc.Bacc("TRN2", target_bir_lowering=False, num_devices=1)
    arrays, args = {}, []
    for name in _INS:
        a = _np.ascontiguousarray(inputs[name])
        arrays[f"in_{name}_dram"] = a
        args.append(nc.dram_tensor(f"in_{name}_dram", a.shape, _mybir.dt.from_np(a.dtype), kind="ExternalInput").ap())
    out = nc.dram_tensor("out_0_dram", inputs['x'].shape, _mybir.dt.float32, kind="ExternalOutput").ap()
    graph_layers(nc, *args, out)
    r = _run(nc, [arrays], core_ids=[0])
    return r.results[0]["out_0_dram"]
```

```python
from contextlib import ExitStack, contextmanager

import concourse.bass as bass
from concourse import mybir

F32 = mybir.dt.float32
F16 = mybir.dt.float16
BF16 = mybir.dt.bfloat16
I32 = mybir.dt.int32
ALU = mybir.AluOpType
ACT = mybir.ActivationFunctionType
AX = mybir.AxisListType
RMAX = bass.bass_isa.ReduceOp.max

P = 128
CHUNK = 7
NC = 4
GROUP = CHUNK * NC
NODES = P
QUAD = 4
WIN = 8
WINS = P // WIN
WT = 4
PER = WINS // NC
RING = 8
LEFTS = {1: 9, 5: 11, 8: 13, 11: 15}
CB = 4
HALF = WINS // 2
COUNTED = 0.53
LN_EPS = 1e-5
LEAK = 0.2
FAR = 1.0e6


def graph_layers(nc, x, src, dst, edge_type, W_msg, b_msg, edge_embed, W_ih, W_hh, b_ih, b_hh,
                 fc_weight, attn, eps, out):
    N, D = x.shape
    E = src.shape[0]
    NT = edge_embed.shape[0]
    assert D == P and W_ih.shape == (3 * D, D)
    NG = -(-E // (P * GROUP))
    TILES = NG * GROUP
    QN = QUAD * NODES
    NQ = -(-N // QN)
    NTL = NQ * QUAD
    SPANS = -(-N // P)
    NPAD = max(NTL * NODES, (SPANS + 1) * P)
    MAXB = NG * (-(-N // P))
    KW = -(-(MAXB + 1) // P)
    GC = max(1, min(NG - 1, round(COUNTED * NG)))
    CT = GC * GROUP
    NBK = -(-(CT + WT) // P)
    CTX = NBK * P
    CODES = SPANS * WIN
    BANK = 512
    WC = -(-((SPANS + 1) * WINS) // P)
    WIDE = max(NPAD, NTL * D, 2 * D + 6 * CTX)
    NOWHERE = (SPANS + 2) * P
    LONG = max(CTX, WC * P)
    MAXR = -(-CT // WT)
    MAXT = max(MAXB, SPANS * MAXR)
    assert NG > 1 and N > P and CODES <= BANK

    rows = nc.dram_tensor("rows", [NPAD, 2 * D], F32).ap()
    parts = nc.dram_tensor("parts", [NPAD, 3 * D], BF16).ap()

    first_of = nc.dram_tensor("first_of", [1, P * KW], I32).ap()
    column_of = nc.dram_tensor("column_of", [1, P * KW], I32).ap()
    first_row = nc.dram_tensor("first_row", [1, P * KW], F32).ap()

    tile_ext = nc.dram_tensor("tile_ext", [2, CTX], F32).ap()
    win_ext = nc.dram_tensor("win_ext", [2, WC * P], F32).ap()

    with ExitStack() as whole:
        def sb(name, shape, dt, ctx=whole):
            return ctx.enter_context(nc.sbuf_tensor(name, shape, dt))

        def psum(name, shape, dt, ctx):
            return ctx.enter_context(nc.psum_tensor(name, shape, dt))

        def sem(name):
            return whole.enter_context(nc.semaphore(name))

        nodes = sb("nodes", [NODES, NTL, D], F32)
        work = sb("work", [P, WIDE], F32)
        sums = sb("sums", [P, max(NPAD, 3 * LONG + 2 * KW * NG)], F32)
        small_rows = sb("small_rows", [P, max(NPAD, WC * P)], F32)
        counts = small_rows[0:NT, :]
        src_tab = sb("src_tab", [P, TILES], I32)
        dst_f = sb("dst_f", [P, TILES], F32)
        type_f = sb("type_f", [P, TILES], F32)
        bodies_i = sb("bodies_i", [P, 1], I32)
        trips_i = sb("trips_i", [P, 1], I32)
        skip_i = sb("skip_i", [P, 1], I32)
        iota_f = sb("iota_f", [P, P], F32)
        ident = sb("ident", [P, P], F32)
        ident_b = sb("ident_b", [P, P], BF16)
        wT = sb("wT", [P, 8, D], F32)
        table = sb("table", [NT, D], F32)
        bih = sb("bih", [P, 3], F32)
        bhh = sb("bhh", [P, 3], F32)
        brz = sb("brz", [P, 2], F32)
        a_all = sb("a_all", [P, D], F32)
        c_x = sb("c_x", [NODES, 1], F32)
        ones = sb("ones", [NT, 1], F32)
        rdeg = sb("rdeg", [NODES, NTL], F32)
        stats = sb("stats", [NODES, QUAD, 6], F32)
        moments = sb("moments", [NODES, NTL, 2], F32)
        rstd = sb("rstd", [NODES, NTL], F32)
        dl = sb("dl", [P, GROUP], F32)
        idx = sb("idx", [P, NC, CHUNK], I32)

        chunk_begun = sem("chunk_begun")

        @contextmanager
        def every_body(eng):
            bodies = eng.value_load(bodies_i[0:1, 0:1], min_val=1, max_val=MAXB)
            with eng.Fori(0, bodies) as k:
                yield k

        def node_of(eng, k):
            return eng.value_load(first_of[:, bass.ds(k, 1)], min_val=0, max_val=N - 1)

        def column(eng, k):
            return eng.value_load(column_of[:, bass.ds(k, 1)], min_val=0, max_val=TILES - GROUP)

        layer0 = whole.enter_context(ExitStack())
        packed = sb("packed", [P, CTX, 5], F16, layer0)
        codes_f = sb("codes_f", [P, CODES], F16, layer0)
        row = slice(P // 4, P // 4 + 1)
        start_i = small_rows[row, 0:WC * P].bitcast(I32)
        rounds_i = sb("rounds_i", [P, SPANS + 1], I32, layer0)
        iota_h = sb("iota_h", [P, P], F16, layer0)
        span_no = sb("span_no", [P, SPANS + 1], F32, layer0)
        zero_b = sb("zero_b", [P, P], BF16, layer0)

        with ExitStack() as ph:
            dst_i = sb("dst_i", [P, TILES], I32, ph)
            type_i = sb("type_i", [P, TILES], I32, ph)
            iota_i = sb("iota_i", [P, P], I32, ph)
            codes_i = sb("codes_i", [P, max(CTX, CODES)], I32, ph)
            win_no_i = sb("win_no_i", [P, WC], I32, ph)
            span_no_i = sb("span_no_i", [P, SPANS + 1], I32, ph)
            tiles_i = sb("tiles_i", [P, 3, CTX], I32, ph)
            turned_i = tiles_i[:, 0:2, :]
            tiles_f = sums[:, 0:3 * CTX].rearrange("p (j t) -> p j t", j=3)
            both = sums[:, 3 * LONG:3 * LONG + 2 * KW * NG].rearrange("p (u k g) -> p u k g", u=2, g=NG)
            past, prod = both[:, 0, :, :], both[:, 1, :, :]
            scratch = work[:, 2 * D:2 * D + 6 * CTX].rearrange("p (j u t) -> p j u t", j=3, u=2)
            high_i, low_i = scratch[:, 0, :, :].bitcast(I32), scratch[:, 1, :, :].bitcast(I32)
            wext_all = sums[:, 0:2 * WC * P].rearrange("p (u w) -> p u w", u=2)
            length = sums[:, 2 * WC * P:3 * WC * P]
            text_all = scratch[:, 2, :, :]
            meets = sums[:, 0:2 * CTX].rearrange("p (u t) -> p u t", u=2)
            text = sb("text", [P, 2, NBK], F32, ph)
            up = sb("up", [P, CTX], F32, ph)
            down = sb("down", [P, CTX], F32, ph)
            win_lo = sb("win_lo", [P, WC], F32, ph)
            win_hi = sb("win_hi", [P, WC], F32, ph)
            wext = sb("wext", [P, 2, WC], F32, ph)
            rounds_f = sb("rounds_f", [P, SPANS + 1], F32, ph)
            in_use = sb("in_use", [P, SPANS + 1], F32, ph)
            top = sb("top", [P, 1], F32, ph)
            trips_f = sb("trips_f", [P, 1], F32, ph)
            trips2_f = sb("trips2_f", [P, 1], F32, ph)
            t_ps = psum("t_ps", [P, 3, CTX], F32, ph)
            tiles_in = sem("tiles_in")
            tiles_set = sem("tiles_set")
            tiles_cast = sem("tiles_cast")
            tiles_turned = sem("tiles_turned")
            packing = sem("packing")
            text_out = sem("text_out")
            text_in = sem("text_in")
            wext_out = sem("wext_out")
            wext_in = sem("wext_in")
            windows = sem("windows")
            extreme_steps = sem("extreme_steps")
            counting = sem("counting")
            last_past = sb("last_past", [P, KW], F32, ph)
            raw = sb("raw", [P, 8, D], F32, ph)
            bmsg = sb("bmsg", [NT, D], F32, ph)
            far = sb("far", [P, GROUP], F32, ph)
            ext = sb("ext", [P, 2 * NG], F32, ph)
            ext_all = sb("ext_all", [P, 2 * NG], F32, ph)
            span_f = sb("span_f", [P, NG], F32, ph)
            span_i = sb("span_i", [P, NG], I32, ph)
            win_i = sb("win_i", [P, NG], I32, ph)
            low = sb("low", [P, NG], F32, ph)
            step = sb("step", [P, NG], F32, ph)
            nwin = sb("nwin", [P, NG], F32, ph)
            upto = sb("upto", [P, NG], F32, ph)
            unit = sb("unit", [P, NG], F32, ph)
            k_i = sb("k_i", [P, KW], I32, ph)
            k_f = sb("k_f", [P, KW], F32, ph)
            of_k = sb("of_k", [P, 3, KW], F32, ph)
            first_k = sb("first_k", [P, KW], F32, ph)
            first_ki = sb("first_ki", [P, KW], I32, ph)
            column_ki = sb("column_ki", [P, KW], I32, ph)
            tables_done = sem("tables_done")
            tables_out = sem("tables_out")
            w_ps = psum("w_ps", [P, 8, D], F32, ph)
            iota_done = sem("iota_done")
            zeroed = sem("zeroed")
            select_done = sem("select_done")
            pads_done = sem("pads_done")
            edges_in = sem("edges_in")
            nodes_in = sem("nodes_in")
            weights_in = sem("weights_in")
            small_in = sem("small_in")
            pad_rows_out = sem("pad_rows_out")
            zeros_done = sem("zeros_done")
            prep = sem("prep")
            ext_done = sem("ext_done")
            ext_reduced = sem("ext_reduced")
            w_turned = sem("w_turned")
            w_copied = sem("w_copied")

            full = NG - 1
            rem = E - full * P * GROUP
            rp, rl = rem // GROUP, rem % GROUP
            n_edge_dmas = 3 * ((full > 0) + (rp > 0) + (rl > 0))
            ft, fr = N // NODES, N % NODES
            n_node_dmas = (ft > 0) + (fr > 0)

            with nc.Block() as block:
                @block.sync
                def _(sp):
                    sp.wait_ge(tiles_set, 3)
                    ctf, ctr = CT // P, CT % P
                    n_tile = 0
                    for j, edges in enumerate((src, dst, edge_type)):
                        if ctf:
                            sp.dma_start(tiles_i[:, j, 0:ctf * P].rearrange("p (b e) -> p b e", e=P),
                                         edges[0:ctf * P * P].rearrange("(b p e) -> p b e", p=P, e=P)
                                         ).then_inc(tiles_in, 16)
                            n_tile += 1
                        if ctr:
                            sp.dma_start(tiles_i[0:ctr, j, ctf * P:(ctf + 1) * P],
                                         edges[ctf * P * P:CT * P].rearrange("(p e) -> p e", e=P)
                                         ).then_inc(tiles_in, 16)
                            n_tile += 1
                    sp.wait_ge(tiles_set, 5)
                    with nc.allow_non_contiguous_dma(reason="an extreme per tile or window, once"):
                        for j in range(2):
                            sp.dma_start(tile_ext[j:j + 1, :].rearrange("o (b p) -> p (o b)", p=P),
                                         text[:, j, :]).then_inc(text_out, 16)
                    sp.wait_ge(text_out, 32)
                    for j in range(2):
                        sp.dma_start(text_all[:, j, :], tile_ext[j:j + 1, :].to_broadcast([P, CTX])
                                     ).then_inc(text_in, 16)
                    sp.wait_ge(pads_done, 4)
                    for tab, edges in ((dst_i, dst), (src_tab, src), (type_i, edge_type)):
                        if full:
                            sp.dma_start(tab[:, 0:full * GROUP].rearrange("p (g j) -> p g j", j=GROUP),
                                         edges[0:full * P * GROUP].rearrange("(g p j) -> p g j", p=P, j=GROUP)
                                         ).then_inc(edges_in, 16)
                        at = full * P * GROUP
                        if rp:
                            sp.dma_start(tab[0:rp, full * GROUP:TILES],
                                         edges[at:at + rp * GROUP].rearrange("(p j) -> p j", j=GROUP)
                                         ).then_inc(edges_in, 16)
                        if rl:
                            sp.dma_start(tab[rp:rp + 1, full * GROUP:full * GROUP + rl],
                                         edges[at + rp * GROUP:E].rearrange("(p j) -> p j", p=1)
                                         ).then_inc(edges_in, 16)
                    if ft:
                        sp.dma_start(nodes[:, 0:ft, :], x[0:ft * NODES, :].rearrange("(t p) f -> p t f", p=NODES)
                                     ).then_inc(nodes_in, 16)
                    if fr:
                        sp.dma_start(nodes[0:fr, ft, :], x[ft * NODES:N, :]).then_inc(nodes_in, 16)
                    sp.wait_ge(windows, 2 * WC + 3)
                    with nc.allow_non_contiguous_dma(reason="an extreme per tile or window, once"):
                        for j in range(2):
                            sp.dma_start(win_ext[j:j + 1, :].rearrange("o (c p) -> p (o c)", p=P),
                                         wext[:, j, :]).then_inc(wext_out, 16)
                    sp.wait_ge(wext_out, 32)
                    for j in range(2):
                        sp.dma_start(wext_all[:, j, :], win_ext[j:j + 1, :].to_broadcast([P, WC * P])
                                     ).then_inc(wext_in, 16)
                    sp.wait_ge(zeros_done, 1)
                    for r in range(NTL * NODES, NPAD, P):
                        m = min(P, NPAD - r)
                        sp.dma_start(rows[r:r + m, :], work[0:m, 0:2 * D]).then_inc(pad_rows_out, 16)
                        sp.dma_start(parts[r:r + m, :], work[0:m, 0:3 * D // 2].bitcast(BF16)
                                     ).then_inc(pad_rows_out, 16)
                    if NPAD > NTL * NODES:
                        sp.wait_ge(pad_rows_out, 32 * (-(-(NPAD - NTL * NODES) // P)))
                    sp.wait_ge(nodes_in, 16 * n_node_dmas)
                    sp.wait_ge(tables_done, 3)
                    for to, table_k in ((first_of, first_ki), (column_of, column_ki), (first_row, first_k)):
                        sp.dma_start(to.rearrange("o (p w) -> (o p) w", w=KW), table_k[:]).then_inc(tables_out, 16)
                    sp.wait_ge(tables_out, 48)

                @block.gpsimd
                def _(pool):
                    pool.iota(iota_i[:], pattern=[[1, P]], base=0, channel_multiplier=0).then_inc(iota_done, 1)
                    pool.iota(k_i[:], pattern=[[1, KW]], base=0, channel_multiplier=KW).then_inc(iota_done, 1)
                    pool.iota(codes_i[:], pattern=[[1, max(CTX, CODES)]], base=1, channel_multiplier=0
                              ).then_inc(iota_done, 1)
                    pool.iota(win_no_i[:], pattern=[[WIN * P, WC]], base=0, channel_multiplier=WIN
                              ).then_inc(iota_done, 1)
                    pool.iota(span_no_i[:], pattern=[[WINS, SPANS + 1]], base=0, channel_multiplier=0
                              ).then_inc(iota_done, 1)
                    pool.memset(zero_b[:], 0.0)
                    pool.memset(counts[:, 0:NPAD], 0.0)
                    pool.memset(ident[:], 0.0).then_inc(zeroed, 1)
                    pool.wait_ge(zeroed, 1)
                    pool.affine_select(out=ident[:], in_=ident[:], compare_op=ALU.not_equal, fill=1.0, base=0,
                                       pattern=[[-1, P]], channel_multiplier=1).then_inc(select_done, 1)
                    pool.wait_ge(ext_done, 4)
                    pool.partition_all_reduce(ext_all[:], ext[:], P, RMAX).then_inc(ext_reduced, 1)
                    pool.wait_ge(counting, 1)
                    pool.memset(sums[:, 0:NPAD // 2], 0.0)

                @block.scalar
                def _(act):
                    act.dma_start(raw[:, 0, :], W_msg).then_inc(weights_in, 16)
                    act.dma_start(raw[:, 1, :], fc_weight).then_inc(weights_in, 16)
                    act.dma_start(raw[:, 2:5, :], W_ih.rearrange("(g h) k -> h g k", g=3)).then_inc(weights_in, 16)
                    act.dma_start(raw[:, 5:8, :], W_hh.rearrange("(g h) k -> h g k", g=3)).then_inc(weights_in, 16)
                    with nc.allow_non_contiguous_dma(reason="bias columns, 768 elements"):
                        act.dma_start(bih[:], b_ih.rearrange("(g h) -> h g", g=3)).then_inc(small_in, 16)
                        act.dma_start(bhh[:], b_hh.rearrange("(g h) -> h g", g=3)).then_inc(small_in, 16)
                    act.dma_start(table[:], edge_embed).then_inc(small_in, 16)
                    act.dma_start(bmsg[:], b_msg.rearrange("(o f) -> o f", o=1).to_broadcast([NT, D])
                                  ).then_inc(small_in, 16)
                    act.dma_start(a_all[:], attn.rearrange("a b f -> (a b) f").to_broadcast([P, D])
                                  ).then_inc(small_in, 16)
                    act.dma_start(c_x[:], eps.rearrange("(o f) -> o f", o=1).to_broadcast([NODES, 1])
                                  ).then_inc(small_in, 16)
                    act.wait_ge(w_turned, 8)
                    act.copy(wT[:, 0:4, :], w_ps[:, 0:4, :]).then_inc(w_copied, 1)
                    act.copy(wT[:, 4:8, :], w_ps[:, 4:8, :]).then_inc(w_copied, 1)

                @block.tensor
                def _(pe):
                    pe.wait_ge(weights_in, 64)
                    pe.wait_ge(select_done, 1)
                    for i in range(8):
                        pe.transpose(w_ps[:, i, :], raw[:, i, :], ident[:]).then_inc(w_turned, 1)
                    pe.wait_ge(tiles_cast, 1)
                    for j in range(3):
                        for b in range(NBK):
                            t = pe.transpose(t_ps[:, j, b * P:(b + 1) * P], tiles_f[:, j, b * P:(b + 1) * P],
                                             ident[:])
                        t.then_inc(tiles_turned, 1)

                @block.vector
                def _(dve):
                    last = slice(full * GROUP, TILES)
                    dve.memset(tiles_i[:, 0, :], 0).then_inc(tiles_set, 1)
                    dve.memset(tiles_i[:, 1, :], NOWHERE).then_inc(tiles_set, 1)
                    dve.memset(tiles_i[:, 2, :], 0).then_inc(tiles_set, 1)
                    dve.memset(src_tab[:, last], 0).then_inc(pads_done, 1)
                    dve.memset(dst_i[:, last], -1).then_inc(pads_done, 1)
                    dve.memset(type_i[:, last], 0).then_inc(pads_done, 1)
                    dve.memset(nodes[:, ft:NTL, :], 0.0).then_inc(pads_done, 1)
                    dve.memset(work[:, 0:2 * D], 0.0).then_inc(zeros_done, 1)
                    dve.memset(ones[:], 1.0)
                    dve.wait_ge(iota_done, 5)
                    dve.tensor_copy(iota_f[:], iota_i[:])
                    dve.tensor_copy(k_f[:], k_i[:])
                    dve.tensor_copy(iota_h[:], iota_i[:])
                    dve.tensor_copy(codes_f[:], codes_i[:, 0:CODES])
                    dve.tensor_copy(up[:], codes_i[:, 0:CTX])
                    dve.tensor_scalar(down[:], codes_i[:, 0:CTX], -1.0, float(CTX + 1), ALU.mult, ALU.add)
                    dve.tensor_copy(win_lo[:], win_no_i[:])
                    dve.tensor_scalar(win_hi[:], win_no_i[:], float(WIN - 1), None, ALU.add)
                    dve.tensor_copy(span_no[:], span_no_i[:])
                    dve.memset(unit[:], 1.0)
                    dve.memset(step[:], 0.0)
                    dve.wait_ge(select_done, 1)
                    dve.tensor_copy(ident_b[:], ident[:])
                    dve.wait_ge(small_in, 96)
                    dve.tensor_tensor(table[:], table[:], bmsg[:], ALU.add)
                    dve.tensor_tensor(brz[:], bih[:, 0:2], bhh[:, 0:2], ALU.add)
                    dve.tensor_scalar(c_x[:], c_x[:], 2.0, None, ALU.add)
                    dve.wait_ge(tiles_in, 16 * 3 * ((CT >= P) + (CT % P > 0)))
                    dve.tensor_copy(tiles_f[:], tiles_i[:]).then_inc(tiles_cast, 1)
                    dve.wait_ge(tiles_cast, 1)
                    by_tile = tiles_f[:, 1, :].rearrange("p (b e) -> p b e", e=P)
                    dve.tensor_reduce(text[:, 0, :], by_tile, AX.X, ALU.min).then_inc(tiles_set, 1)
                    dve.tensor_reduce(text[:, 1, :], by_tile, AX.X, ALU.max).then_inc(tiles_set, 1)
                    dve.wait_ge(tiles_turned, 3)
                    dve.tensor_copy(turned_i[:], t_ps[:, 0:2, :]).then_inc(packing, 1)
                    dve.tensor_scalar(packed[:, :, 4], t_ps[:, 2, :], 0.0, float(NT - 1), ALU.max, ALU.min)
                    dve.wait_ge(packing, 1)
                    for j, bits in ((0, 7), (1, 3)):
                        dve.tensor_single_scalar(high_i[:, j, :], turned_i[:, j, :], bits, ALU.arith_shift_right
                                                 ).then_inc(packing, 1)
                        dve.tensor_single_scalar(low_i[:, j, :], turned_i[:, j, :], 2 ** bits - 1, ALU.bitwise_and
                                                 ).then_inc(packing, 1)
                    dve.wait_ge(packing, 5)
                    dve.tensor_scalar(packed[:, :, 2], low_i[:, 1, :], 1.0, None, ALU.add).then_inc(packing, 1)
                    dve.tensor_copy(packed[:, :, 0], high_i[:, 1, :])
                    dve.tensor_copy(packed[:, :, 3], low_i[:, 0, :])
                    dve.wait_ge(packing, 6)
                    dve.scalar_tensor_tensor(out=packed[:, :, 1], in0=high_i[:, 0, :], scalar=float(WIN),
                                             in1=packed[:, :, 2], op0=ALU.mult, op1=ALU.add)
                    dve.wait_ge(text_in, 32)
                    for c in range(WC):
                        if c:
                            dve.wait_ge(windows, 2 * c)
                        dve.tensor_scalar(meets[:, 0, :], text_all[:, 1, :], win_lo[:, c:c + 1], None, ALU.is_ge
                                          ).then_inc(packing, 1)
                        dve.wait_ge(packing, 7 + 2 * c)
                        dve.scalar_tensor_tensor(out=meets[:, 1, :], in0=text_all[:, 0, :],
                                                 scalar=win_hi[:, c:c + 1], in1=meets[:, 0, :],
                                                 op0=ALU.is_le, op1=ALU.mult).then_inc(packing, 1)
                        dve.wait_ge(packing, 8 + 2 * c)
                        dve.tensor_tensor_reduce(meets[:, 0, :], meets[:, 1, :], down[:], 1.0, 0.0,
                                                 ALU.mult, ALU.max, wext[:, 0, c:c + 1]).then_inc(windows, 1)
                        dve.tensor_tensor_reduce(meets[:, 1, :], meets[:, 1, :], up[:], 1.0, 0.0,
                                                 ALU.mult, ALU.max, wext[:, 1, c:c + 1]).then_inc(windows, 1)
                    dve.wait_ge(windows, 2 * WC)
                    dve.tensor_scalar(wext[:, 0, :], wext[:, 0, :], -1.0, float(CTX), ALU.mult, ALU.add
                                      ).then_inc(windows, 1)
                    dve.wait_ge(windows, 2 * WC + 1)
                    dve.tensor_scalar(wext[:, 0, :], wext[:, 0, :], float(CT), None, ALU.min).then_inc(windows, 1)
                    dve.sem_inc(windows, 1)
                    dve.wait_ge(edges_in, 16 * n_edge_dmas)
                    dve.tensor_copy(dst_f[:], dst_i[:]).then_inc(prep, 1)
                    dve.tensor_scalar(type_f[:], type_i[:], 0.0, float(NT - 1), ALU.max, ALU.min)
                    dve.wait_ge(prep, 1)
                    dve.tensor_scalar(far[:], dst_f[:, last], 0.0, FAR, ALU.is_lt, ALU.mult).then_inc(prep, 1)
                    dve.tensor_reduce(ext[:, NG:2 * NG], dst_f[:].rearrange("p (g j) -> p g j", j=GROUP),
                                      AX.X, ALU.max).then_inc(ext_done, 1)
                    dve.tensor_reduce(ext[:, 0:NG], dst_f[:].rearrange("p (g j) -> p g j", j=GROUP),
                                      AX.X, ALU.min).then_inc(ext_done, 1)
                    dve.wait_ge(prep, 2)
                    dve.tensor_tensor(far[:], far[:], dst_f[:, last], ALU.add).then_inc(prep, 1)
                    dve.wait_ge(prep, 3)
                    dve.wait_ge(ext_done, 2)
                    dve.tensor_reduce(ext[:, full:full + 1], far[:], AX.X, ALU.min).then_inc(ext_done, 1)
                    dve.wait_ge(ext_done, 3)
                    dve.tensor_scalar(ext[:, 0:NG], ext[:, 0:NG], -1.0, None, ALU.mult).then_inc(ext_done, 1)
                    dve.wait_ge(ext_reduced, 1)
                    dve.tensor_scalar(low[:], ext_all[:, 0:NG], -1.0, None, ALU.mult).then_inc(prep, 1)
                    dve.tensor_tensor(span_f[:], ext_all[:, NG:2 * NG], ext_all[:, 0:NG], ALU.add).then_inc(prep, 1)
                    dve.wait_ge(prep, 5)
                    dve.tensor_copy(span_i[:], span_f[:]).then_inc(prep, 1)
                    dve.wait_ge(prep, 6)
                    dve.tensor_single_scalar(win_i[:], span_i[:], 7, ALU.arith_shift_right).then_inc(prep, 1)
                    dve.wait_ge(prep, 7)
                    dve.tensor_scalar(nwin[:], win_i[:], 1.0, None, ALU.add).then_inc(prep, 1)
                    dve.wait_ge(prep, 8)
                    dve.tensor_tensor_scan(upto[:], unit[:], nwin[:], 0.0, ALU.mult, ALU.add).then_inc(prep, 1)
                    if NG > 1:
                        dve.tensor_tensor(step[:, 0:NG - 1], low[:, 1:NG], low[:, 0:NG - 1], ALU.subtract
                                          ).then_inc(prep, 1)
                    else:
                        dve.sem_inc(prep, 1)
                    dve.wait_ge(prep, 10)
                    dve.tensor_copy(bodies_i[:], upto[:, NG - 1:NG])
                    dve.tensor_copy(skip_i[:], upto[:, GC - 1:GC])
                    dve.tensor_reduce(top[:], ext_all[:, NG:NG + GC], AX.X, ALU.max)
                    wide = [P, KW, NG]
                    dve.tensor_tensor(past[:], k_f[:].unsqueeze(2).to_broadcast(wide),
                                      upto[:].unsqueeze(1).to_broadcast(wide), ALU.is_ge).then_inc(prep, 1)
                    dve.wait_ge(prep, 11)
                    dve.tensor_copy(last_past[:], past[:, :, NG - 1])
                    dve.tensor_reduce(of_k[:, 0, :], past[:], AX.X, ALU.add).then_inc(prep, 1)
                    dve.tensor_tensor(prod[:], past[:], step[:].unsqueeze(1).to_broadcast(wide), ALU.mult
                                      ).then_inc(prep, 1)
                    dve.wait_ge(prep, 13)
                    dve.tensor_tensor(past[:], past[:], nwin[:].unsqueeze(1).to_broadcast(wide), ALU.mult
                                      ).then_inc(prep, 1)
                    dve.tensor_reduce(of_k[:, 1, :], prod[:], AX.X, ALU.add).then_inc(prep, 1)
                    dve.wait_ge(prep, 14)
                    dve.tensor_reduce(of_k[:, 2, :], past[:], AX.X, ALU.add).then_inc(prep, 1)
                    dve.wait_ge(prep, 16)
                    dve.tensor_tensor(of_k[:, 2, :], k_f[:], of_k[:, 2, :], ALU.subtract).then_inc(prep, 1)
                    dve.tensor_scalar(of_k[:, 1, :], of_k[:, 1, :], low[:, 0:1], None, ALU.add).then_inc(prep, 1)
                    dve.wait_ge(prep, 18)
                    dve.scalar_tensor_tensor(out=first_k[:], in0=of_k[:, 2, :], scalar=float(P), in1=of_k[:, 1, :],
                                             op0=ALU.mult, op1=ALU.add).then_inc(prep, 1)
                    dve.tensor_scalar(column_ki[:], of_k[:, 0, :], float(NG - 1), float(GROUP), ALU.min, ALU.mult
                                      ).then_inc(tables_done, 1)
                    dve.wait_ge(prep, 19)
                    dve.tensor_scalar(first_k[:], first_k[:], float(N - 1), None, ALU.min).then_inc(tables_done, 1)
                    dve.wait_ge(tables_done, 2)
                    dve.tensor_copy(first_ki[:], first_k[:]).then_inc(prep, 1)
                    dve.wait_ge(prep, 20)
                    dve.scalar_tensor_tensor(out=first_k[:], in0=last_past[:], scalar=FAR, in1=first_k[:],
                                             op0=ALU.mult, op1=ALU.add).then_inc(tables_done, 1)
                    dve.wait_ge(wext_in, 32)
                    dve.tensor_copy(start_i[:], wext_all[row, 0, :]).then_inc(windows, 1)
                    dve.tensor_tensor(length[:], wext_all[:, 1, :], wext_all[:, 0, :], ALU.subtract
                                      ).then_inc(windows, 1)
                    dve.wait_ge(windows, 2 * WC + 5)
                    dve.tensor_reduce(rounds_f[:], length[:, 0:(SPANS + 1) * WINS].rearrange(
                        "p (s i) -> p s i", i=WINS), AX.X, ALU.max).then_inc(windows, 1)
                    dve.wait_ge(windows, 2 * WC + 6)
                    dve.tensor_scalar(rounds_f[:], rounds_f[:], 1.0, float(WT - 1), ALU.max, ALU.add
                                      ).then_inc(counting, 1)
                    dve.wait_ge(counting, 1)
                    dve.tensor_copy(rounds_i[:], rounds_f[:]).then_inc(windows, 1)
                    dve.wait_ge(windows, 2 * WC + 7)
                    dve.tensor_single_scalar(rounds_i[:], rounds_i[:], 2, ALU.arith_shift_right
                                             ).then_inc(windows, 1)
                    dve.wait_ge(windows, 2 * WC + 8)
                    dve.tensor_copy(rounds_f[:], rounds_i[:]).then_inc(counting, 1)
                    dve.tensor_scalar(in_use[:], span_no[:], float(WIN), top[:, 0:1], ALU.mult, ALU.is_le
                                      ).then_inc(counting, 1)
                    dve.wait_ge(counting, 3)
                    dve.tensor_tensor(in_use[:], in_use[:], rounds_f[:], ALU.mult).then_inc(counting, 1)
                    dve.tensor_tensor(trips2_f[:], upto[:, NG - 1:NG], upto[:, GC - 1:GC], ALU.subtract
                                      ).then_inc(counting, 1)
                    dve.wait_ge(counting, 5)
                    dve.tensor_reduce(trips_f[:], in_use[:], AX.X, ALU.add).then_inc(counting, 1)
                    dve.wait_ge(counting, 6)
                    dve.tensor_tensor(trips_i[:], trips_f[:], trips2_f[:], ALU.max)
                    dve.memset(sums[:, NPAD // 2:NPAD], 0.0)

        with layer0 as ph:
            cols_sb = work[:, 0:SPANS * P].rearrange("p (t d) -> p t d", d=P)
            got = sb("got0", [P, NC, CHUNK, D], F32, ph)
            hot = sb("hot0", [P, 2, CHUNK, P], F32, ph)
            hot_b = sb("hot_b", [P, 2, CHUNK, P], BF16, ph)
            kind = sb("kind", [P, 2, CHUNK, NT], BF16, ph)
            stage = sb("stage", [P, 2, HALF * WT, 5], F16, ph)
            win_no = sb("win_no", [P, WINS], F32, ph)
            win_0 = sb("win_0", [P, WINS], F32, ph)
            iota_1 = sb("iota_1", [P, WIN], F32, ph)
            inside = sb("inside", [P, HALF * WT], F32, ph)
            coded = sb("coded", [P, 2, HALF * WT, 2], F32, ph)
            kind_w = sb("kind_w", [P, 2, HALF * WT, NT], BF16, ph)
            hot_w = sb("hot_w", [P, 2, HALF * WT, WIN], BF16, ph)
            left = sb("left", [P, RING, WT, P], BF16, ph)
            right = sb("right", [P, RING, WT, CODES], BF16, ph)
            c_ps = psum("c_ps", [P, CB, BANK], F32, ph)
            span_ps = psum("span_ps", [P, BANK], F32, ph)
            kinds_ps = psum("kinds_ps", [P, BANK], F32, ph)
            sum_ps = psum("sum_ps", [P, BANK], F32, ph)
            cnt_ps = psum("cnt_ps", [P, BANK], F32, ph)
            edges_now = sb("edges_now", [P, 2, GROUP], F32, ph)
            types = sb("types", [P, GROUP], F32, ph)
            at_now = sb("at_now", [P, 1], I32, ph)
            low_f = sb("low_f", [P, 2, HALF * WT], F32, ph)
            apart = sb("apart", [P, WT, P], BF16, ph)
            one = sb("one", [P, 1], F32, ph)
            acc_s = sb("acc_s", [P, 4, P], F32, ph)
            body_in = sem("body_in")
            body_begun = sem("body_begun")
            first_now = sb("first_now", [P, 1], F32, ph)
            body_taken = sem("body_taken")
            apart_done = sem("apart_done")
            left_made = sem("left_made")
            idx_in = [sem(f"idx_in0_{c}") for c in range(NC)]
            gathered = [sem(f"gathered0_{c}") for c in range(NC)]
            stage_in = [sem(f"stage_in{h}") for h in range(2)]
            stage_used = sem("stage_used")
            hot_done = sem("hot_done0")
            hot_cast = sem("hot_cast")
            summed = sem("summed0")
            added = sem("added0")
            drained = sem("drained")
            dl_done = sem("dl_done0")
            inside_done = sem("inside_done")
            coded_done = sem("coded_done")
            made = sem("made")
            counted = sem("counted")
            c_copied = sem("c_copied")
            applied = sem("applied")

            @contextmanager
            def every_trip(eng):
                trips = eng.value_load(trips_i[0:1, 0:1], min_val=1, max_val=MAXT)
                with eng.Fori(0, trips) as k:
                    yield k

            def states(eng, what):
                body, span, turn = (eng.alloc_register(f"{name}_{what}") for name in ("body", "span", "round"))
                eng.reg_mov(body, eng.value_load(skip_i[0:1, 0:1], min_val=1, max_val=MAXB))
                eng.reg_mov(span, 0)
                eng.reg_mov(turn, 0)
                return body, span, turn

            def advance(eng, body, span, turn, tmp):
                rounds = eng.value_load(rounds_i[0:1, bass.ds(eng.snap(span, min_val=0, max_val=SPANS), 1)],
                                        min_val=1, max_val=MAXR)
                eng.reg_alu(body, body, 1, op=ALU.add)
                eng.reg_alu(body, body, P * KW - 1, op=ALU.min)
                eng.reg_alu(turn, turn, 1, op=ALU.add)
                eng.reg_mov(tmp, rounds)
                eng.reg_alu(tmp, turn, tmp, op=ALU.is_ge)
                eng.reg_alu(span, span, tmp, op=ALU.add)
                eng.reg_alu(span, span, SPANS, op=ALU.min)
                eng.reg_alu(tmp, tmp, 1, op=ALU.bitwise_xor)
                eng.reg_alu(turn, turn, tmp, op=ALU.mult)

            with nc.Block() as block:
                @block.sync
                def _(sp):
                    body, span, turn = states(sp, "sp")
                    tmp, start = sp.alloc_register("tmp_sp"), sp.alloc_register("start_sp")
                    with every_trip(sp) as k:
                        now = sp.snap(body, min_val=0, max_val=P * KW - 1)
                        col = column(sp, now)
                        sp.wait_ge(body_taken, k + 1)
                        sp.sem_inc(body_begun, 1)
                        sp.dma_start(edges_now[:, 0, :], dst_f[:, bass.ds(col, GROUP)]).then_inc(body_in, 16)
                        sp.dma_start(edges_now[:, 1, :], type_f[:, bass.ds(col, GROUP)]).then_inc(body_in, 16)
                        sp.dma_start(first_now[:], first_row[:, bass.ds(now, 1)].to_broadcast([P, 1])
                                     ).then_inc(body_in, 16)
                        sp.dma_start(at_now[0:1, 0:1], first_of[:, bass.ds(now, 1)]).then_inc(body_in, 16)
                        for c in range(NC):
                            sp.wait_ge(summed, NC * k + c + 1)
                            sp.sem_inc(body_begun, 1)
                            sp.dma_start(idx[:, c, :], src_tab[:, bass.ds(col + c * CHUNK, CHUNK)]
                                         ).then_inc(idx_in[c], 16)
                            for i in range(PER * c, PER * c + PER):
                                at = sp.value_load(start_i[0:1, bass.ds(
                                    sp.snap(span, min_val=0, max_val=SPANS) * WINS + i, 1)], min_val=0, max_val=CT)
                                sp.reg_alu(tmp, turn, WT, op=ALU.mult)
                                sp.reg_mov(start, at)
                                sp.reg_alu(start, start, tmp, op=ALU.add)
                                sp.reg_alu(start, start, CT, op=ALU.min)
                                j = i % HALF * WT
                                if i % HALF == 0:
                                    sp.wait_ge(stage_used, 2 * k + i // HALF + 1)
                                    sp.sem_inc(body_begun, 1)
                                sp.dma_start(stage[:, i // HALF, j:j + WT, :],
                                             packed[:, bass.ds(sp.snap(start, min_val=0, max_val=CT), WT), :]
                                             ).then_inc(stage_in[i // HALF], 16)
                        advance(sp, body, span, turn, tmp)

                @block.gpsimd
                def _(pool):
                    with every_trip(pool) as k:
                        for c in range(NC):
                            pool.wait_ge(idx_in[c], 16 * k + 16)
                            pool.sem_inc(chunk_begun, 1)
                            for i in range(CHUNK):
                                pool.indirect_dma_start(
                                    got[:, c, i, :], None, x,
                                    bass.IndirectOffsetOnAxis(ap=idx[:, c, i:i + 1], axis=0)
                                ).then_inc(gathered[c], 16)

                @block.vector
                def _(dve):
                    body, span, turn = states(dve, "dve")
                    tmp = dve.alloc_register("tmp_dve")
                    at_before, span_before = dve.alloc_register("at_before"), dve.alloc_register("span_before")
                    dve.reg_mov(at_before, 0)
                    dve.reg_mov(span_before, 0)
                    dve.tensor_copy(win_0[:], iota_f[:, 0:WINS]).then_inc(dl_done, 1)
                    dve.tensor_scalar(iota_1[:], iota_f[:, 0:WIN], 1.0, None, ALU.add).then_inc(dl_done, 1)
                    dve.memset(one[:], 1.0).then_inc(dl_done, 1)
                    dve.wait_ge(dl_done, 3)

                    def add_body(k):
                        at = dve.snap(at_before, min_val=0, max_val=N - 1)
                        at_span = dve.snap(span_before, min_val=0, max_val=SPANS) * P
                        dve.wait_ge(drained, 2 * k + 2)
                        for j, (to, part, col) in enumerate(((sums, acc_s[:, 0, :], at),
                                                             (counts, acc_s[0:NT, 1, :], at),
                                                             (sums, acc_s[:, 3, :], at_span),
                                                             (counts, acc_s[0:NT, 2, :], at_span))):
                            if j >= 2:
                                dve.wait_ge(added, 4 * k + j + 3)
                            dve.tensor_tensor(to[:, bass.ds(col, P)], to[:, bass.ds(col, P)], part, ALU.add
                                              ).then_inc(added, 1)

                    dve.sem_inc(added, 4)
                    dve.sem_inc(left_made, 1)
                    dve.sem_inc(body_taken, 1)
                    dve.sem_inc(stage_used, 2)
                    dve.sem_inc(hot_done, 1)
                    dve.sem_inc(inside_done, 1)
                    dve.sem_inc(coded_done, 1)
                    with every_trip(dve) as k:
                        dve.wait_ge(hot_done, NC * k + 1)
                        dve.wait_ge(body_in, 64 * k + 64)
                        dve.tensor_copy(types[:], edges_now[:, 1, :]).then_inc(dl_done, 1)
                        dve.tensor_scalar(dl[:], edges_now[:, 0, :],
                                          first_now[:], None, ALU.subtract).then_inc(dl_done, 1)
                        dve.wait_ge(inside_done, 2 * k + 1)
                        dve.tensor_scalar(win_no[:], win_0[:],
                                          span_no[:, bass.ds(dve.snap(span, min_val=0, max_val=SPANS), 1)],
                                          None, ALU.add).then_inc(dl_done, 1)
                        dve.wait_ge(dl_done, 3 * k + 6)
                        dve.sem_inc(body_begun, 1)
                        at = dve.value_load(at_now[0:1, 0:1], min_val=0, max_val=N - 1)
                        dve.sem_inc(body_taken, 1)
                        for c in range(NC):
                            n = NC * k + c
                            if c % 2 == 0:
                                h = c // 2
                                st = stage[:, h, :, :]
                                dve.wait_ge(stage_in[h], 16 * HALF * k + 16 * HALF)
                                dve.wait_ge(counted, WINS * k + HALF * h + HALF)
                                dve.wait_ge(coded_done, 2 * k + h + 1)
                                dve.tensor_tensor(
                                    inside[:].rearrange("p (i t) -> p i t", t=WT),
                                    st[:, :, 0].rearrange("p (i t) -> p i t", t=WT),
                                    win_no[:, h * HALF:(h + 1) * HALF].unsqueeze(2).to_broadcast([P, HALF, WT]),
                                    ALU.is_equal).then_inc(inside_done, 1)
                                dve.tensor_tensor(
                                    kind_w[:, h, :, :],
                                    st[:, :, 4:5].to_broadcast([P, HALF * WT, NT]),
                                    iota_f[:, 0:NT].unsqueeze(1).to_broadcast([P, HALF * WT, NT]), ALU.is_equal)
                                dve.tensor_copy(low_f[:, h, :], st[:, :, 3])
                                dve.wait_ge(inside_done, 2 * k + h + 2)
                                dve.tensor_tensor(
                                    coded[:, h, :, :], st[:, :, 1:3],
                                    inside[:].unsqueeze(2).to_broadcast([P, HALF * WT, 2]), ALU.mult
                                ).then_inc(coded_done, 1)
                            dve.wait_ge(summed, n + NC - 1)
                            dve.tensor_tensor(
                                kind[:, c % 2, :, :],
                                types[:, c * CHUNK:(c + 1) * CHUNK].unsqueeze(2)
                                .to_broadcast([P, CHUNK, NT]),
                                iota_f[:, 0:NT].unsqueeze(1).to_broadcast([P, CHUNK, NT]), ALU.is_equal)
                            dve.tensor_tensor(
                                hot[:, c % 2, :, :],
                                iota_f[:].unsqueeze(1).to_broadcast([P, CHUNK, P]),
                                dl[:, c * CHUNK:(c + 1) * CHUNK].unsqueeze(2).to_broadcast([P, CHUNK, P]),
                                ALU.is_equal).then_inc(hot_done, 1)
                            for i in range(PER * c, PER * c + PER):
                                m = WINS * k + i
                                dve.wait_ge(counted, m + WINS - RING + 1)
                                j = i % HALF * WT
                                if i % 2 == 0:
                                    dve.tensor_tensor(
                                        left[:, i % RING, :, :],
                                        iota_h[:].unsqueeze(1).to_broadcast([P, WT, P]),
                                        st[:, j:j + WT, 3:4].to_broadcast([P, WT, P]), ALU.is_equal)
                                if i % HALF == 0:
                                    dve.wait_ge(coded_done, 2 * k + h + 2)
                                    dve.tensor_tensor(
                                        hot_w[:, h, :, :],
                                        coded[:, h, :, 1:2].to_broadcast([P, HALF * WT, WIN]),
                                        iota_1[:, 0:WIN].unsqueeze(1).to_broadcast([P, HALF * WT, WIN]),
                                        ALU.is_equal)
                                for t in range(WT):
                                    mm = dve.tensor_scalar(right[:, i % RING, t, :], codes_f[:],
                                                           coded[:, h, j + t, 0:1], None, ALU.is_equal)
                                mm.then_inc(made, 1)
                                if i % HALF == HALF - 1:
                                    dve.wait_ge(made, m + 1)
                                    dve.sem_inc(stage_used, 1)
                            if c == 1:
                                add_body(k)
                                dve.reg_mov(at_before, at)
                                dve.reg_mov(span_before, span)
                        advance(dve, body, span, turn, tmp)
                    add_body(dve.value_load(trips_i[0:1, 0:1], min_val=1, max_val=MAXT))

                @block.scalar
                def _(act):
                    def make_left(i, k):
                        n = WINS // 2 * k + i // 2
                        act.wait_ge(coded_done, 2 * k + i // HALF + 2)
                        act.wait_ge(left_made, n + 1)
                        for t in range(WT):
                            j = i % HALF * WT + t
                            m = act.activation(apart[:, t, :], iota_f[:], ACT.Abs, scale=-1.0,
                                               bias=low_f[:, i // HALF, j:j + 1])
                        m.then_inc(apart_done, 1)
                        act.wait_ge(apart_done, n + 1)
                        act.wait_ge(counted, WINS * k + i + WINS - RING + 1)
                        act.activation(left[:, i % RING, :, :], apart[:], ACT.Relu, scale=-1.0, bias=one[:]
                                       ).then_inc(left_made, 1)

                    def drain_chunks(k):
                        act.wait_ge(summed, NC * k + NC)
                        act.wait_ge(added, 4 * k + 4)
                        act.copy(acc_s[:, 0, :], sum_ps[:, 0:P])
                        act.copy(acc_s[0:NT, 1, :], cnt_ps[0:NT, 0:P])
                        act.copy(acc_s[0:NT, 2, :], kinds_ps[0:NT, 0:P]).then_inc(drained, 1)

                    def drain_span(k):
                        act.wait_ge(applied, k + 1)
                        act.copy(acc_s[:, 3, :], span_ps[:, 0:P]).then_inc(drained, 1)

                    act.sem_inc(c_copied, CB)
                    with every_trip(act) as k:
                        drain_chunks(k)
                        for c in range(NC):
                            act.wait_ge(hot_done, NC * k + c + 2)
                            act.copy(hot_b[:, c % 2, :, :], hot[:, c % 2, :, :]).then_inc(hot_cast, 1)
                            for i in range(PER * c, PER * c + PER):
                                m = WINS * k + i
                                if i == 0:
                                    for j in range(1, RING, 2):
                                        make_left(j, k)
                                    drain_span(k)
                                if i in LEFTS:
                                    make_left(LEFTS[i], k)
                                act.wait_ge(counted, m + WINS + 1)
                                act.copy(cols_sb[:, :, i * WIN:(i + 1) * WIN],
                                         c_ps[:, i % CB, 0:CODES].rearrange("p (t d) -> p t d", d=WIN)
                                         ).then_inc(c_copied, 1)

                    trips = act.value_load(trips_i[0:1, 0:1], min_val=1, max_val=MAXT)
                    drain_chunks(trips)
                    drain_span(trips)

                @block.tensor
                def _(pe):
                    for ps, done, count in ((span_ps[:, 0:P], applied, 1), (kinds_ps[0:NT, 0:P], applied, 0),
                                            (cnt_ps[0:NT, 0:P], applied, 0), (sum_ps[:, 0:P], summed, NC)):
                        mm = pe.matmul(ps, zero_b[:, 0:ps.shape[0]], zero_b[:], start=True, stop=True)
                        if count:
                            mm.then_inc(done, count)
                    pe.sem_inc(counted, WINS)
                    with every_trip(pe) as k:
                        for c in range(NC):
                            for i in range(PER * c, PER * c + PER):
                                m, h = WINS * k + i, i // HALF
                                pe.wait_ge(c_copied, m + 1)
                                if i == 0:
                                    pe.wait_ge(drained, 2 * k + 1)
                                pe.wait_ge(made, m + 1)
                                if i % 2:
                                    pe.wait_ge(left_made, WINS // 2 * k + i // 2 + 2)
                                for t in range(WT):
                                    j, ends = i % HALF * WT + t, dict(start=(t == 0), stop=(t == WT - 1))
                                    pe.matmul(c_ps[:, i % CB, 0:CODES], left[:, i % RING, t, :],
                                              right[:, i % RING, t, :], **ends)
                                    mm = pe.matmul(kinds_ps[0:NT, i * WIN:(i + 1) * WIN], kind_w[:, h, j, :],
                                                   hot_w[:, h, j, :], **ends)
                                mm.then_inc(counted, 1)
                            pe.wait_ge(gathered[c], 16 * CHUNK * k + 16 * CHUNK)
                            pe.wait_ge(hot_cast, NC * k + c + 1)
                            for i in range(CHUNK):
                                n = c * CHUNK + i
                                pe.matmul(cnt_ps[0:NT, 0:P], kind[:, c % 2, i, :], hot_b[:, c % 2, i, :],
                                          start=(n == 0), stop=(n == GROUP - 1))
                                mm = pe.matmul(sum_ps[:, 0:P], got[:, c, i, :], hot[:, c % 2, i, :],
                                               start=(n == 0), stop=(n == GROUP - 1))
                            mm.then_inc(summed, 1)
                        pe.wait_ge(c_copied, WINS * k + WINS + CB)
                        pe.wait_ge(drained, 2 * k + 2)
                        for t in range(SPANS):
                            mm = pe.matmul(span_ps[:, 0:P], nodes[:, t, :], cols_sb[:, t, :],
                                           start=(t == 0), stop=(t == SPANS - 1))
                        mm.then_inc(applied, 1)

        with ExitStack() as ph:
            msg = sb("msg", [P, QN], F32, ph)
            r_s = sb("r_s", [P, QN], F32, ph)
            z_s = sb("z_s", [P, QN], F32, ph)
            n_s = sb("n_s", [P, QN], F32, ph)
            t_s = sb("t_s", [P, QN], F32, ph)
            d_s = sb("d_s", [P, QN], F32, ph)
            msg_ps = psum("msg_ps", [P, 512], F32, ph)
            r_ps = psum("r_ps", [P, 512], F32, ph)
            z_ps = psum("z_ps", [P, 512], F32, ph)
            i_ps = psum("i_ps", [P, 512], F32, ph)
            h_ps = psum("h_ps", [P, 512], F32, ph)
            xt_ps = psum("xt_ps", [P, 2, 512], F32, ph)
            xt_done = sem("xt_done")
            xt_copied = sem("xt_copied")
            msg_done = sem("msg_done")
            msg_copied = sem("msg_copied")
            gates = sem("gates")
            r_done = sem("r_done")
            z_done = sem("z_done")
            pre_done = sem("pre_done")
            n_done = sem("n_done")
            y_done = sem("y_done")

            with nc.Block() as block:
                @block.tensor
                def _(pe):
                    for q in range(NQ):
                        pe.wait_ge(xt_copied, q + 1)
                        for i in range(QUAD):
                            t = pe.transpose(xt_ps[:, q % 2, i * NODES:(i + 1) * NODES],
                                             nodes[:, q * QUAD + i, :], ident[:])
                        t.then_inc(xt_done, 1)
                    pe.wait_ge(xt_copied, NQ + 2)
                    pe.sem_inc(gates, 3)
                    with pe.Fori(0, NQ) as q:
                        cols = bass.ds(q * QN, QN)
                        pe.wait_ge(msg_copied, q + 1)
                        pe.matmul(msg_ps[:, 0:QN], wT[:, 0, :], sums[:, cols], start=True, stop=False)
                        pe.matmul(msg_ps[:, 0:QN], table[:], counts[:, cols], start=False, stop=True
                                  ).then_inc(msg_done, 1)
                        pe.wait_ge(z_done, q + 1)
                        pe.wait_ge(pre_done, 2 * q + 2)
                        pe.matmul(r_ps[:, 0:QN], wT[:, 5, :], work[:, cols], start=True, stop=False)
                        pe.matmul(z_ps[:, 0:QN], wT[:, 6, :], work[:, cols], start=True, stop=False)
                        pe.matmul(h_ps[:, 0:QN], wT[:, 7, :], work[:, cols], start=True, stop=True)
                        pe.wait_ge(msg_copied, q + 2)
                        pe.matmul(r_ps[:, 0:QN], wT[:, 2, :], msg[:], start=False, stop=True).then_inc(gates, 1)
                        pe.matmul(i_ps[:, 0:QN], wT[:, 4, :], msg[:], start=True, stop=True).then_inc(gates, 1)
                        pe.matmul(z_ps[:, 0:QN], wT[:, 3, :], msg[:], start=False, stop=True).then_inc(gates, 1)

                @block.scalar
                def _(act):
                    act.sem_inc(xt_copied, 2)
                    for q in range(NQ):
                        act.wait_ge(xt_done, q + 1)
                        act.copy(work[:, q * QN:(q + 1) * QN], xt_ps[:, q % 2, 0:QN]).then_inc(xt_copied, 1)
                    act.sem_inc(msg_copied, 1)
                    act.sem_inc(z_done, 1)
                    with act.Fori(0, NQ) as q:
                        act.wait_ge(msg_done, q + 1)
                        act.wait_ge(gates, 3 * q + 3)
                        act.copy(msg[:], msg_ps[:, 0:QN]).then_inc(msg_copied, 1)
                        act.wait_ge(gates, 3 * q + 4)
                        act.activation(r_s[:], r_ps[:, 0:QN], ACT.Sigmoid, bias=brz[:, 0:1]).then_inc(r_done, 1)
                        act.wait_ge(gates, 3 * q + 6)
                        act.wait_ge(y_done, 4 * q + 4)
                        act.activation(z_s[:], z_ps[:, 0:QN], ACT.Sigmoid, bias=brz[:, 1:2]).then_inc(z_done, 1)
                        act.wait_ge(pre_done, 2 * q + 4)
                        act.activation(n_s[:], t_s[:], ACT.Tanh, bias=bih[:, 2:3]).then_inc(n_done, 1)

                @block.vector
                def _(dve):
                    dve.sem_inc(pre_done, 2)
                    dve.sem_inc(y_done, 4)
                    with dve.Fori(0, NQ) as q:
                        cols = bass.ds(q * QN, QN)
                        dve.wait_ge(r_done, q + 1)
                        dve.wait_ge(gates, 3 * q + 5)
                        dve.scalar_tensor_tensor(out=t_s[:], in0=h_ps[:, 0:QN], scalar=bhh[:, 2:3], in1=r_s[:],
                                                 op0=ALU.add, op1=ALU.mult).then_inc(pre_done, 1)
                        dve.wait_ge(pre_done, 2 * q + 3)
                        dve.tensor_tensor(t_s[:], t_s[:], i_ps[:, 0:QN], ALU.add).then_inc(pre_done, 1)
                        dve.wait_ge(n_done, q + 1)
                        dve.wait_ge(z_done, q + 2)
                        dve.tensor_tensor(d_s[:], work[:, cols], n_s[:], ALU.subtract).then_inc(y_done, 1)
                        dve.wait_ge(y_done, 4 * q + 5)
                        dve.tensor_tensor(d_s[:], d_s[:], z_s[:], ALU.mult).then_inc(y_done, 1)
                        dve.wait_ge(y_done, 4 * q + 6)
                        dve.tensor_tensor(d_s[:], d_s[:], n_s[:], ALU.add).then_inc(y_done, 1)
                        dve.wait_ge(y_done, 4 * q + 7)
                        dve.tensor_tensor(work[:, cols], work[:, cols], d_s[:], ALU.add).then_inc(y_done, 1)

        with ExitStack() as ph:
            y_ps = psum("y_ps", [NODES, 2, QUAD, D], F32, ph)
            deg_ps = psum("deg_ps", [NODES, 512], F32, ph)
            y_turned = sem("y_turned")
            y_copied = sem("y_copied")
            stats_done = sem("stats_done")
            aggr_done = sem("aggr_done")
            spread = sem("spread0")

            with nc.Block() as block:
                @block.tensor
                def _(pe):
                    for q in range(NQ):
                        pe.wait_ge(y_copied, q + 1)
                        for i in range(QUAD):
                            tile = q * QUAD + i
                            pe.matmul(deg_ps[:, tile:tile + 1], counts[:, tile * NODES:(tile + 1) * NODES],
                                      ones[:], start=True, stop=True)
                            t = pe.transpose(y_ps[:, q % 2, i, :], work[:, tile * NODES:(tile + 1) * NODES], ident[:])
                        t.then_inc(y_turned, 1)

                @block.scalar
                def _(act):
                    act.sem_inc(y_copied, 2)
                    for q in range(NQ):
                        act.wait_ge(y_turned, q + 1)
                        act.copy(nodes[:, q * QUAD:(q + 1) * QUAD, :], y_ps[:, q % 2, :, :]).then_inc(y_copied, 1)
                    act.wait_ge(spread, 1)
                    act.activation(rstd[:], rstd[:], ACT.Sqrt).then_inc(spread, 1)

                @block.vector
                def _(dve):
                    for q in range(NQ):
                        dve.wait_ge(y_copied, q + 3)
                        if q:
                            dve.wait_ge(aggr_done, QUAD * q)
                        for i in range(QUAD):
                            dve.bn_stats(stats[:, i, :], nodes[:, q * QUAD + i, :]).then_inc(stats_done, 1)
                        for i in range(QUAD):
                            dve.wait_ge(stats_done, QUAD * q + i + 1)
                            dve.bn_aggr(moments[:, q * QUAD + i, :], stats[:, i, :]).then_inc(aggr_done, 1)
                    dve.wait_ge(aggr_done, NTL)
                    dve.tensor_scalar(rstd[:], moments[:, :, 1], LN_EPS, None, ALU.add).then_inc(spread, 1)
                    dve.tensor_scalar(rdeg[:], deg_ps[:, 0:NTL], 1.0, None, ALU.max).then_inc(stats_done, 1)
                    dve.wait_ge(stats_done, NTL + 1)
                    dve.reciprocal(rdeg[:], rdeg[:])
                    dve.wait_ge(spread, 2)
                    dve.reciprocal(rstd[:], rstd[:])

        first_f = sb("first_f", [P, P * KW], F32)

        def each_quad(eng, quad):
            if NQ > 1:
                with eng.Fori(0, NQ // 2) as h:
                    for b in range(2):
                        quad(h, b)
            if NQ % 2:
                quad(NQ // 2, 0)

        proj = work[0:NODES, 0:NTL * D].rearrange("p (t f) -> p t f", f=D)
        with ExitStack() as ph:
            f_s = sb("f_s", [P, 2, QN], F32, ph)
            rest = sb("rest", [NODES, 2, QUAD, D], F32, ph)
            split = sb("split", [NODES, 2, QUAD, 3, D], BF16, ph)
            f_ps = psum("f_ps", [P, 2, 512], F32, ph)
            p_ps = psum("p_ps", [NODES, 2, QUAD, D], F32, ph)
            normed = sem("normed")
            f_turned = sem("f_turned")
            f_copied = sem("f_copied")
            p_done = sem("p_done")
            p_copied = sem("p_copied")
            cut = sem("cut")
            feat_out = sem("feat_out")
            proj_out = sem("proj_out")
            first_in = sem("first_in")
            parts_out = [sem(f"parts_out{b}") for b in range(2)]
            rows_q = rows[0:NTL * NODES, :].rearrange("(t p) f -> p t f", p=NODES)
            parts_q = parts[0:NTL * NODES, :].rearrange("(t p) (s f) -> p t s f", p=NODES, s=3)

            with nc.Block() as block:
                @block.vector
                def _(dve):
                    for q in range(NQ + 2):
                        if q < NQ:
                            for t in range(q * QUAD, (q + 1) * QUAD):
                                dve.tensor_scalar(nodes[:, t, :], nodes[:, t, :], moments[:, t, 0:1],
                                                  rstd[:, t:t + 1], ALU.subtract, ALU.mult).then_inc(normed, 1)
                        if q >= 2:
                            n = q - 2
                            b, pr = n % 2, proj[:, n * QUAD:(n + 1) * QUAD, :]
                            dve.wait_ge(p_copied, n + 3)
                            dve.tensor_tensor(rest[:, b, :, :], pr, split[:, b, :, 0, :], ALU.subtract
                                              ).then_inc(cut, 1)
                            dve.wait_ge(cut, 3 * n + 1)
                            dve.tensor_copy(split[:, b, :, 1, :], rest[:, b, :, :]).then_inc(cut, 1)
                            dve.wait_ge(cut, 3 * n + 2)
                            dve.tensor_tensor(split[:, b, :, 2, :], rest[:, b, :, :], split[:, b, :, 1, :],
                                              ALU.subtract).then_inc(cut, 1)

                @block.tensor
                def _(pe):
                    pe.sem_inc(p_done, 2)
                    for q in range(NQ):
                        b = q % 2
                        pe.wait_ge(normed, QUAD * q + QUAD)
                        pe.wait_ge(f_copied, q + 1)
                        for i in range(QUAD):
                            t = pe.transpose(f_ps[:, b, i * NODES:(i + 1) * NODES],
                                             nodes[:, q * QUAD + i, :],
                                             ident[0:NODES, 0:NODES])
                        t.then_inc(f_turned, 1)
                        pe.wait_ge(f_copied, q + 3)
                        pe.wait_ge(p_copied, q + 1)
                        for i in range(QUAD):
                            mm = pe.matmul(p_ps[:, b, i, :], f_s[:, b, i * NODES:(i + 1) * NODES], wT[:, 1, :],
                                           start=True, stop=True)
                        mm.then_inc(p_done, 1)

                @block.scalar
                def _(act):
                    act.sem_inc(f_copied, 2)
                    act.sem_inc(p_copied, 2)
                    def copy_quad(h, b):
                        q = h * 2 + b
                        act.wait_ge(f_turned, q + 1)
                        act.wait_ge(p_done, q + 1)
                        act.copy(f_s[:, b, :], f_ps[:, b, 0:QN]).then_inc(f_copied, 1)
                        act.wait_ge(p_done, q + 3)
                        act.copy(proj[:, bass.ds(q * QUAD, QUAD), :], p_ps[:, b, :, :])
                        act.wait_ge(parts_out[b], 16 * h + 16)
                        act.copy(split[:, b, :, 0, :], p_ps[:, b, :, :]).then_inc(p_copied, 1)

                    each_quad(act, copy_quad)

                @block.sync
                def _(sp):
                    sp.dma_start(first_f[:], first_row.to_broadcast([P, P * KW])).then_inc(first_in, 16)
                    for b in range(2):
                        sp.sem_inc(parts_out[b], 16)
                    def store_quad(h, b):
                        q = h * 2 + b
                        t = bass.ds(q * QUAD, QUAD)
                        sp.wait_ge(normed, QUAD * q + QUAD)
                        sp.dma_start(rows_q[:, t, D:2 * D], nodes[:, t, :]).then_inc(feat_out, 16)
                        sp.wait_ge(p_copied, q + 3)
                        sp.dma_start(rows_q[:, t, 0:D], proj[:, t, :]).then_inc(proj_out, 16)
                        sp.wait_ge(cut, 3 * q + 3)
                        sp.dma_start(parts_q[:, t, :, :], split[:, b, :, :, :]).then_inc(parts_out[b], 16)

                    each_quad(sp, store_quad)
                    sp.wait_ge(first_in, 16)
                    sp.wait_ge(feat_out, 16 * NQ)
                    sp.wait_ge(proj_out, 16 * NQ)
                    for b in range(2):
                        sp.wait_ge(parts_out[b], 16 * ((NQ + 1 - b) // 2) + 16)

        with ExitStack() as ph:
            got = sb("got1", [P, NC, CHUNK, 2 * D], F32, ph)
            hot = sb("hot1", [P, NC, CHUNK, P], BF16, ph)
            hot_t = sb("hot_t", [P, 2, CHUNK, P], BF16, ph)
            whot = sb("whot", [P, 2, CHUNK, P], F32, ph)
            win_in = sb("win_in", [P, 3, D], BF16, ph)
            win = sb("win", [P, 3, D], BF16, ph)
            s_s = sb("s_s", [P, CHUNK, D], F32, ph)
            l_s = sb("l_s", [P, CHUNK, D], F32, ph)
            pr_s = sb("pr_s", [P, CHUNK, D], F32, ph)
            q_s = sb("q_s", [P, NC, CHUNK], F32, ph)
            e_s = sb("e_s", [P, NC, CHUNK], F32, ph)
            gate_s = sb("gate_s", [P, NC, CHUNK], F32, ph)
            eg_s = sb("eg_s", [P, NC, CHUNK], F32, ph)
            w_s = sb("w_s", [P, NC, CHUNK], F32, ph)
            hot_ps = psum("hot_ps", [P, 2, 1024], BF16, ph)
            er_ps = psum("er_ps", [P, 2, 1024], F32, ph)
            sum_ps = psum("sum_ps1", [P, 512], F32, ph)
            idx_in = [sem(f"idx_in1_{c}") for c in range(NC)]
            gathered = [sem(f"gathered1_{c}") for c in range(NC)]
            win_loaded = sem("win_loaded")
            win_copied = sem("win_copied")
            dl_done = sem("dl_done1")
            hot_done = sem("hot_done1")
            turned = sem("turned")
            hot_copied = sem("hot_copied")
            er_done = sem("er_done")
            s_done = sem("s_done")
            q_done = sem("q_done")
            l_done = sem("l_done")
            e_done = sem("e_done")
            gate_done = sem("gate_done")
            eg_done = sem("eg_done")
            w_done = sem("w_done")
            whot_done = sem("whot_done")
            summed = sem("summed1")
            zeros_set = sem("zeros_set")
            added = sem("added1")

            with nc.Block() as block:
                @block.sync
                def _(sp):
                    sp.dma_start(win_in[:].rearrange("p s f -> p (s f)"), parts[bass.ds(node_of(sp, 0), P), :]
                                 ).then_inc(win_loaded, 16)
                    with every_body(sp) as k:
                        col = column(sp, k)
                        for c in range(NC):
                            sp.wait_ge(summed, NC * k + c + 1)
                            sp.dma_start(idx[:, c, :], src_tab[:, bass.ds(col + c * CHUNK, CHUNK)]
                                         ).then_inc(idx_in[c], 16)
                        at = node_of(sp, k + 1)
                        sp.wait_ge(win_copied, k + 1)
                        sp.dma_start(win_in[:].rearrange("p s f -> p (s f)"), parts[bass.ds(at, P), :]
                                     ).then_inc(win_loaded, 16)

                @block.gpsimd
                def _(pool):
                    with every_body(pool) as k:
                        for c in range(NC):
                            pool.wait_ge(idx_in[c], 16 * k + 16)
                            pool.sem_inc(chunk_begun, 1)
                            for i in range(CHUNK):
                                pool.indirect_dma_start(
                                    got[:, c, i, :], None, rows,
                                    bass.IndirectOffsetOnAxis(ap=idx[:, c, i:i + 1], axis=0)
                                ).then_inc(gathered[c], 16)

                @block.vector
                def _(dve):
                    def relative(k, col):
                        dve.tensor_scalar(dl[:], dst_f[:, bass.ds(col, GROUP)],
                                          first_f[:, bass.ds(k, 1)], None, ALU.subtract).then_inc(dl_done, 1)

                    def one_hot(c, k):
                        dve.wait_ge(whot_done, NC * k + c + 1)
                        dve.tensor_tensor(
                            hot[:, c, :, :],
                            iota_f[:].unsqueeze(1).to_broadcast([P, CHUNK, P]),
                            dl[:, c * CHUNK:(c + 1) * CHUNK].unsqueeze(2).to_broadcast([P, CHUNK, P]),
                            ALU.is_equal).then_inc(hot_done, 1)

                    def add_body(at, k):
                        dve.wait_ge(summed, NC * k + NC)
                        dve.tensor_tensor(sums[:, bass.ds(at, P)], sums[:, bass.ds(at, P)],
                                          sum_ps[:, 0:P], ALU.add).then_inc(added, 1)

                    dve.memset(got[:, NC - 1, :, D:2 * D], 0.0).then_inc(zeros_set, 1)
                    dve.memset(whot[:, 1, :, :], 0.0).then_inc(zeros_set, 1)
                    dve.memset(sums[:, 0:NPAD], 0.0).then_inc(zeros_set, 1)
                    relative(0, column(dve, 0))
                    dve.wait_ge(dl_done, 1)
                    one_hot(0, 0)
                    one_hot(1, 0)
                    dve.wait_ge(zeros_set, 3)
                    dve.sem_inc(q_done, 2)
                    before = dve.alloc_register("before")
                    dve.reg_mov(before, 0)
                    with every_body(dve) as k:
                        for c in range(NC):
                            n = NC * k + c
                            el = got[:, c, :, 0:D]
                            er = er_ps[:, c % 2, 0:CHUNK * D].rearrange("p (i f) -> p i f", f=D)
                            dve.wait_ge(gathered[c], 16 * CHUNK * k + 16 * CHUNK)
                            dve.wait_ge(er_done, n + NC + 1)
                            dve.tensor_tensor(s_s[:], el, er, ALU.add).then_inc(s_done, 1)
                            for i in range(CHUNK):
                                mm = dve.tensor_tensor_reduce(pr_s[:, i, :], el[:, i, :], er[:, i, :], 1.0, 0.0,
                                                              ALU.mult, ALU.add, q_s[:, c, i:i + 1])
                            mm.then_inc(q_done, 1)
                            dve.wait_ge(s_done, n + 1)
                            dve.scalar_tensor_tensor(out=l_s[:], in0=s_s[:], scalar=LEAK, in1=s_s[:],
                                                     op0=ALU.mult, op1=ALU.max).then_inc(l_done, 1)
                            if c == NC - 2:
                                col = column(dve, k + 1)
                                dve.wait_ge(hot_done, NC * k + NC)
                                relative(k + 1, col)
                                dve.wait_ge(dl_done, k + 2)
                            one_hot((c + 2) % NC, k + (c + 2) // NC)
                            dve.wait_ge(l_done, n + 1)
                            for i in range(CHUNK):
                                mm = dve.tensor_tensor_reduce(l_s[:, i, :], l_s[:, i, :], a_all[:], 1.0, 0.0,
                                                              ALU.mult, ALU.add, e_s[:, c, i:i + 1])
                            mm.then_inc(e_done, 1)
                            if c == 0:
                                add_body(dve.snap(before, min_val=0, max_val=N - 1), k)
                                dve.reg_mov(before, node_of(dve, k))
                            dve.wait_ge(gate_done, n + 1)
                            dve.wait_ge(e_done, n + 1)
                            dve.tensor_tensor(eg_s[:, c, :], e_s[:, c, :], gate_s[:, c, :], ALU.mult
                                              ).then_inc(eg_done, 1)
                    add_body(dve.snap(before, min_val=0, max_val=N - 1),
                             dve.value_load(bodies_i[0:1, 0:1], min_val=1, max_val=MAXB))

                @block.scalar
                def _(act):
                    def copy_hot(c, k):
                        n = NC * k + c
                        act.wait_ge(turned, n + 1)
                        act.wait_ge(er_done, n + NC - 1)
                        act.copy(hot_t[:, c % 2, :, :],
                                 hot_ps[:, c % 2, 0:CHUNK * P].rearrange("p (i e) -> p i e", e=P)
                                 ).then_inc(hot_copied, 1)

                    def copy_window(k):
                        act.wait_ge(win_loaded, 16 * k + 16)
                        act.wait_ge(er_done, NC * k + NC)
                        act.copy(win[:], win_in[:]).then_inc(win_copied, 1)

                    act.sem_inc(hot_copied, 2)
                    act.sem_inc(whot_done, NC)
                    copy_window(0)
                    copy_hot(0, 0)
                    with every_body(act) as k:
                        for c in range(NC):
                            n = NC * k + c
                            copy_hot((c + 1) % NC, k + (c + 1) // NC)
                            if c == NC - 1:
                                copy_window(k + 1)
                            act.wait_ge(q_done, n + 3)
                            act.activation(gate_s[:, c, :], q_s[:, c, :], ACT.Sigmoid).then_inc(gate_done, 1)
                            act.wait_ge(eg_done, n + 1)
                            act.activation(w_s[:, c, :], eg_s[:, c, :], ACT.Sigmoid).then_inc(w_done, 1)
                            act.wait_ge(w_done, n + 1)
                            act.wait_ge(summed, n + NC - 1)
                            for i in range(CHUNK):
                                m = act.activation(whot[:, c % 2, i, :], hot[:, c, i, :], ACT.Copy,
                                                   scale=w_s[:, c, i:i + 1])
                            m.then_inc(whot_done, 1)

                @block.tensor
                def _(pe):
                    def turn(c, k):
                        n = NC * k + c
                        pe.wait_ge(hot_done, n + 1)
                        pe.wait_ge(hot_copied, n + 1)
                        for i in range(CHUNK):
                            t = pe.transpose(hot_ps[:, c % 2, i * P:(i + 1) * P], hot[:, c, i, :], ident_b[:])
                        t.then_inc(turned, 1)

                    def sum_rows(c):
                        for i in range(CHUNK):
                            mm = pe.matmul(sum_ps[:, 0:P], got[:, c, i, D:2 * D], whot[:, c % 2, i, :],
                                           start=(c == 0 and i == 0), stop=(c == NC - 1 and i == CHUNK - 1))
                        mm.then_inc(summed, 1)

                    pe.sem_inc(er_done, NC)
                    pe.sem_inc(summed, NC - 1)
                    turn(0, 0)
                    pe.wait_ge(zeros_set, 3)
                    pe.matmul(sum_ps[:, 0:P], got[:, NC - 1, 0, D:2 * D], whot[:, 1, 0, :], start=True, stop=False)
                    with every_body(pe) as k:
                        for c in range(NC):
                            n = NC * k + c
                            turn((c + 1) % NC, k + (c + 1) // NC)
                            if c == 0:
                                pe.wait_ge(win_copied, k + 1)
                            pe.wait_ge(hot_copied, n + 3)
                            pe.wait_ge(q_done, n + 1)
                            for i in range(CHUNK):
                                for part in range(3):
                                    mm = pe.matmul(er_ps[:, c % 2, i * D:(i + 1) * D], hot_t[:, c % 2, i, :],
                                                   win[:, part, :], start=(part == 0), stop=(part == 2))
                            mm.then_inc(er_done, 1)
                            if c == 1:
                                pe.wait_ge(added, k + 1)
                            pe.wait_ge(whot_done, n + NC)
                            sum_rows((c - 1) % NC)
                    bodies = pe.value_load(bodies_i[0:1, 0:1], min_val=1, max_val=MAXB)
                    pe.wait_ge(whot_done, bodies * NC + NC)
                    sum_rows(NC - 1)

        with ExitStack() as ph:
            mean_s = sb("mean_s", [NODES, QUAD, D], F32, ph)
            m_ps = psum("m_ps", [NODES, 2, QUAD, D], F32, ph)
            m_turned = sem("m_turned")
            steps = sem("steps")
            spread = sem("spread1")
            finished = sem("finished")
            stored = sem("stored")
            finished_pool = sem("finished_pool")
            S = 2 + 2 * QUAD
            HERE = NTL * 3 // 4 // QUAD * QUAD + QUAD if NQ > 4 else NTL

            def normalise(eng, tiles, done):
                for t in tiles:
                    eng.tensor_scalar(nodes[:, t, :], nodes[:, t, :], moments[:, t, 0:1], rstd[:, t:t + 1],
                                      ALU.subtract, ALU.mult).then_inc(done, 1)

            with nc.Block() as block:
                @block.tensor
                def _(pe):
                    for q in range(NQ):
                        if q >= 2:
                            pe.wait_ge(steps, S * (q - 2) + 2)
                        for i in range(QUAD):
                            tile = q * QUAD + i
                            t = pe.transpose(m_ps[:, q % 2, i, :], sums[:, tile * NODES:(tile + 1) * NODES], ident[:])
                        t.then_inc(m_turned, 1)

                @block.scalar
                def _(act):
                    act.wait_ge(spread, 1)
                    act.activation(rstd[:], rstd[:], ACT.Sqrt).then_inc(spread, 1)

                @block.vector
                def _(dve):
                    dve.sem_inc(steps, 1)
                    for q in range(NQ):
                        t = slice(q * QUAD, (q + 1) * QUAD)
                        dve.wait_ge(m_turned, q + 1)
                        dve.wait_ge(steps, S * q + 1)
                        dve.tensor_tensor(mean_s[:], m_ps[:, q % 2, :, :],
                                          rdeg[:, t].unsqueeze(2).to_broadcast([NODES, QUAD, D]), ALU.mult
                                          ).then_inc(steps, 1)
                        dve.wait_ge(steps, S * q + 2)
                        dve.scalar_tensor_tensor(out=nodes[:, t, :], in0=nodes[:, t, :], scalar=c_x[:],
                                                 in1=mean_s[:], op0=ALU.mult, op1=ALU.add).then_inc(steps, 1)
                        dve.wait_ge(steps, S * q + 3)
                        for i in range(QUAD):
                            dve.bn_stats(stats[:, i, :], nodes[:, q * QUAD + i, :]).then_inc(steps, 1)
                        for i in range(QUAD):
                            dve.wait_ge(steps, S * q + 4 + i)
                            dve.bn_aggr(moments[:, q * QUAD + i, :], stats[:, i, :]).then_inc(steps, 1)
                    dve.wait_ge(steps, S * NQ + 1)
                    dve.tensor_scalar(rstd[:], moments[:, :, 1], LN_EPS, None, ALU.add).then_inc(spread, 1)
                    dve.wait_ge(spread, 2)
                    dve.reciprocal(rstd[:], rstd[:]).then_inc(spread, 1)
                    dve.wait_ge(spread, 3)
                    dve.sem_inc(spread, 1)
                    normalise(dve, range(0, HERE), finished)

                @block.gpsimd
                def _(pool):
                    pool.wait_ge(spread, 4)
                    normalise(pool, range(HERE, NTL), finished_pool)

                @block.sync
                def _(sp):
                    n = 0
                    starts = sorted(range(0, ft, 4), key=lambda t: t - (HERE if t >= HERE else 0))
                    for at in starts:
                        m = min(4, ft - at)
                        if at >= HERE:
                            sp.wait_ge(finished_pool, at - HERE + m)
                        else:
                            sp.wait_ge(finished, at + m)
                        sp.dma_start(out[at * NODES:(at + m) * NODES, :].rearrange("(t p) f -> p t f", p=NODES),
                                     nodes[:, at:at + m, :]).then_inc(stored, 16)
                        n += 1
                    if fr:
                        if ft >= HERE:
                            sp.wait_ge(finished_pool, ft - HERE + 1)
                        else:
                            sp.wait_ge(finished, ft + 1)
                        sp.dma_start(out[ft * NODES:N, :], nodes[0:fr, ft, :]).then_inc(stored, 16)
                        n += 1
                    sp.wait_ge(stored, 16 * n)


_INS = ['x', 'src', 'dst', 'edge_type_9', 'L0_gnn_W_msg', 'L0_gnn_b_msg', 'L0_gnn_edge_embed', 'L0_gnn_W_ih',
        'L0_gnn_W_hh', 'L0_gnn_b_ih', 'L0_gnn_b_hh', 'L1_gnn_fc_weight', 'L1_gnn_attn', 'L1_gnn_eps']


def kernel(**inputs):
    import numpy as _np
    import concourse.bacc as _bacc
    from concourse import mybir as _mybir
    from concourse.bass_utils import run_bass_kernel_spmd as _run

    nc = _bacc.Bacc("TRN2", target_bir_lowering=False, num_devices=1)
    arrays, args = {}, []
    for name in _INS:
        a = _np.ascontiguousarray(inputs[name])
        arrays[f"in_{name}_dram"] = a
        args.append(nc.dram_tensor(f"in_{name}_dram", a.shape, _mybir.dt.from_np(a.dtype), kind="ExternalInput").ap())
    out = nc.dram_tensor("out_0_dram", inputs['x'].shape, _mybir.dt.float32, kind="ExternalOutput").ap()
    graph_layers(nc, *args, out)
    r = _run(nc, [arrays], core_ids=[0])
    return r.results[0]["out_0_dram"]
```
